# Optimizing a Trainium2 kernel written in Bass

```python
import numpy as np
import jax
import jax.numpy as jnp

def _softmax(x, axis=-1):
    return jax.nn.softmax(x, axis=axis)

def _gelu(x):
    return jax.nn.gelu(x, approximate=True)

def _silu(x):
    return jax.nn.silu(x)

def _sigmoid(x):
    return jax.nn.sigmoid(x)

def _layernorm(x, axis=-1, eps=1e-05):
    m = jnp.mean(x, axis=axis, keepdims=True)
    v = jnp.var(x, axis=axis, keepdims=True)
    return (x - m) / jnp.sqrt(v + eps)

def _scatter_add(tgt, idx, src, axis=0):
    return tgt.at[idx].add(src)

def _segment_sum(src, seg, n):
    return jax.ops.segment_sum(src, seg, n)
kernel_name = 'mk_gnn_resnorm_d4_gnn_r16_723f54'

def setup_inputs(seed: int=0):
    np.random.seed(seed)
    _w = jnp.asarray

    def _rec_inputs():
        import jax
        import jax.numpy as jnp
        _gk = jax.random.key(seed)
        x = -0.0001074 + 0.9999 * jax.random.normal(jax.random.fold_in(_gk, 1), (6250, 128), jnp.float32)
        src = jax.random.randint(jax.random.fold_in(_gk, 2), (100000,), 0, 6250, jnp.int32)
        dst = jnp.minimum((6250 * jax.random.uniform(jax.random.fold_in(_gk, 3), (100000,)) ** 2.0).astype(jnp.int32), 99999)
        _o = jnp.argsort(dst, stable=True)
        src = src[_o]
        dst = dst[_o]
        edge_attr_4 = 0.251022 + 0.967981 * jax.random.normal(jax.random.fold_in(_gk, 12), (100000, 4), jnp.float32)
        edge_attr_8 = jax.random.uniform(jax.random.fold_in(_gk, 13), (100000, 8), jnp.float32, 0.0, 1)
        edge_weight = jax.random.uniform(jax.random.fold_in(_gk, 15), (100000,), jnp.float32, 0.0, 1)
        return (x, src, dst, edge_attr_4, edge_attr_8, edge_weight)
    x, src, dst, edge_attr_4, edge_attr_8, edge_weight = _rec_inputs()

    def _L0_gnn_setup():
        import jax, jax.numpy as jnp
        import numpy as np
        N = 6250
        E = 40000
        C = 128
        NEG_SLOPE = 0.2

        def _param(key, shape, scale=0.1):
            return jax.random.normal(key, shape, dtype=jnp.float32) * scale

        def gatv2_layer(x, Wl, bl, Wr, br, att, Wres, bias, src, dst):
            xl = x @ Wl.T + bl
            xr = x @ Wr.T + br
            m = jax.nn.leaky_relu(xl[src] + xr[dst], NEG_SLOPE)
            e = m @ att
            emax = jax.ops.segment_max(e, dst, num_segments=N)
            ex = jnp.exp(e - emax[dst])
            denom = jax.ops.segment_sum(ex, dst, num_segments=N)
            alpha = ex / denom[dst]
            out = jax.ops.segment_sum(alpha[:, None] * xl[src], dst, num_segments=N)
            return out + x @ Wres.T + bias
        key = jax.random.key(seed)
        ks = jax.random.split(key, 20)
        edge_index = jax.random.randint(ks[0], (2, E), 0, N, dtype=jnp.int32)
        emb = jax.random.normal(ks[1], (N, C), dtype=jnp.float32)
        d = {'edge_index': edge_index, 'emb': emb}
        names = ['Wl', 'bl', 'Wr', 'br', 'att', 'Wres', 'bias']
        shapes = [(C, C), (C,), (C, C), (C,), (C,), (C, C), (C,)]
        i = 2
        for layer in (1, 2):
            for nm, sh in zip(names, shapes):
                d[f'l{layer}_{nm}'] = _param(ks[i], sh)
                i += 1
        return d
    _L0_gnn_all = _L0_gnn_setup()
    _L0_gnn_in = {k: v for k, v in _L0_gnn_all.items() if k in ('l1_Wl', 'l1_bl', 'l1_Wr', 'l1_br', 'l1_att', 'l1_Wres', 'l1_bias', 'l2_Wl', 'l2_bl', 'l2_Wr', 'l2_br', 'l2_att', 'l2_Wres', 'l2_bias')}
    del _L0_gnn_all

    def _L1_gnn_setup():
        import jax, jax.numpy as jnp
        import numpy as np
        N = 6250
        E = 50000
        D = 128
        key = jax.random.key(seed)
        ks = jax.random.split(key, 12)
        s = lambda fan_in: 1.0 / np.sqrt(fan_in)
        return {'h': jax.random.normal(ks[0], (N, D), dtype=jnp.float32), 'w': jax.random.uniform(ks[1], (E,), dtype=jnp.float32), 'src': jax.random.randint(ks[2], (E,), 0, N, dtype=jnp.int32), 'dst': jax.random.randint(ks[3], (E,), 0, N, dtype=jnp.int32), 'W1': jax.random.uniform(ks[4], (2 * D + 1, D), jnp.float32, -s(2 * D + 1), s(2 * D + 1)), 'b1': jnp.zeros((D,), jnp.float32), 'W2': jax.random.uniform(ks[5], (D, D), jnp.float32, -s(D), s(D)), 'b2': jnp.zeros((D,), jnp.float32), 'U1': jax.random.uniform(ks[6], (2 * D, D), jnp.float32, -s(2 * D), s(2 * D)), 'c1': jnp.zeros((D,), jnp.float32), 'U2': jax.random.uniform(ks[7], (D, D), jnp.float32, -s(D), s(D)), 'c2': jnp.zeros((D,), jnp.float32)}
    _L1_gnn_all = _L1_gnn_setup()
    _L1_gnn_in = {k: v for k, v in _L1_gnn_all.items() if k in ('W1', 'b1', 'W2', 'b2', 'U1', 'c1', 'U2', 'c2')}
    del _L1_gnn_all

    def _L2_gnn_setup():
        import jax, jax.numpy as jnp
        import numpy as np
        import math
        MUL = 32
        N_NODES = 3125
        N_EDGES = 50000
        RB = 8
        HID = 64
        AVG_N = 16.0
        SILU_C = 1.6790524
        INV_SQRT3 = 1.0 / math.sqrt(3.0)

        def _forward(x, sh, rb, W1_s, W1_v, mW0, mb0, mW1, mb1, mW2, mb2, W2_s, W2_v, Ws_s, Ws_v, senders, receivers):
            N = x.shape[0]
            E = senders.shape[0]
            s = x[:, :MUL]
            v = x[:, MUL:].reshape(N, MUL, 3)
            inv = 1.0 / math.sqrt(MUL)
            s1 = s @ W1_s * inv
            v1 = jnp.einsum('nud,uv->nvd', v, W1_v) * inv
            h = jax.nn.silu(rb @ mW0 + mb0)
            h = jax.nn.silu(h @ mW1 + mb1)
            w = h @ mW2 + mb2
            w0, w1, w2, w3 = jnp.split(w, 4, axis=-1)
            xs = s1[senders]
            xv = v1[senders]
            sh0 = sh[:, :1]
            sh1 = sh[:, 1:]
            m0 = w0 * xs * sh0
            m1 = w1 * jnp.einsum('eud,ed->eu', xv, sh1) * INV_SQRT3
            m2 = w2[:, :, None] * xs[:, :, None] * sh1[:, None, :]
            m3 = w3[:, :, None] * xv * sh0[:, :, None]
            msg = jnp.concatenate([m0, m1, m2.reshape(E, 3 * MUL), m3.reshape(E, 3 * MUL)], axis=-1)
            agg = jax.ops.segment_sum(msg, receivers, num_segments=N) / math.sqrt(AVG_N)
            a_s = agg[:, :2 * MUL]
            a_v = agg[:, 2 * MUL:].reshape(N, 2 * MUL, 3)
            inv2 = 1.0 / math.sqrt(2 * MUL)
            g_s = a_s @ W2_s * inv2
            g_v = jnp.einsum('nud,uv->nvd', a_v, W2_v) * inv2
            extra = jax.nn.silu(g_s[:, :MUL]) * SILU_C
            gates = jax.nn.silu(g_s[:, MUL:]) * SILU_C
            gated_v = gates[:, :, None] * g_v
            skip_s = s @ Ws_s * inv
            skip_v = jnp.einsum('nud,uv->nvd', v, Ws_v) * inv
            out_s = extra + skip_s
            out_v = gated_v + skip_v
            return jnp.concatenate([out_s, out_v.reshape(N, 3 * MUL)], axis=-1)
        key = jax.random.key(seed)
        ks = jax.random.split(key, 18)
        x = jax.random.normal(ks[0], (N_NODES, 4 * MUL), jnp.float32)
        senders = jax.random.randint(ks[1], (N_EDGES,), 0, N_NODES)
        receivers = jax.random.randint(ks[2], (N_EDGES,), 0, N_NODES)
        vec = jax.random.normal(ks[3], (N_EDGES, 3), jnp.float32)
        unit = vec / (jnp.linalg.norm(vec, axis=-1, keepdims=True) + 1e-09)
        sh = jnp.concatenate([jnp.ones((N_EDGES, 1), jnp.float32), math.sqrt(3.0) * unit], axis=-1)
        rb = jax.random.uniform(ks[4], (N_EDGES, RB), jnp.float32)
        W1_s = jax.random.normal(ks[5], (MUL, MUL), jnp.float32)
        W1_v = jax.random.normal(ks[6], (MUL, MUL), jnp.float32)
        mW0 = jax.random.normal(ks[7], (RB, HID), jnp.float32) * math.sqrt(1.0 / RB)
        mb0 = jnp.zeros((HID,), jnp.float32)
        mW1 = jax.random.normal(ks[8], (HID, HID), jnp.float32) * math.sqrt(1.0 / HID)
        mb1 = jnp.zeros((HID,), jnp.float32)
        mW2 = jax.random.normal(ks[9], (HID, 4 * MUL), jnp.float32) * math.sqrt(1.0 / HID)
        mb2 = jnp.zeros((4 * MUL,), jnp.float32)
        W2_s = jax.random.normal(ks[10], (2 * MUL, 2 * MUL), jnp.float32)
        W2_v = jax.random.normal(ks[11], (2 * MUL, MUL), jnp.float32)
        Ws_s = jax.random.normal(ks[12], (MUL, MUL), jnp.float32)
        Ws_v = jax.random.normal(ks[13], (MUL, MUL), jnp.float32)
        return {'x': x, 'senders': senders, 'receivers': receivers, 'sh': sh, 'rb': rb, 'W1_s': W1_s, 'W1_v': W1_v, 'mW0': mW0, 'mb0': mb0, 'mW1': mW1, 'mb1': mb1, 'mW2': mW2, 'mb2': mb2, 'W2_s': W2_s, 'W2_v': W2_v, 'Ws_s': Ws_s, 'Ws_v': Ws_v}
    _L2_gnn_all = _L2_gnn_setup()
    _L2_gnn_in = {k: v for k, v in _L2_gnn_all.items() if k in ('W1_s', 'W1_v', 'mW0', 'mb0', 'mW1', 'mb1', 'mW2', 'mb2', 'W2_s', 'W2_v', 'Ws_s', 'Ws_v')}
    del _L2_gnn_all

    def _L3_gnn_setup():
        import jax, jax.numpy as jnp
        import numpy as np
        N_NODES = 6250
        N_EDGES = 62500
        EMB_DIM = 128
        NEG_SLOPE = 0.01
        key = jax.random.key(seed)
        k1, k2, k3, k4 = jax.random.split(key, 4)
        x = jax.random.normal(k1, (N_NODES, EMB_DIM), dtype=jnp.float32)
        edge_index = jax.random.randint(k2, (2, N_EDGES), 0, N_NODES, dtype=jnp.int64)
        edge_attrs = jax.random.uniform(k3, (N_EDGES,), dtype=jnp.float32)
        limit = float(np.sqrt(6.0 / (EMB_DIM + EMB_DIM)))
        W1_w = jax.random.uniform(k4, (EMB_DIM, EMB_DIM), dtype=jnp.float32, minval=-limit, maxval=limit)
        W1_b = jnp.zeros((EMB_DIM,), dtype=jnp.float32)
        return {'x': x, 'edge_index': edge_index, 'edge_attrs': edge_attrs, 'W1_w': W1_w, 'W1_b': W1_b}
    _L3_gnn_all = _L3_gnn_setup()
    _L3_gnn_in = {k: v for k, v in _L3_gnn_all.items() if k in ('W1_w', 'W1_b')}
    del _L3_gnn_all
    return {'x': x, 'src': src, 'dst': dst, 'edge_attr_4': edge_attr_4, 'edge_attr_8': edge_attr_8, 'edge_weight': edge_weight, 'L0_gnn_l1_Wl': _L0_gnn_in['l1_Wl'], 'L0_gnn_l1_bl': _L0_gnn_in['l1_bl'], 'L0_gnn_l1_Wr': _L0_gnn_in['l1_Wr'], 'L0_gnn_l1_br': _L0_gnn_in['l1_br'], 'L0_gnn_l1_att': _L0_gnn_in['l1_att'], 'L0_gnn_l1_Wres': _L0_gnn_in['l1_Wres'], 'L0_gnn_l1_bias': _L0_gnn_in['l1_bias'], 'L0_gnn_l2_Wl': _L0_gnn_in['l2_Wl'], 'L0_gnn_l2_bl': _L0_gnn_in['l2_bl'], 'L0_gnn_l2_Wr': _L0_gnn_in['l2_Wr'], 'L0_gnn_l2_br': _L0_gnn_in['l2_br'], 'L0_gnn_l2_att': _L0_gnn_in['l2_att'], 'L0_gnn_l2_Wres': _L0_gnn_in['l2_Wres'], 'L0_gnn_l2_bias': _L0_gnn_in['l2_bias'], 'L1_gnn_W1': _L1_gnn_in['W1'], 'L1_gnn_b1': _L1_gnn_in['b1'], 'L1_gnn_W2': _L1_gnn_in['W2'], 'L1_gnn_b2': _L1_gnn_in['b2'], 'L1_gnn_U1': _L1_gnn_in['U1'], 'L1_gnn_c1': _L1_gnn_in['c1'], 'L1_gnn_U2': _L1_gnn_in['U2'], 'L1_gnn_c2': _L1_gnn_in['c2'], 'L2_gnn_W1_s': _L2_gnn_in['W1_s'], 'L2_gnn_W1_v': _L2_gnn_in['W1_v'], 'L2_gnn_mW0': _L2_gnn_in['mW0'], 'L2_gnn_mb0': _L2_gnn_in['mb0'], 'L2_gnn_mW1': _L2_gnn_in['mW1'], 'L2_gnn_mb1': _L2_gnn_in['mb1'], 'L2_gnn_mW2': _L2_gnn_in['mW2'], 'L2_gnn_mb2': _L2_gnn_in['mb2'], 'L2_gnn_W2_s': _L2_gnn_in['W2_s'], 'L2_gnn_W2_v': _L2_gnn_in['W2_v'], 'L2_gnn_Ws_s': _L2_gnn_in['Ws_s'], 'L2_gnn_Ws_v': _L2_gnn_in['Ws_v'], 'L3_gnn_W1_w': _L3_gnn_in['W1_w'], 'L3_gnn_W1_b': _L3_gnn_in['W1_b']}

def reference(x, src, dst, edge_attr_4, edge_attr_8, edge_weight, L0_gnn_l1_Wl, L0_gnn_l1_bl, L0_gnn_l1_Wr, L0_gnn_l1_br, L0_gnn_l1_att, L0_gnn_l1_Wres, L0_gnn_l1_bias, L0_gnn_l2_Wl, L0_gnn_l2_bl, L0_gnn_l2_Wr, L0_gnn_l2_br, L0_gnn_l2_att, L0_gnn_l2_Wres, L0_gnn_l2_bias, L1_gnn_W1, L1_gnn_b1, L1_gnn_W2, L1_gnn_b2, L1_gnn_U1, L1_gnn_c1, L1_gnn_U2, L1_gnn_c2, L2_gnn_W1_s, L2_gnn_W1_v, L2_gnn_mW0, L2_gnn_mb0, L2_gnn_mW1, L2_gnn_mb1, L2_gnn_mW2, L2_gnn_mb2, L2_gnn_W2_s, L2_gnn_W2_v, L2_gnn_Ws_s, L2_gnn_Ws_v, L3_gnn_W1_w, L3_gnn_W1_b):
    import jax
    import jax.numpy as jnp

    def _L0_gnn_ref(edge_index, emb, l1_Wl, l1_bl, l1_Wr, l1_br, l1_att, l1_Wres, l1_bias, l2_Wl, l2_bl, l2_Wr, l2_br, l2_att, l2_Wres, l2_bias):
        import jax, jax.numpy as jnp
        import numpy as np
        N = 6250
        E = 40000
        C = 128
        NEG_SLOPE = 0.2

        def _param(key, shape, scale=0.1):
            return jax.random.normal(key, shape, dtype=jnp.float32) * scale

        def gatv2_layer(x, Wl, bl, Wr, br, att, Wres, bias, src, dst):
            xl = x @ Wl.T + bl
            xr = x @ Wr.T + br
            m = jax.nn.leaky_relu(xl[src] + xr[dst], NEG_SLOPE)
            e = m @ att
            emax = jax.ops.segment_max(e, dst, num_segments=N)
            ex = jnp.exp(e - emax[dst])
            denom = jax.ops.segment_sum(ex, dst, num_segments=N)
            alpha = ex / denom[dst]
            out = jax.ops.segment_sum(alpha[:, None] * xl[src], dst, num_segments=N)
            return out + x @ Wres.T + bias
        loops = jnp.arange(N, dtype=edge_index.dtype)
        src = jnp.concatenate([edge_index[0], loops])
        dst = jnp.concatenate([edge_index[1], loops])
        h = gatv2_layer(emb, l1_Wl, l1_bl, l1_Wr, l1_br, l1_att, l1_Wres, l1_bias, src, dst)
        h = jax.nn.relu(h)
        out = gatv2_layer(h, l2_Wl, l2_bl, l2_Wr, l2_br, l2_att, l2_Wres, l2_bias, src, dst)
        return out

    def _L1_gnn_ref(h, w, src, dst, W1, b1, W2, b2, U1, c1, U2, c2):
        import jax, jax.numpy as jnp
        import numpy as np
        N = 6250
        E = 50000
        D = 128
        n = h.shape[0]
        msg_in = jnp.concatenate([h[src], h[dst], w[:, None]], axis=1)
        msg = jax.nn.relu(msg_in @ W1 + b1) @ W2 + b2
        agg = jax.ops.segment_max(msg, dst, num_segments=n)
        deg = jax.ops.segment_sum(jnp.ones((dst.shape[0],), jnp.int32), dst, num_segments=n)
        agg = jnp.where((deg > 0)[:, None], agg, jnp.zeros((), h.dtype))
        upd_in = jnp.concatenate([h, agg], axis=1)
        return jax.nn.relu(upd_in @ U1 + c1) @ U2 + c2

    def _L2_gnn_ref(x, senders, receivers, sh, rb, W1_s, W1_v, mW0, mb0, mW1, mb1, mW2, mb2, W2_s, W2_v, Ws_s, Ws_v):
        import jax, jax.numpy as jnp
        import numpy as np
        import math
        MUL = 32
        N_NODES = 3125
        N_EDGES = 50000
        RB = 8
        HID = 64
        AVG_N = 16.0
        SILU_C = 1.6790524
        INV_SQRT3 = 1.0 / math.sqrt(3.0)

        def _forward(x, sh, rb, W1_s, W1_v, mW0, mb0, mW1, mb1, mW2, mb2, W2_s, W2_v, Ws_s, Ws_v, senders, receivers):
            N = x.shape[0]
            E = senders.shape[0]
            s = x[:, :MUL]
            v = x[:, MUL:].reshape(N, MUL, 3)
            inv = 1.0 / math.sqrt(MUL)
            s1 = s @ W1_s * inv
            v1 = jnp.einsum('nud,uv->nvd', v, W1_v) * inv
            h = jax.nn.silu(rb @ mW0 + mb0)
            h = jax.nn.silu(h @ mW1 + mb1)
            w = h @ mW2 + mb2
            w0, w1, w2, w3 = jnp.split(w, 4, axis=-1)
            xs = s1[senders]
            xv = v1[senders]
            sh0 = sh[:, :1]
            sh1 = sh[:, 1:]
            m0 = w0 * xs * sh0
            m1 = w1 * jnp.einsum('eud,ed->eu', xv, sh1) * INV_SQRT3
            m2 = w2[:, :, None] * xs[:, :, None] * sh1[:, None, :]
            m3 = w3[:, :, None] * xv * sh0[:, :, None]
            msg = jnp.concatenate([m0, m1, m2.reshape(E, 3 * MUL), m3.reshape(E, 3 * MUL)], axis=-1)
            agg = jax.ops.segment_sum(msg, receivers, num_segments=N) / math.sqrt(AVG_N)
            a_s = agg[:, :2 * MUL]
            a_v = agg[:, 2 * MUL:].reshape(N, 2 * MUL, 3)
            inv2 = 1.0 / math.sqrt(2 * MUL)
            g_s = a_s @ W2_s * inv2
            g_v = jnp.einsum('nud,uv->nvd', a_v, W2_v) * inv2
            extra = jax.nn.silu(g_s[:, :MUL]) * SILU_C
            gates = jax.nn.silu(g_s[:, MUL:]) * SILU_C
            gated_v = gates[:, :, None] * g_v
            skip_s = s @ Ws_s * inv
            skip_v = jnp.einsum('nud,uv->nvd', v, Ws_v) * inv
            out_s = extra + skip_s
            out_v = gated_v + skip_v
            return jnp.concatenate([out_s, out_v.reshape(N, 3 * MUL)], axis=-1)
        return _forward(x, sh, rb, W1_s, W1_v, mW0, mb0, mW1, mb1, mW2, mb2, W2_s, W2_v, Ws_s, Ws_v, senders, receivers)

    def _L3_gnn_ref(x, edge_index, edge_attrs, W1_w, W1_b):
        import jax, jax.numpy as jnp
        import numpy as np
        N_NODES = 6250
        N_EDGES = 62500
        EMB_DIM = 128
        NEG_SLOPE = 0.01
        n = x.shape[0]
        from_, to_ = (edge_index[0], edge_index[1])
        deg = jax.ops.segment_sum(jnp.ones((to_.shape[0],), dtype=x.dtype), to_, num_segments=n)
        deg_inv = jnp.where(deg > 0, 1.0 / jnp.sqrt(deg), 0.0)
        norm = deg_inv[from_] * deg_inv[to_]
        x_i = x[from_]
        x_j = x[to_]
        m_j = norm[:, None] * (x_j + x_j * x_i @ W1_w.T + W1_b)
        out = jax.ops.segment_sum(m_j, to_, num_segments=n)
        out = jnp.where(out >= 0, out, NEG_SLOPE * out)
        return out
    edge_index = jnp.stack([src, dst])
    x = _layernorm(x + _L0_gnn_ref(edge_index, x, L0_gnn_l1_Wl, L0_gnn_l1_bl, L0_gnn_l1_Wr, L0_gnn_l1_br, L0_gnn_l1_att, L0_gnn_l1_Wres, L0_gnn_l1_bias, L0_gnn_l2_Wl, L0_gnn_l2_bl, L0_gnn_l2_Wr, L0_gnn_l2_br, L0_gnn_l2_att, L0_gnn_l2_Wres, L0_gnn_l2_bias), axis=-1)
    x = _layernorm(x + _L1_gnn_ref(x, edge_weight, src, dst, L1_gnn_W1, L1_gnn_b1, L1_gnn_W2, L1_gnn_b2, L1_gnn_U1, L1_gnn_c1, L1_gnn_U2, L1_gnn_c2), axis=-1)
    x = _layernorm(x + _L2_gnn_ref(x, src, dst, edge_attr_4, edge_attr_8, L2_gnn_W1_s, L2_gnn_W1_v, L2_gnn_mW0, L2_gnn_mb0, L2_gnn_mW1, L2_gnn_mb1, L2_gnn_mW2, L2_gnn_mb2, L2_gnn_W2_s, L2_gnn_W2_v, L2_gnn_Ws_s, L2_gnn_Ws_v), axis=-1)
    x = _layernorm(x + _L3_gnn_ref(x, edge_index, edge_weight, L3_gnn_W1_w, L3_gnn_W1_b), axis=-1)
    return x

_drawn_inputs = setup_inputs


def setup_inputs(seed=0):
    import zlib

    import numpy as np

    out = dict(_drawn_inputs(seed))
    spreads = {'L1_gnn_b1': (0.0, 0.8),
     'L1_gnn_b2': (0.0, 0.375),
     'L1_gnn_c1': (0.0, 0.1),
     'L1_gnn_c2': (0.0, 0.1),
     'L2_gnn_mb0': (0.0, 0.444),
     'L2_gnn_mb1': (0.0, 0.1),
     'L2_gnn_mb2': (0.0, 0.1),
     'L3_gnn_W1_b': (0.0, 0.1)}
    factors = {'edge_weight': 200.0, 'L0_gnn_l1_br': 5.306, 'L0_gnn_l2_br': 8.0}
    for name, (base, spread) in spreads.items():
        noise = np.random.default_rng([zlib.crc32(name.encode()), seed]).standard_normal(out[name].shape)
        drawn = base * np.exp(spread * noise) if base else spread * noise
        out[name] = jnp.asarray(drawn.astype(out[name].dtype))
    for name, factor in factors.items():
        out[name] = (out[name] * factor).astype(out[name].dtype)
    return out
```

```python
from contextlib import ExitStack

import concourse.bass as bass
from concourse import mybir

P = 128
NODES = 6250
EDGES = 100000
D = 128
WINDOWS = -(-NODES // P)
NPAD = WINDOWS * P
GROUP = 4
UNROLL = 8
STEP = GROUP * UNROLL
BLOCKS = 7
TABLE = BLOCKS * P
TILES_B = -(-(EDGES // P + WINDOWS + 1) // STEP) * STEP
TILES_A = -(-(EDGES // P + 2 * WINDOWS + 1) // STEP) * STEP
TAIL = P * 116
EDGE0 = NPAD
BATCH = 7
NBATCH = WINDOWS // BATCH
COUNT_P = 125
BIG = 1e30
FAR = 1000000
EPS = 1e-5

F32 = mybir.dt.float32
I32 = mybir.dt.int32
ALU = mybir.AluOpType
ACT = mybir.ActivationFunctionType
AX = mybir.AxisListType
assert TILES_A <= TABLE and NBATCH * BATCH == WINDOWS and COUNT_P * 800 == EDGES


def wait(eng, sem, value):
    if isinstance(value, int) and value <= 0:
        return
    eng.wait_ge(sem, value)


def uses(q, r, ring):
    return r * (UNROLL // ring) + q // ring


def run_groups(eng, groups, stages):
    last = max(lag for lag, _ in stages)

    def peeled(g):
        for lag, f in stages:
            if 0 <= g - lag < groups:
                f(g - lag, (g - lag) % UNROLL, (g - lag) // UNROLL)

    head = 2 * UNROLL
    for g in range(head):
        peeled(g)
    with eng.Fori(head // UNROLL, groups // UNROLL) as r:
        for q in range(UNROLL):
            for lag, f in stages:
                back = (lag - q + UNROLL - 1) // UNROLL if lag > q else 0
                f(r * UNROLL + (q - lag), (q - lag) % UNROLL, r - back)
    for g in range(groups, groups + last):
        peeled(g)


class Chain:

    def __init__(self, eng, sem, start=0):
        self.eng, self.sem, self.start, self.n = eng, sem, start, 0

    def __call__(self, instruction):
        self.n += 1
        instruction.then_inc(self.sem, 1)
        self.eng.wait_ge(self.sem, self.start + self.n)


def bcast_mid(ap, n):
    return ap.unsqueeze(1).to_broadcast([ap.shape[0], n, ap.shape[1]])


def bcast_last(ap, n):
    return ap.unsqueeze(2).to_broadcast([ap.shape[0], ap.shape[1], n])


class Store:
    pass


def allocate(nc, ctx, t):
    def sb(name, shape, dt=F32):
        return ctx.enter_context(nc.sbuf_tensor(name, shape, dt))

    def dram(name, shape, dt=F32):
        return nc.dram_tensor(name, shape, dt, kind="Internal").ap()

    t.iota_f = sb("iota_f", [P, P])
    t.iota_p = sb("iota_p", [P, 1])
    t.ident = sb("ident", [P, P])
    t.ones = sb("ones", [P, P])
    t.window = {x: sb(f"window_{x}", [P, BLOCKS]) for x in "AB"}
    t.start = {x: sb(f"start_{x}", [P, BLOCKS]) for x in "AB"}
    t.offsets = {n: sb(f"offsets_{n}", [P, BLOCKS], I32) for n in ("A", "B", "Bprev", "ew", "ea4", "ea8")}
    t.last_tile = {x: sb(f"last_tile_{x}", [P, WINDOWS], I32) for x in "AB"}
    t.filled = sb("filled", [P, WINDOWS])
    t.window_row = {x: sb(f"window_row_{x}", [1, TABLE], I32) for x in "AB"}
    t.same = {x: sb(f"same_{x}", [P, TABLE]) for x in "AB"}
    t.newwin = sb("newwin", [P, TABLE])
    t.src = {x: sb(f"src_{x}", [P, TABLE], I32) for x in "AB"}
    t.dstrel = {x: sb(f"dstrel_{x}", [P, TABLE]) for x in "AB"}
    t.lastrel = sb("lastrel", [P, TABLE])
    t.dinv_sb = sb("dinv_sb", [P, WINDOWS])
    t.ea4 = sb("ea4", [P, TABLE, 4])
    t.ea8 = sb("ea8", [P, TABLE, 8])

    t.dst_all = dram("dst_all", [EDGE0 + EDGES + TAIL], I32)
    t.src_all = dram("src_all", [EDGE0 + EDGES + TAIL], I32)
    t.ew_all = dram("ew_all", [EDGES + TAIL])
    t.ea4_all = dram("ea4_all", [(EDGES + TAIL) * 4])
    t.ea8_all = dram("ea8_all", [(EDGES + TAIL) * 8])
    t.x_pad = dram("x_pad", [NPAD, D])
    t.win_f = {x: dram(f"win_f_{x}", [TABLE]) for x in "AB"}
    t.win_i = {x: dram(f"win_i_{x}", [TABLE], I32) for x in "AB"}
    t.dst_rows = {x: dram(f"dst_rows_{x}", [TABLE, P]) for x in "AB"}
    t.seg_rows = dram("seg_rows", [TABLE, P])
    t.ew_rows = dram("ew_rows", [TABLE, P])
    t.xl = [dram(f"xl{i}", [NPAD, D + 1]) for i in range(2)]
    t.xr = [dram(f"xr{i}", [NPAD, D + 1]) for i in range(2)]
    t.res = [dram(f"res{i}", [NPAD, D]) for i in range(2)]
    t.x1 = dram("x1", [NPAD, D])
    t.ha = dram("ha", [NPAD, D])
    t.hb = dram("hb", [NPAD, D])
    t.x2 = dram("x2", [NPAD, D])
    t.sv = dram("sv", [NPAD, D])
    t.skip = dram("skip", [NPAD, D])
    t.x3 = dram("x3", [NPAD, D])
    t.xd = dram("xd", [NPAD, D + 1])
    t.slab_att = [dram(f"slab_att{i}", [TILES_A, P, D + 1]) for i in range(2)]
    t.slab_max = dram("slab_max", [TILES_B, P, D + 1])
    t.slab_equi = dram("slab_equi", [TILES_B, P, 2 * D])
    t.slab_norm = dram("slab_norm", [TILES_B, P, D + 1])


def prepare_schedule(nc, t, x, src, dst, edge_weight, edge_attr_4, edge_attr_8):
    with nc.cleanup_on_exit(), ExitStack() as ctx:
        def sem(name):
            return nc.alloc_semaphore("ps" + "_" + name)

        def sb(name, shape, dt=F32):
            return ctx.enter_context(nc.sbuf_tensor("ps_" + name, shape, dt))

        iota_fi = sb("iota_fi", [P, P], I32)
        iota_pi = sb("iota_pi", [P, 1], I32)
        self_id = sb("self_id", [P, WINDOWS], I32)
        tile_i = sb("tile_i", [P, BLOCKS], I32)
        zeros = sb("zeros", [P, 8 * TAIL // P])
        zeros_i = sb("zeros_i", [P, TAIL // P], I32)
        far = sb("far", [P, TAIL // P], I32)
        dst_i = sb("dst_i", [COUNT_P, 800], I32)
        dst_f = sb("dst_f", [COUNT_P, 800])
        junk = sb("junk", [P, 800])
        below = sb("below", [P, WINDOWS - 1])
        first = sb("first", [P, WINDOWS + 1])
        count = sb("count", [P, WINDOWS])
        rounded = sb("rounded", [P, WINDOWS])
        tiles_i = sb("tiles_i", [P, WINDOWS], I32)
        tiles_s = sb("tiles_s", [P, WINDOWS], I32)
        tiles = sb("tiles", [P, WINDOWS])
        tile0 = {k: sb(f"tile0_{k}", [P, WINDOWS + 1]) for k in "AB"}
        shift = {k: sb(f"shift_{k}", [P, WINDOWS]) for k in "AB"}
        last_f = {k: sb(f"last_f_{k}", [P, WINDOWS]) for k in "AB"}
        tile_f = sb("tile_f", [P, BLOCKS])
        ssum = {k: sb(f"ssum_{k}", [P, BLOCKS]) for k in "AB"}
        isself = sb("isself", [P, BLOCKS])
        pos = sb("pos", [P, BLOCKS])
        gap = sb("gap", [P, BLOCKS])
        edge_f = sb("edge_f", [P, BLOCKS])
        win_i = {k: sb(f"win_i_{k}", [P, BLOCKS], I32) for k in "AB"}
        total = ctx.enter_context(nc.psum_tensor("ps_total", [P, 512], F32))

        s_iota = sem("s_iota")
        s_fill = sem("s_fill")
        s_copy = sem("s_copy")
        s_dst = sem("s_dst")
        s_dve = sem("s_dve")
        s_counted = sem("s_counted")
        s_total = sem("s_total")
        s_windows = sem("s_windows")
        s_lists = sem("s_lists")

        with nc.Block() as block:
            @block.gpsimd
            def _(pool):
                pool.iota(iota_fi[:, :], pattern=[[1, P]], base=0, channel_multiplier=0).then_inc(s_iota, 1)
                pool.iota(iota_pi[:, :], pattern=[[0, 1]], base=0, channel_multiplier=1).then_inc(s_iota, 1)
                pool.iota(tile_i[:, :], pattern=[[P, BLOCKS]], base=0, channel_multiplier=1).then_inc(s_iota, 1)
                pool.iota(self_id[:, :], pattern=[[1, WINDOWS]], base=0, channel_multiplier=WINDOWS).then_inc(s_fill, 1)
                pool.memset(zeros[:, :], 0.0).then_inc(s_fill, 1)
                pool.memset(zeros_i[:, :], 0).then_inc(s_fill, 1)
                pool.memset(far[:, :], FAR).then_inc(s_fill, 1)

            @block.sync
            def _(sp):
                sp.dma_start(dst_i[:, :], dst.rearrange("(p j) -> p j", p=COUNT_P)).then_inc(s_dst, 16)
                sp.dma_start(t.dst_all[EDGE0:EDGE0 + EDGES].rearrange("(p j) -> p j", p=P // 4),
                             dst.rearrange("(p j) -> p j", p=P // 4)).then_inc(s_copy, 16)
                sp.dma_start(t.src_all[EDGE0:EDGE0 + EDGES].rearrange("(p j) -> p j", p=P // 4),
                             src.rearrange("(p j) -> p j", p=P // 4)).then_inc(s_copy, 16)
                sp.dma_start(t.ew_all[0:EDGES].rearrange("(p j) -> p j", p=P // 4),
                             edge_weight.rearrange("(p j) -> p j", p=P // 4)).then_inc(s_copy, 16)
                sp.dma_start(t.ea4_all[0:EDGES * 4].rearrange("(p j) -> p j", p=P // 4),
                             edge_attr_4.rearrange("(p j) k -> p (j k)", p=P // 4)).then_inc(s_copy, 16)
                sp.dma_start(t.ea8_all[0:EDGES * 8].rearrange("(p j) -> p j", p=P // 4),
                             edge_attr_8.rearrange("(p j) k -> p (j k)", p=P // 4)).then_inc(s_copy, 16)
                sp.dma_start(t.x_pad[0:NODES, :], x).then_inc(s_copy, 16)
                sp.wait_ge(s_fill, 4)
                for a in (t.dst_all, t.src_all):
                    sp.dma_start(a[0:NPAD].rearrange("(p j) -> p j", p=P), self_id[:, :]).then_inc(s_copy, 16)
                sp.dma_start(t.dst_all[EDGE0 + EDGES:].rearrange("(p j) -> p j", p=P), far[:, :]).then_inc(s_copy, 16)
                sp.dma_start(t.src_all[EDGE0 + EDGES:].rearrange("(p j) -> p j", p=P), zeros_i[:, :]).then_inc(s_copy, 16)
                for a, k in ((t.ew_all, 1), (t.ea4_all, 4), (t.ea8_all, 8)):
                    sp.dma_start(a[k * EDGES:].rearrange("(p j) -> p j", p=P), zeros[:, 0:k * TAIL // P]).then_inc(s_copy, 16)
                sp.dma_start(t.x_pad[NODES:NPAD, :], zeros[0:NPAD - NODES, 0:D]).then_inc(s_copy, 16)
                sp.wait_ge(s_copy, 16 * 14)
                sp.wait_ge(s_windows, 1)
                for k in "AB":
                    sp.dma_start(t.win_f[k].rearrange("(b p) -> p b", p=P), t.window[k][:, :],
                                 allow_slow_non_contiguous=True).then_inc(s_lists, 16)
                    sp.dma_start(t.win_i[k].rearrange("(b p) -> p b", p=P), win_i[k][:, :],
                                 allow_slow_non_contiguous=True).then_inc(s_lists, 16)
                sp.wait_ge(s_lists, 64)

            @block.tensor
            def _(pe):
                pe.wait_ge(s_counted, 1)
                pe.matmul(total[:, 0:WINDOWS - 1], t.ones[0:COUNT_P, :], below[0:COUNT_P, :],
                          start=True, stop=True).then_inc(s_total, 1)

            @block.vector
            def _(dve):
                step = Chain(dve, s_dve)
                dve.wait_ge(s_iota, 3)
                step(dve.tensor_copy(t.iota_f[:, :], iota_fi[:, :]))
                step(dve.tensor_copy(t.iota_p[:, :], iota_pi[:, :]))
                step(dve.tensor_copy(tile_f[:, :], tile_i[:, :]))
                step(dve.memset(t.ones[:, :], 1.0))
                step(dve.tensor_scalar(t.ident[:, :], t.iota_f[:, :], t.iota_p[:, :], None, ALU.is_equal))
                dve.wait_ge(s_dst, 16)
                step(dve.tensor_copy(dst_f[:, :], dst_i[:, :]))
                for w in range(1, WINDOWS):
                    step(dve.tensor_scalar(junk[0:COUNT_P, :], dst_f[:, :], float(P * w), 0.0, ALU.is_lt, ALU.add,
                                           accum_out=below[0:COUNT_P, w - 1:w]))
                dve.engine_nop().then_inc(s_counted, 1)
                dve.wait_ge(s_total, 1)
                step(dve.memset(first[:, 0:1], 0.0))
                step(dve.tensor_copy(first[:, 1:WINDOWS], total[:, 0:WINDOWS - 1]))
                step(dve.memset(first[:, WINDOWS:], float(EDGES)))
                step(dve.tensor_tensor(count[:, :], first[:, 1:], first[:, 0:WINDOWS], ALU.subtract))
                step(dve.tensor_scalar(rounded[:, :], count[:, :], float(P - 1), None, ALU.add))
                step(dve.tensor_copy(tiles_i[:, :], rounded[:, :]))
                step(dve.tensor_scalar(tiles_s[:, :], tiles_i[:, :], 7, None, ALU.logical_shift_right))
                step(dve.tensor_copy(tiles[:, :], tiles_s[:, :]))
                step(dve.tensor_scalar(t.filled[:, :], tiles[:, :], 1.0, None, ALU.min))
                step(dve.memset(tile0["B"][:, 0:1], 0.0))
                step(dve.tensor_tensor_scan(tile0["B"][:, 1:], t.ones[:, 0:WINDOWS], tiles[:, :], 0.0, ALU.mult, ALU.add))
                step(dve.tensor_tensor(tile0["A"][:, :], tile0["B"][:, :], t.iota_f[:, 0:WINDOWS + 1], ALU.add))
                step(dve.scalar_tensor_tensor(out=shift["B"][:, :], in0=tiles[:, :], scalar=-float(P), in1=count[:, :],
                                              op0=ALU.mult, op1=ALU.add))
                step(dve.tensor_scalar(shift["A"][:, :], shift["B"][:, :], -float(P), None, ALU.add))
                step(dve.tensor_scalar(shift["A"][:, WINDOWS - 1:], shift["A"][:, WINDOWS - 1:], float(P), None, ALU.add))
                for k in "AB":
                    step(dve.tensor_scalar(last_f[k][:, :], tile0[k][:, 1:], -1.0, 0.0, ALU.add, ALU.max))
                    step(dve.tensor_copy(t.last_tile[k][:, :], last_f[k][:, :]))
                    for b in range(BLOCKS):
                        tile = tile_f[:, b:b + 1]
                        step(dve.tensor_scalar(junk[:, 0:WINDOWS - 1], tile0[k][:, 1:WINDOWS], tile, 0.0, ALU.is_le, ALU.add,
                                               accum_out=t.window[k][:, b:b + 1]))
                        step(dve.scalar_tensor_tensor(out=junk[:, 0:WINDOWS], in0=tile0[k][:, 1:], scalar=tile, in1=shift[k][:, :],
                                                      op0=ALU.is_le, op1=ALU.mult, accum_out=ssum[k][:, b:b + 1]))
                        if k == "A":
                            step(dve.tensor_scalar(junk[:, 0:WINDOWS], tile0["A"][:, 0:WINDOWS], tile, 0.0, ALU.is_equal, ALU.add,
                                                   accum_out=isself[:, b:b + 1]))
                    step(dve.tensor_copy(win_i[k][:, :], t.window[k][:, :]))
                    step(dve.scalar_tensor_tensor(out=pos[:, :], in0=tile_f[:, :], scalar=float(P), in1=ssum[k][:, :],
                                                  op0=ALU.mult, op1=ALU.add))
                    if k == "B":
                        step(dve.tensor_scalar(t.start["B"][:, :], pos[:, :], float(EDGE0), None, ALU.add))
                    else:
                        step(dve.tensor_scalar(t.start["A"][:, :], pos[:, :], float(EDGE0 - P), None, ALU.add))
                        step(dve.scalar_tensor_tensor(out=gap[:, :], in0=t.window["A"][:, :], scalar=float(P), in1=t.start["A"][:, :],
                                                      op0=ALU.mult, op1=ALU.subtract))
                        step(dve.tensor_tensor(gap[:, :], gap[:, :], isself[:, :], ALU.mult))
                        step(dve.tensor_tensor(t.start["A"][:, :], t.start["A"][:, :], gap[:, :], ALU.add))
                    step(dve.tensor_copy(t.offsets[k][:, :], t.start[k][:, :]))
                dve.engine_nop().then_inc(s_windows, 1)
                step(dve.tensor_scalar(edge_f[:, :], t.start["B"][:, :], -1.0, None, ALU.add))
                step(dve.tensor_copy(t.offsets["Bprev"][:, :], edge_f[:, :]))
                for name, k in (("ew", 1), ("ea4", 4), ("ea8", 8)):
                    step(dve.tensor_scalar(edge_f[:, :], t.start["B"][:, :], -float(EDGE0), float(k), ALU.add, ALU.mult))
                    step(dve.tensor_copy(t.offsets[name][:, :], edge_f[:, :]))


def prepare_tables(nc, t):
    with nc.cleanup_on_exit(), ExitStack() as ctx:
        def sem(name):
            return nc.alloc_semaphore("pt" + "_" + name)

        def sb(name, shape, dt=F32):
            return ctx.enter_context(nc.sbuf_tensor("pt_" + name, shape, dt))

        src_i = {k: sb(f"src_i_{k}", [P, BLOCKS, P], I32) for k in "AB"}
        src_f = {k: sb(f"src_f_{k}", [P, BLOCKS, P]) for k in "AB"}
        width = {"A": P, "B": P + 2}
        dst_i = {k: sb(f"dst_i_{k}", [P, BLOCKS, width[k]], I32) for k in "AB"}
        dst_f = {k: sb(f"dst_f_{k}", [P, BLOCKS, width[k]]) for k in "AB"}
        rel = {k: sb(f"rel_{k}", [P, BLOCKS, P]) for k in "AB"}
        w128 = {k: sb(f"w128_{k}", [P, BLOCKS]) for k in "AB"}
        seg = sb("seg", [P, BLOCKS, P])
        last = sb("last", [P, BLOCKS, P])
        ew = sb("ew", [P, BLOCKS, P])
        ea4 = sb("ea4", [P, 1, P * 4])
        ea8 = sb("ea8", [P, 1, P * 8])
        wrow = {k: sb(f"wrow_{k}", [P, TABLE]) for k in "AB"}
        bank = ctx.enter_context(nc.psum_tensor("pt_bank", [P, 4, 512], F32))

        s_rows = sem("s_rows")
        s_ew = sem("s_ew")
        s_attr = sem("s_attr")
        s_wrow = sem("s_wrow")
        s_dve = sem("s_dve2")
        s_ready = sem("s_ready")
        s_turned = sem("s_turned")
        s_taken = sem("s_taken")
        s_saved = sem("s_saved")

        turns = []
        for k in "AB":
            for b in range(BLOCKS):
                turns.append((rel[k][:, b, :], t.dstrel[k][:, b * P:(b + 1) * P]))
                turns.append((src_f[k][:, b, :], t.src[k][:, b * P:(b + 1) * P]))
        for b in range(BLOCKS):
            turns.append((last[:, b, :], t.lastrel[:, b * P:(b + 1) * P]))
        plain = len(turns)
        a4 = ea4[:, 0, :].rearrange("p (e k) -> p k e", k=4)
        a8 = ea8[:, 0, :].rearrange("p (e k) -> p k e", k=8)
        for b in range(BLOCKS):
            turns += [(a4[:, k, :], t.ea4[:, b * P:(b + 1) * P, k]) for k in range(4)]
            turns += [(a8[:, k, :], t.ea8[:, b * P:(b + 1) * P, k]) for k in range(8)]

        def gather(pool, out, source, name, b):
            return pool.indirect_dma_start(
                out=out, out_offset=None, in_=source.rearrange("(n o) -> n o", o=1),
                in_offset=bass.IndirectOffsetOnAxis(ap=t.offsets[name][:, b:b + 1], axis=0))

        with nc.Block() as block:
            @block.gpsimd
            def _(pool):
                for b in range(BLOCKS):
                    for k in "AB":
                        gather(pool, src_i[k][:, b, :], t.src_all, k, b).then_inc(s_rows, 16)
                        gather(pool, dst_i[k][:, b, :], t.dst_all, "A" if k == "A" else "Bprev", b).then_inc(s_rows, 16)
                    gather(pool, ew[:, b, :], t.ew_all, "ew", b).then_inc(s_ew, 16)
                for b in range(BLOCKS):
                    wait(pool, s_turned, plain + 12 * b if b else 0)
                    gather(pool, ea4[:, 0, :], t.ea4_all, "ea4", b).then_inc(s_attr, 16)
                    gather(pool, ea8[:, 0, :], t.ea8_all, "ea8", b).then_inc(s_attr, 16)

            @block.sync
            def _(sp):
                for k in "AB":
                    sp.dma_start(wrow[k][:, :], t.win_f[k].rearrange("(o n) -> o n", o=1).to_broadcast([P, TABLE])).then_inc(s_wrow, 16)
                    sp.dma_start(t.window_row[k][:, :], t.win_i[k].rearrange("(o n) -> o n", o=1)).then_inc(s_wrow, 16)
                sp.wait_ge(s_wrow, 64)
                sp.wait_ge(s_ew, 16 * BLOCKS)
                sp.dma_start(t.ew_rows.rearrange("(b p) e -> p b e", p=P), ew[:, :, :]).then_inc(s_saved, 16)
                sp.wait_ge(s_ready, 3)
                for k in "AB":
                    sp.dma_start(t.dst_rows[k].rearrange("(b p) e -> p b e", p=P), rel[k][:, :, :]).then_inc(s_saved, 16)
                sp.dma_start(t.seg_rows.rearrange("(b p) e -> p b e", p=P), seg[:, :, :]).then_inc(s_saved, 16)
                sp.wait_ge(s_saved, 64)

            @block.vector
            def _(dve):
                step = Chain(dve, s_dve)
                dve.wait_ge(s_rows, 16 * 4 * BLOCKS)
                for k in "AB":
                    step(dve.tensor_scalar(w128[k][:, :], t.window[k][:, :], float(P), None, ALU.mult))
                    step(dve.tensor_copy(src_f[k][:, :, :], src_i[k][:, :, :]))
                    step(dve.tensor_copy(dst_f[k][:, :, :], dst_i[k][:, :, :]))
                    o = 0 if k == "A" else 1
                    step(dve.tensor_tensor(rel[k][:, :, :], dst_f[k][:, :, o:o + P], bcast_last(w128[k][:, :], P), ALU.subtract))
                    dve.engine_nop().then_inc(s_ready, 1)
                f = dst_f["B"]
                step(dve.tensor_tensor(seg[:, :, :], f[:, :, 1:P + 1], f[:, :, 0:P], ALU.not_equal))
                step(dve.tensor_scalar(seg[:, :, :], seg[:, :, :], -BIG, None, ALU.mult))
                step(dve.tensor_tensor(last[:, :, :], f[:, :, 1:P + 1], f[:, :, 2:P + 2], ALU.is_equal))
                step(dve.scalar_tensor_tensor(out=last[:, :, :].rearrange("p b e -> p (b e)"), in0=last[:, :, :].rearrange("p b e -> p (b e)"),
                                              scalar=float(FAR), in1=rel["B"][:, :, :].rearrange("p b e -> p (b e)"), op0=ALU.mult, op1=ALU.add))
                dve.engine_nop().then_inc(s_ready, 1)
                dve.wait_ge(s_wrow, 64)
                for k in "AB":
                    step(dve.memset(t.same[k][:, 0:1], 0.0))
                    step(dve.tensor_tensor(t.same[k][:, 1:], wrow[k][:, 1:], wrow[k][:, 0:TABLE - 1], ALU.is_equal))
                step(dve.tensor_scalar(t.newwin[:, :], t.same["A"][:, :], -1.0, BIG, ALU.add, ALU.mult))
                for n, (_, out) in enumerate(turns):
                    dve.wait_ge(s_turned, n + 1)
                    dve.tensor_copy(out, bank[:, n % 4, 0:P]).then_inc(s_taken, 1)

            @block.tensor
            def _(pe):
                pe.wait_ge(s_ready, 3)
                for n, (source, _) in enumerate(turns):
                    if n >= 4:
                        pe.wait_ge(s_taken, n - 3)
                    if n >= plain and (n - plain) % 12 == 0:
                        pe.wait_ge(s_attr, 32 * ((n - plain) // 12 + 1))
                    pe.transpose(bank[:, n % 4, 0:P], source, t.ident[:, :]).then_inc(s_turned, 1)


def gather_rows(pool, t, sched, groups, table, width, slots, rows, s_rows_used, used_per_group, s_index, s_gathered, s_tick):
    def stage(g, q, r):
        wait(pool, s_gathered[q], 16 * GROUP * r)
        wait(pool, s_rows_used, (g - UNROLL + 1) * used_per_group)
        pool.sem_inc(s_tick, 1)
        pool.tensor_copy(slots[:, q, :], t.src[sched][:, bass.ds(g * GROUP, GROUP)]).then_inc(s_index, 1)
        wait(pool, s_index, g + 1)
        pool.sem_inc(s_tick, 1)
        for j in range(GROUP):
            pool.indirect_dma_start(out=rows[:, q, j, 0:width], out_offset=None, in_=table,
                                    in_offset=bass.IndirectOffsetOnAxis(ap=slots[:, q, j:j + 1], axis=0)).then_inc(s_gathered[q], 16)
    run_groups(pool, groups, [(0, stage)])


def load_windows(nc, sp, t, sched, g, table, out, sem):
    _, windows = nc.values_load_multi_w_load_instructions(
        t.window_row[sched][0:1, bass.ds(g * GROUP, GROUP)], engines=[mybir.EngineType.SP], min_val=0, max_val=WINDOWS - 1)
    for j in range(GROUP):
        sp.dma_start(out[:, j, :], table.rearrange("(w p) d -> w p d", p=P)[bass.ds(windows[j], 1)]
                     .rearrange("w p d -> p (w d)")).then_inc(sem, 16)


def node_batch(ap, b):
    return ap[b * BATCH * P:(b + 1) * BATCH * P, :].rearrange("(w p) d -> p w d", p=P)


def load_last(nc, sp, t, sched, b, slab, out, sem):
    _, tiles = nc.values_load_multi_w_load_instructions(
        t.last_tile[sched][0:1, b * BATCH:(b + 1) * BATCH], engines=[mybir.EngineType.SP], min_val=0,
        max_val=(TILES_A if sched == "A" else TILES_B) - 1)
    for w in range(BATCH):
        sp.dma_start(out[:, w, :], slab[bass.ds(tiles[w], 1)].rearrange("w p d -> p (w d)")).then_inc(sem, 16)


def row(ap):
    return ap.rearrange("(o n) -> o n", o=1).to_broadcast([P, ap.shape[0]])


def attention_nodes(nc, t, layer, Wl, bl, Wr, br, att, Wres, bias):
    with nc.cleanup_on_exit(), ExitStack() as ctx:
        def sem(name):
            return nc.alloc_semaphore(f"an{layer}" + "_" + name)

        def sb(name, shape, dt=F32):
            return ctx.enter_context(nc.sbuf_tensor(f"an{layer}_" + name, shape, dt))

        W = sb("W", [P, 3, P])
        WT = sb("WT", [P, 3, P])
        biases = sb("biases", [P, 3, P])
        att_row = sb("att_row", [P, P])
        H = sb("H", [P, 2, BATCH, D])
        acc = sb("acc", [P, 2, BATCH, D + 1])
        res = sb("res", [P, 2, BATCH, D])
        rec = sb("rec", [P, BATCH])
        HT = sb("HT", [P, BATCH, P])
        O = sb("O", [P, 2, BATCH, 3 * (D + 1)])
        junk = sb("junk", [P, 2 * BATCH, P])
        turned = ctx.enter_context(nc.psum_tensor(f"an{layer}_turned", [P, 2, 512], F32))
        prod = ctx.enter_context(nc.psum_tensor(f"an{layer}_prod", [P, 4, 512], F32))

        s_w = sem("s_w")
        s_wturn = sem("s_wturn")
        s_wt = sem("s_wt")
        s_in = [sem(f"s_in{p}") for p in range(2)]
        s_dve = sem("s_dve")
        s_h = sem("s_h")
        s_turn = sem("s_turn")
        s_ht = sem("s_ht")
        s_prod = sem("s_prod")
        s_o = sem("s_o")
        s_ready = sem("s_ready")
        s_out = [sem(f"s_out{p}") for p in range(2)]
        loads = 1 if layer == 0 else BATCH + 1

        with nc.Block() as block:
            @block.sync
            def _(sp):
                for i, m in enumerate((Wl, Wr, Wres)):
                    sp.dma_start(W[:, i, :], m).then_inc(s_w, 16)
                for i, v in enumerate((bl, br, bias)):
                    sp.dma_start(biases[:, i, :], row(v)).then_inc(s_w, 16)
                sp.dma_start(att_row[:, :], row(att)).then_inc(s_w, 16)

                def load(b):
                    p = b % 2
                    wait(sp, s_turn, b - 1)
                    if layer == 0:
                        sp.dma_start(H[:, p, :, :], node_batch(t.x_pad, b)).then_inc(s_in[p], 16)
                    else:
                        load_last(nc, sp, t, "A", b, t.slab_att[0], acc[:, p], s_in[p])
                        sp.dma_start(res[:, p, :, :], node_batch(t.res[0], b)).then_inc(s_in[p], 16)

                load(0)
                for b in range(NBATCH):
                    if b + 1 < NBATCH:
                        load(b + 1)
                    p = b % 2
                    sp.wait_ge(s_ready, b + 1)
                    for k, table in enumerate((t.xl[layer], t.xr[layer])):
                        sp.dma_start(node_batch(table, b), O[:, p, :, k * (D + 1):(k + 1) * (D + 1)]).then_inc(s_out[p], 16)
                    sp.dma_start(node_batch(t.res[layer], b), O[:, p, :, 2 * (D + 1) + 1:]).then_inc(s_out[p], 16)
                for p in range(2):
                    sp.wait_ge(s_out[p], 48 * ((NBATCH + 1 - p) // 2))

            @block.vector
            def _(dve):
                step = Chain(dve, s_dve)
                dve.wait_ge(s_wturn, 1)
                dve.tensor_copy(WT[:, :, :].rearrange("k m n -> k (m n)"), prod[:, 0, 0:3 * P]).then_inc(s_wt, 1)
                dve.wait_ge(s_w, 16 * 7)
                for b in range(NBATCH):
                    p = b % 2
                    if layer > 0:
                        dve.wait_ge(s_in[p], 16 * loads * (b // 2 + 1))
                        step(dve.reciprocal(rec[:, :], acc[:, p, :, D]))
                        step(dve.tensor_tensor(H[:, p], acc[:, p, :, 0:D], bcast_last(rec[:, :], D), ALU.mult))
                        step(dve.tensor_tensor(H[:, p], H[:, p], res[:, p], ALU.add))
                        dve.tensor_scalar(H[:, p], H[:, p], 0.0, None, ALU.max).then_inc(s_h, 1)
                    wait(dve, s_out[p], 48 * (b // 2))
                    for w in range(BATCH):
                        n = b * BATCH + w
                        dve.wait_ge(s_prod, n + 1)
                        dve.tensor_tensor(O[:, p, w, :].rearrange("p (k c) -> p k c", k=3)[:, :, 1:],
                                          prod[:, n % 4, 0:3 * P].rearrange("p (k c) -> p k c", k=3),
                                          biases[:, :, :], ALU.add).then_inc(s_o, 1)
                    dve.wait_ge(s_o, (b + 1) * BATCH)
                    for w in range(BATCH):
                        for k in range(2):
                            c = k * (D + 1)
                            last = dve.tensor_tensor_reduce(junk[:, 2 * w + k, :], O[:, p, w, c + 1:c + 1 + D], att_row[:, :], 0.2, 0.0,
                                                            ALU.mult, ALU.add, O[:, p, w, c:c + 1])
                    last.then_inc(s_ready, 1)
                    dve.wait_ge(s_ready, b + 1)

            @block.scalar
            def _(act):
                for b in range(NBATCH):
                    act.wait_ge(s_turn, b + 1)
                    wait(act, s_prod, b * BATCH)
                    act.activation(HT[:, 0:4, :], turned[:, 0, :].rearrange("p (w n) -> p w n", w=4), ACT.Copy)
                    act.activation(HT[:, 4:7, :], turned[:, 1, 0:3 * P].rearrange("p (w n) -> p w n", w=3), ACT.Copy).then_inc(s_ht, 1)

            @block.tensor
            def _(pe):
                pe.wait_ge(s_w, 16 * 7)
                for i in range(3):
                    last = pe.transpose(prod[:, 0, i * P:(i + 1) * P], W[:, i, :], t.ident[:, :])
                last.then_inc(s_wturn, 1)
                pe.wait_ge(s_wt, 1)
                for b in range(NBATCH):
                    p = b % 2
                    if layer == 0:
                        pe.wait_ge(s_in[p], 16 * (b // 2 + 1))
                    else:
                        pe.wait_ge(s_h, b + 1)
                    wait(pe, s_ht, b)
                    for w in range(BATCH):
                        last = pe.transpose(turned[:, w // 4, (w % 4) * P:(w % 4 + 1) * P], H[:, p, w, :], t.ident[:, :])
                    last.then_inc(s_turn, 1)
                    pe.wait_ge(s_ht, b + 1)
                    for w in range(BATCH):
                        n = b * BATCH + w
                        wait(pe, s_o, n - 3)
                        pe.matmul(prod[:, n % 4, 0:3 * P], HT[:, w, :], WT[:, :, :].rearrange("k m n -> k (m n)"),
                                  start=True, stop=True).then_inc(s_prod, 1)


def attention_sweep(nc, t, layer, att):
    groups = TILES_A // GROUP
    C = D + 1
    with nc.cleanup_on_exit(), ExitStack() as ctx:
        def sem(name):
            return nc.alloc_semaphore(f"as{layer}" + "_" + name)

        def sb(name, shape, dt=F32):
            return ctx.enter_context(nc.sbuf_tensor(f"as{layer}_" + name, shape, dt))

        def ps(name, shape):
            return ctx.enter_context(nc.psum_tensor(f"as{layer}_" + name, shape, F32))

        slots = sb("slots", [P, UNROLL, GROUP], I32)
        rows = sb("rows", [P, UNROLL, GROUP, C + 1])
        xr = sb("xr", [P, 4, GROUP, C])
        dst_row = sb("dst_row", [P, 4, GROUP * P])
        hot_t = sb("hot_t", [P, 4, GROUP, P])
        outside = sb("outside", [P, 2, GROUP, P])
        relu = sb("relu", [P, 2, GROUP, P])
        att_row = sb("att_row", [P, P])
        part = sb("part", [P, 2, GROUP])
        score = sb("score", [P, 4, GROUP])
        tile_max = sb("tile_max", [P, 2, GROUP])
        run_max = sb("run_max", [P, TILES_A + 1])
        args = sb("args", [P, 2, 2 * GROUP])
        exps = sb("exps", [P, 2, 2 * GROUP])
        weight = sb("weight", [P, 2, GROUP, P])
        acc = sb("acc", [P, 4, GROUP, C])
        z = ps("z", [P, 2, 2, 512])
        score_row = ps("score_row", [P, GROUP, P])
        edge_max = ps("edge_max", [P, 512])
        total = ps("total", [P, 2, 512])

        s_att = sem("s_att")
        s_init = sem("s_init")
        s_tick = sem("s_tick")
        s_index = sem("s_index")
        s_pace = sem("s_pace")
        s_gathered = [sem(f"s_gathered{q}") for q in range(UNROLL)]
        s_window = [sem(f"s_window{q}") for q in range(4)]
        s_hot = sem("s_hot")
        s_z = sem("s_z")
        s_relu = sem("s_relu")
        s_outside = sem("s_outside")
        s_part = sem("s_part")
        s_score = sem("s_score")
        s_row = sem("s_row")
        s_tmax = sem("s_tmax")
        s_max = sem("s_max")
        s_emax = sem("s_emax")
        s_sub = sem("s_sub")
        s_args = sem("s_args")
        s_exps = sem("s_exps")
        s_weight = sem("s_weight")
        s_total = sem("s_total")
        s_acc = sem("s_acc")
        s_stored = [sem(f"s_stored{q}") for q in range(4)]

        def pair(ap, h):
            return ap[:, h, 0:2 * C]

        with nc.Block() as block:
            @block.gpsimd
            def _(pool):
                gather_rows(pool, t, "A", groups, t.xl[layer], C, slots, rows, s_total, 1, s_index, s_gathered, s_tick)

            @block.sync
            def _(sp):
                sp.dma_start(att_row[:, :], row(att)).then_inc(s_att, 16)

                def stage(g, q, r):
                    wait(sp, s_z, g - 3)
                    wait(sp, s_hot, g - 3)
                    load_windows(nc, sp, t, "A", g, t.xr[layer], xr[:, q % 4], s_window[q % 4])
                    sp.dma_start(dst_row[:, q % 4, :], t.dst_rows["A"].rearrange("(g j) e -> g (j e)", j=GROUP)[bass.ds(g, 1)]
                                 .to_broadcast([P, GROUP * P])).then_inc(s_window[q % 4], 16)
                run_groups(sp, groups, [(0, stage)])
                for q in range(4):
                    sp.wait_ge(s_stored[q], 16 * groups // 4)

            @block.scalar
            def _(act):
                def store(g, q, r):
                    wait(act, s_acc, GROUP * (g + 1))
                    act.dma_start(t.slab_att[layer][bass.ds(g * GROUP, GROUP)].rearrange("j p c -> p j c"), acc[:, q % 4]).then_inc(s_stored[q % 4], 16)

                def relu_z(g, q, r):
                    wait(act, s_z, g + 1)
                    wait(act, s_score, g - 1)
                    act.activation(relu[:, q % 2].rearrange("p (h j) d -> p h j d", h=2),
                                   z[:, q % 2, :, 0:2 * C].rearrange("p h (j c) -> p h j c", c=C)[:, :, :, 1:], ACT.Relu).then_inc(s_relu, 1)

                def outside_t(g, q, r):
                    wait(act, s_hot, g + 1)
                    wait(act, s_max, g - 1)
                    act.activation(outside[:, q % 2], hot_t[:, q % 4], ACT.Copy, scale=BIG, bias=-BIG).then_inc(s_outside, 1)

                def exps_g(g, q, r):
                    wait(act, s_args, g + 1)
                    wait(act, s_acc, GROUP * (g - 1))
                    act.activation(exps[:, q % 2, :], args[:, q % 2, :], ACT.Exp).then_inc(s_exps, 1)
                run_groups(act, groups, [(4, store), (0, relu_z), (0, outside_t), (2, exps_g)])

            @block.tensor
            def _(pe):
                pe.wait_ge(s_init, 1)

                def edge_max_g(g, q, r):
                    wait(pe, s_max, g + 1)
                    wait(pe, s_sub, g - 1)
                    for j in range(GROUP):
                        o = (q % 2) * GROUP + j
                        last = pe.matmul(edge_max[:, o:o + 1], hot_t[:, q % 4, j, :], run_max[:, bass.ds(g * GROUP + (j + 1), 1)],
                                         start=True, stop=True)
                    last.then_inc(s_emax, 1)

                def z_g(g, q, r):
                    wait(pe, s_gathered[q], 16 * GROUP * (r + 1))
                    wait(pe, s_window[q % 4], 16 * (GROUP + 1) * (uses(q, r, 4) + 1))
                    wait(pe, s_hot, g + 1)
                    wait(pe, s_relu, g - 1)
                    wait(pe, s_score, g - 1)
                    for h in range(2):
                        pe.matmul(pair(z[:, q % 2], h), t.ident[:, :], rows[:, q, 2 * h:2 * h + 2, 0:C], start=True, stop=False,
                                  skip_group_check=True)
                        for j in (2 * h, 2 * h + 1):
                            c = (j % 2) * C
                            last = pe.matmul(z[:, q % 2, h, c:c + C], hot_t[:, q % 4, j, :], xr[:, q % 4, j, :], start=False, stop=True,
                                             skip_group_check=True)
                    last.then_inc(s_z, 1)

                def total_g(g, q, r):
                    wait(pe, s_weight, g + 1)
                    wait(pe, s_acc, GROUP * g)
                    for j in range(GROUP):
                        last = pe.matmul(total[:, j // 2, (j % 2) * C:(j % 2 + 1) * C], weight[:, q % 2, j, :], rows[:, q, j, 1:C + 1],
                                         start=True, stop=True)
                    last.then_inc(s_total, 1)

                def score_row_g(g, q, r):
                    wait(pe, s_score, g + 1)
                    wait(pe, s_max, g)
                    for j in range(GROUP):
                        last = pe.matmul(score_row[:, j, :], score[:, q % 4, j:j + 1].to_broadcast([P, P]), t.ident[:, :],
                                         start=True, stop=True)
                    last.then_inc(s_row, 1)
                run_groups(pe, groups, [(2, edge_max_g), (0, z_g), (3, total_g), (1, score_row_g)])

            @block.vector
            def _(dve):
                dve.memset(rows[:, :, :, C:C + 1], 1.0)
                dve.memset(run_max[:, 0:1], -BIG)
                dve.memset(acc[:, 3, GROUP - 1, :], 0.0).then_inc(s_init, 1)
                dve.wait_ge(s_init, 1)
                dve.wait_ge(s_att, 16)
                dve.tensor_scalar(att_row[:, :], att_row[:, :], 0.8, None, ALU.mult).then_inc(s_init, 1)
                dve.wait_ge(s_init, 2)

                def max_g(g, q, r):
                    wait(dve, s_row, g + 1)
                    wait(dve, s_outside, g + 1)
                    dve.sem_inc(s_pace, 1)
                    for j in range(GROUP):
                        last = dve.tensor_tensor_reduce(outside[:, q % 2, j, :], score_row[:, j, :], outside[:, q % 2, j, :], 1.0, -BIG,
                                                        ALU.add, ALU.max, tile_max[:, q % 2, j:j + 1])
                    last.then_inc(s_tmax, 1)
                    wait(dve, s_tmax, g + 1)
                    dve.tensor_tensor_scan(run_max[:, bass.ds(g * GROUP + 1, GROUP)], t.newwin[:, bass.ds(g * GROUP, GROUP)],
                                           tile_max[:, q % 2, :], run_max[:, bass.ds(g * GROUP, 1)], ALU.add, ALU.max).then_inc(s_max, 1)

                def hot_g(g, q, r):
                    wait(dve, s_window[q % 4], 16 * (GROUP + 1) * (uses(q, r, 4) + 1))
                    wait(dve, s_emax, g - 3)
                    dve.tensor_scalar(hot_t[:, q % 4].rearrange("p j e -> p (j e)"), dst_row[:, q % 4, :], t.iota_p[:, :], None,
                                      ALU.is_equal).then_inc(s_hot, 1)

                def weight_g(g, q, r):
                    wait(dve, s_exps, g + 1)
                    wait(dve, s_total, g - 1)
                    for j in range(GROUP):
                        last = dve.tensor_scalar(weight[:, q % 2, j, :], t.iota_f[:, :], t.dstrel["A"][:, bass.ds(g * GROUP + j, 1)],
                                                 exps[:, q % 2, j:j + 1], ALU.is_equal, ALU.mult)
                    last.then_inc(s_weight, 1)

                def score_g(g, q, r):
                    wait(dve, s_relu, g + 1)
                    for j in range(GROUP):
                        last = dve.tensor_tensor_reduce(relu[:, q % 2, j, :], relu[:, q % 2, j, :], att_row[:, :], 1.0, 0.0,
                                                        ALU.mult, ALU.add, part[:, q % 2, j:j + 1])
                    last.then_inc(s_part, 1)
                    wait(dve, s_part, g + 1)
                    wait(dve, s_row, g - 3)
                    dve.tensor_tensor(score[:, q % 4, :].rearrange("p (h j) -> p h j", h=2), part[:, q % 2, :].rearrange("p (h j) -> p h j", h=2),
                                      z[:, q % 2, :, 0:2 * C].rearrange("p h (j c) -> p h j c", c=C)[:, :, :, 0],
                                      ALU.add).then_inc(s_score, 1)

                def args_g(g, q, r):
                    wait(dve, s_exps, g - 1)
                    wait(dve, s_max, g + 1)
                    dve.tensor_tensor(args[:, q % 2, GROUP:], run_max[:, bass.ds(g * GROUP, GROUP)], t.newwin[:, bass.ds(g * GROUP, GROUP)],
                                      ALU.add)
                    wait(dve, s_emax, g + 1)
                    dve.tensor_tensor(args[:, q % 2, 0:GROUP], score[:, q % 4, :], edge_max[:, (q % 2) * GROUP:(q % 2 + 1) * GROUP],
                                      ALU.subtract).then_inc(s_sub, 1)
                    wait(dve, s_sub, g + 1)
                    dve.tensor_scalar(args[:, q % 2, 0:GROUP], args[:, q % 2, 0:GROUP], 0.0, None, ALU.min)
                    dve.tensor_tensor(args[:, q % 2, GROUP:], args[:, q % 2, GROUP:], run_max[:, bass.ds(g * GROUP + 1, GROUP)],
                                      ALU.subtract).then_inc(s_args, 1)

                def acc_g(g, q, r):
                    wait(dve, s_total, g + 1)
                    wait(dve, s_stored[q % 4], 16 * uses(q, r, 4))
                    for j in range(GROUP):
                        before = acc[:, q % 4, j - 1, :] if j else acc[:, (q - 1) % 4, GROUP - 1, :]
                        wait(dve, s_acc, g * GROUP + j)
                        dve.scalar_tensor_tensor(out=acc[:, q % 4, j, :], in0=before, scalar=exps[:, q % 2, GROUP + j:GROUP + j + 1],
                                                 in1=total[:, j // 2, (j % 2) * C:(j % 2 + 1) * C], op0=ALU.mult, op1=ALU.add).then_inc(s_acc, 1)
                run_groups(dve, groups, [(2, max_g), (0, hot_g), (3, weight_g), (1, score_g), (2, args_g), (3, acc_g)])


def normalise(dve, step, y, stats, square, s_var, s_sd, n):
    mean, var, dev, inv, tmp = (stats[:, i, :] for i in range(5))
    step(dve.tensor_reduce(mean, y, AX.X, ALU.add))
    step(dve.tensor_scalar(mean, mean, 1.0 / D, None, ALU.mult))
    step(dve.tensor_tensor(y, y, bcast_last(mean, D), ALU.subtract))
    step(dve.tensor_tensor(square, y, y, ALU.mult))
    step(dve.tensor_reduce(var, square, AX.X, ALU.add))
    dve.tensor_scalar(var, var, 1.0 / D, EPS, ALU.mult, ALU.add).then_inc(s_var, 1)
    dve.wait_ge(s_sd, n)
    inverse_root(dve, step, var, dev, inv, tmp)
    step(dve.tensor_tensor(y, y, bcast_last(inv, D), ALU.mult))


def inverse_root(dve, step, value, root, inv, tmp):
    step(dve.reciprocal(inv, root))
    step(dve.tensor_tensor(tmp, inv, inv, ALU.mult))
    step(dve.tensor_tensor(tmp, tmp, value, ALU.mult))
    step(dve.tensor_scalar(tmp, tmp, -0.5, 1.5, ALU.mult, ALU.add))
    step(dve.tensor_tensor(inv, inv, tmp, ALU.mult))


def turn_batch(pe, t, bank, source):
    for w in range(BATCH):
        last = pe.transpose(bank[:, w // 4, (w % 4) * P:(w % 4 + 1) * P], source[:, w, :], t.ident[:, :])
    return last


def copy_batch(act, out, bank):
    act.activation(out[:, 0:4, :], bank[:, 0, :].rearrange("p (w n) -> p w n", w=4), ACT.Copy)
    return act.activation(out[:, 4:7, :], bank[:, 1, 0:3 * P].rearrange("p (w n) -> p w n", w=3), ACT.Copy)


def max_nodes(nc, t, W1, b1):
    with nc.cleanup_on_exit(), ExitStack() as ctx:
        def sem(name):
            return nc.alloc_semaphore("mn_" + name)

        def sb(name, shape, dt=F32):
            return ctx.enter_context(nc.sbuf_tensor("mn_" + name, shape, dt))

        W = sb("W", [P, 2, P])
        bias = sb("bias", [P, P])
        acc = sb("acc", [P, 2, BATCH, D + 1])
        res = sb("res", [P, 2, BATCH, D])
        x = sb("x", [P, 2, BATCH, D])
        y = sb("y", [P, 2, BATCH, D])
        square = sb("square", [P, BATCH, D])
        rec = sb("rec", [P, BATCH])
        stats = sb("stats", [P, 5, BATCH])
        yT = sb("yT", [P, BATCH, P])
        O = sb("O", [P, 2, BATCH, 2 * D])
        turned = ctx.enter_context(nc.psum_tensor("mn_turned", [P, 2, 512], F32))
        prod = ctx.enter_context(nc.psum_tensor("mn_prod", [P, 4, 512], F32))
        s_w = sem("s_w")
        s_in = [sem(f"s_in{p}") for p in range(2)]
        s_dve = sem("s_dve")
        s_used = sem("s_used")
        s_var = sem("s_var")
        s_sd = sem("s_sd")
        s_y = sem("s_y")
        s_turn = sem("s_turn")
        s_yt = sem("s_yt")
        s_prod = sem("s_prod")
        s_o = sem("s_o")
        s_out = [sem(f"s_out{p}") for p in range(2)]
        s_xout = [sem(f"s_xout{p}") for p in range(2)]

        with nc.Block() as block:
            @block.sync
            def _(sp):
                sp.dma_start(W[:, :, :], W1[0:2 * D, :].rearrange("(k p) n -> p k n", p=P)).then_inc(s_w, 16)
                sp.dma_start(bias[:, :], row(b1)).then_inc(s_w, 16)

                def load(b):
                    p = b % 2
                    wait(sp, s_used, b - 1)
                    load_last(nc, sp, t, "A", b, t.slab_att[1], acc[:, p], s_in[p])
                    sp.dma_start(res[:, p], node_batch(t.res[1], b)).then_inc(s_in[p], 16)
                    sp.dma_start(x[:, p], node_batch(t.x_pad, b)).then_inc(s_in[p], 16)

                load(0)
                for b in range(NBATCH):
                    if b + 1 < NBATCH:
                        load(b + 1)
                    p = b % 2
                    sp.wait_ge(s_y, b + 1)
                    sp.dma_start(node_batch(t.x1, b), y[:, p]).then_inc(s_xout[p], 16)
                    sp.wait_ge(s_o, (b + 1) * BATCH)
                    sp.dma_start(node_batch(t.ha, b), O[:, p, :, 0:D]).then_inc(s_out[p], 16)
                    sp.dma_start(node_batch(t.hb, b), O[:, p, :, D:]).then_inc(s_out[p], 16)
                for p in range(2):
                    n = (NBATCH + 1 - p) // 2
                    sp.wait_ge(s_out[p], 32 * n)
                    sp.wait_ge(s_xout[p], 16 * n)

            @block.vector
            def _(dve):
                step = Chain(dve, s_dve)
                dve.wait_ge(s_w, 32)
                for b in range(NBATCH):
                    p = b % 2
                    dve.wait_ge(s_in[p], 16 * (BATCH + 2) * (b // 2 + 1))
                    step(dve.reciprocal(rec[:, :], acc[:, p, :, D]))
                    wait(dve, s_xout[p], 16 * (b // 2))
                    wait(dve, s_turn, b - 1)
                    step(dve.tensor_tensor(y[:, p], acc[:, p, :, 0:D], bcast_last(rec[:, :], D), ALU.mult))
                    step(dve.tensor_tensor(y[:, p], y[:, p], res[:, p], ALU.add))
                    dve.tensor_tensor(y[:, p], y[:, p], x[:, p], ALU.add).then_inc(s_used, 1)
                    dve.wait_ge(s_used, b + 1)
                    normalise(dve, step, y[:, p], stats, square[:, :, :], s_var, s_sd, b + 1)
                    dve.engine_nop().then_inc(s_y, 1)
                    wait(dve, s_out[p], 32 * (b // 2))
                    for w in range(BATCH):
                        n = b * BATCH + w
                        dve.wait_ge(s_prod, n + 1)
                        dve.tensor_copy(O[:, p, w, 0:D], prod[:, n % 4, 0:D])
                        dve.tensor_tensor(O[:, p, w, D:], prod[:, n % 4, D:2 * D], bias[:, :], ALU.add).then_inc(s_o, 1)

            @block.scalar
            def _(act):
                for b in range(NBATCH):
                    act.wait_ge(s_var, b + 1)
                    act.activation(stats[:, 2, :], stats[:, 1, :], ACT.Sqrt).then_inc(s_sd, 1)
                    act.wait_ge(s_turn, b + 1)
                    wait(act, s_prod, b * BATCH)
                    copy_batch(act, yT, turned).then_inc(s_yt, 1)

            @block.tensor
            def _(pe):
                pe.wait_ge(s_w, 32)
                for b in range(NBATCH):
                    pe.wait_ge(s_y, b + 1)
                    wait(pe, s_yt, b)
                    turn_batch(pe, t, turned, y[:, b % 2]).then_inc(s_turn, 1)
                    pe.wait_ge(s_yt, b + 1)
                    for w in range(BATCH):
                        n = b * BATCH + w
                        wait(pe, s_o, n - 3)
                        pe.matmul(prod[:, n % 4, 0:2 * D], yT[:, w, :], W[:, :, :].rearrange("p k n -> p (k n)"),
                                  start=True, stop=True).then_inc(s_prod, 1)


def max_sweep(nc, t, W1, W2):
    groups = TILES_B // GROUP
    E = GROUP * P
    with nc.cleanup_on_exit(), ExitStack() as ctx:
        def sem(name):
            return nc.alloc_semaphore("ms_" + name)

        def sb(name, shape, dt=F32):
            return ctx.enter_context(nc.sbuf_tensor("ms_" + name, shape, dt))

        def ps(name, shape):
            return ctx.enter_context(nc.psum_tensor("ms_" + name, shape, F32))

        slots = sb("slots", [P, UNROLL, GROUP], I32)
        rows = sb("rows", [P, UNROLL, GROUP, D])
        hb = sb("hb", [P, 4, GROUP, D])
        dst_row = sb("dst_row", [P, 4, E])
        seg_row = sb("seg_row", [P, 4, E])
        ew_row = sb("ew_row", [1, 4, E])
        W1c = sb("W1c", [1, D])
        W2_sb = sb("W2", [P, D])
        hot_t = sb("hot_t", [P, 2, GROUP, P])
        hidden_sb = sb("hidden", [P, 2, E])
        running = sb("running", [P, 2, E])
        edge_major = sb("edge_major", [P, 2, GROUP, P])
        pick = sb("pick", [P, 2, GROUP, P])
        degree = sb("degree", [P, 2, GROUP])
        acc = sb("acc", [P, 4, GROUP, D + 1])
        hidden = ps("hidden_ps", [P, 2, E])
        message = ps("message", [P, 2, E])
        turned = ps("turned", [P, 2, E])
        total = ps("total", [P, 2, GROUP, P])

        s_w = sem("s_w")
        s_init = sem("s_init")
        s_tick = sem("s_tick")
        s_index = sem("s_index")
        s_gathered = [sem(f"s_gathered{q}") for q in range(UNROLL)]
        s_window = [sem(f"s_window{q}") for q in range(4)]
        s_hot = sem("s_hot")
        s_degree = sem("s_degree")
        s_hidden = sem("s_hidden")
        s_relu = sem("s_relu")
        s_message = sem("s_message")
        s_running = sem("s_running")
        s_turned = sem("s_turned")
        s_edge = sem("s_edge")
        s_pick = sem("s_pick")
        s_total = sem("s_total")
        s_acc = sem("s_acc")
        s_summed = sem("s_summed")
        s_stored = [sem(f"s_stored{q}") for q in range(4)]
        LOADS = GROUP + 3

        with nc.Block() as block:
            @block.gpsimd
            def _(pool):
                gather_rows(pool, t, "B", groups, t.ha, D, slots, rows, s_hidden, 1, s_index, s_gathered, s_tick)

            @block.sync
            def _(sp):
                sp.dma_start(W1c[:, :], W1[2 * D:2 * D + 1, :]).then_inc(s_w, 16)
                sp.dma_start(W2_sb[:, :], W2).then_inc(s_w, 16)

                def stage(g, q, r):
                    k = q % 4
                    wait(sp, s_hidden, g - 3)
                    wait(sp, s_hot, g - 3)
                    wait(sp, s_running, g - 3)
                    load_windows(nc, sp, t, "B", g, t.hb, hb[:, k], s_window[k])
                    for out, table in ((dst_row, t.dst_rows["B"]), (seg_row, t.seg_rows)):
                        sp.dma_start(out[:, k, :], table.rearrange("(g j) e -> g (j e)", j=GROUP)[bass.ds(g, 1)]
                                     .to_broadcast([P, E])).then_inc(s_window[k], 16)
                    sp.dma_start(ew_row[:, k, :], t.ew_rows.rearrange("(g j) e -> g (j e)", j=GROUP)[bass.ds(g, 1)]).then_inc(s_window[k], 16)
                run_groups(sp, groups, [(0, stage)])
                for q in range(4):
                    sp.wait_ge(s_stored[q], 16 * groups // 4)

            @block.scalar
            def _(act):
                def store(g, q, r):
                    wait(act, s_acc, GROUP * (g + 1))
                    wait(act, s_summed, g + 1)
                    act.dma_start(t.slab_max[bass.ds(g * GROUP, GROUP)].rearrange("j p c -> p j c"), acc[:, q % 4]).then_inc(s_stored[q % 4], 16)

                def relu_g(g, q, r):
                    wait(act, s_hidden, g + 1)
                    wait(act, s_message, g - 1)
                    act.activation(hidden_sb[:, q % 2, :], hidden[:, q % 2, :], ACT.Relu).then_inc(s_relu, 1)

                def edge_g(g, q, r):
                    wait(act, s_turned, g + 1)
                    wait(act, s_total, g - 1)
                    act.activation(edge_major[:, q % 2].rearrange("p j e -> p (j e)"), turned[:, q % 2, :], ACT.Copy).then_inc(s_edge, 1)
                run_groups(act, groups, [(4, store), (0, relu_g), (2, edge_g)])

            @block.tensor
            def _(pe):
                pe.wait_ge(s_w, 32)

                def message_g(g, q, r):
                    wait(pe, s_relu, g + 1)
                    wait(pe, s_running, g - 1)
                    pe.matmul(message[:, q % 2, :], W2_sb[:, :], hidden_sb[:, q % 2, :], start=True, stop=True).then_inc(s_message, 1)

                def hidden_g(g, q, r):
                    wait(pe, s_gathered[q], 16 * GROUP * (r + 1))
                    wait(pe, s_window[q % 4], 16 * LOADS * (uses(q, r, 4) + 1))
                    wait(pe, s_hot, g + 1)
                    wait(pe, s_relu, g - 1)
                    pe.matmul(hidden[:, q % 2, :], W1c[:, :], ew_row[:, q % 4, :], start=True, stop=False, skip_group_check=True)
                    for j in range(GROUP):
                        out = hidden[:, q % 2, j * P:(j + 1) * P]
                        pe.matmul(out, rows[:, q, j, :], t.ident[:, :], start=False, stop=False, skip_group_check=True)
                        last = pe.matmul(out, hb[:, q % 4, j, :], hot_t[:, q % 2, j, :], start=False, stop=True, skip_group_check=True)
                    last.then_inc(s_hidden, 1)

                def turn_g(g, q, r):
                    wait(pe, s_running, g + 1)
                    wait(pe, s_edge, g - 1)
                    for j in range(GROUP):
                        last = pe.transpose(turned[:, q % 2, j * P:(j + 1) * P], running[:, q % 2, j * P:(j + 1) * P], t.ident[:, :])
                    last.then_inc(s_turned, 1)

                def total_g(g, q, r):
                    wait(pe, s_pick, g + 1)
                    wait(pe, s_edge, g + 1)
                    wait(pe, s_acc, GROUP * (g - 1))
                    for j in range(GROUP):
                        last = pe.matmul(total[:, q % 2, j, :], pick[:, q % 2, j, :], edge_major[:, q % 2, j, :], start=True, stop=True)
                    last.then_inc(s_total, 1)
                run_groups(pe, groups, [(1, message_g), (0, hidden_g), (2, turn_g), (3, total_g)])

            @block.vector
            def _(dve):
                dve.memset(running[:, 1, E - 1:E], 0.0)
                dve.memset(acc[:, 3, GROUP - 1, :], 0.0).then_inc(s_init, 1)
                dve.wait_ge(s_init, 1)

                def hot_g(g, q, r):
                    wait(dve, s_window[q % 4], 16 * LOADS * (uses(q, r, 4) + 1))
                    wait(dve, s_hidden, g - 1)
                    dve.tensor_scalar(hot_t[:, q % 2].rearrange("p j e -> p (j e)"), dst_row[:, q % 4, :], t.iota_p[:, :], None,
                                      ALU.is_equal).then_inc(s_hot, 1)
                    wait(dve, s_hot, g + 1)
                    dve.tensor_reduce(degree[:, q % 2, :], hot_t[:, q % 2], AX.X, ALU.add).then_inc(s_degree, 1)

                def running_g(g, q, r):
                    wait(dve, s_message, g + 1)
                    wait(dve, s_turned, g - 1)
                    wait(dve, s_running, g)
                    dve.tensor_tensor_scan(running[:, q % 2, :], seg_row[:, q % 4, :], message[:, q % 2, :],
                                           running[:, (q - 1) % 2, E - 1:E], ALU.add, ALU.max).then_inc(s_running, 1)

                def pick_g(g, q, r):
                    wait(dve, s_total, g - 1)
                    for j in range(GROUP):
                        last = dve.tensor_scalar(pick[:, q % 2, j, :], t.iota_f[:, :], t.lastrel[:, bass.ds(g * GROUP + j, 1)],
                                                 None, ALU.is_equal)
                    last.then_inc(s_pick, 1)

                def degree_g(g, q, r):
                    wait(dve, s_stored[q % 4], 16 * uses(q, r, 4))
                    wait(dve, s_degree, g + 1)
                    wait(dve, s_summed, g)
                    dve.tensor_tensor_scan(acc[:, q % 4, :, D], t.same["B"][:, bass.ds(g * GROUP, GROUP)], degree[:, q % 2, :],
                                           acc[:, (q - 1) % 4, GROUP - 1, D:], ALU.mult, ALU.add).then_inc(s_summed, 1)

                def acc_g(g, q, r):
                    wait(dve, s_total, g + 1)
                    wait(dve, s_stored[q % 4], 16 * uses(q, r, 4))
                    for j in range(GROUP):
                        before = acc[:, q % 4, j - 1, 0:D] if j else acc[:, (q - 1) % 4, GROUP - 1, 0:D]
                        wait(dve, s_acc, g * GROUP + j)
                        dve.scalar_tensor_tensor(out=acc[:, q % 4, j, 0:D], in0=before, scalar=t.same["B"][:, bass.ds(g * GROUP + j, 1)],
                                                 in1=total[:, q % 2, j, :], op0=ALU.mult, op1=ALU.add).then_inc(s_acc, 1)
                run_groups(dve, groups, [(0, hot_g), (1, running_g), (1, degree_g), (2, pick_g), (3, acc_g)])


def update_nodes(nc, t, b2, U1, c1, U2, c2, W1_s, W1_v, Ws_s, Ws_v):
    inv = 1.0 / 32 ** 0.5
    with nc.cleanup_on_exit(), ExitStack() as ctx:
        def sem(name):
            return nc.alloc_semaphore("un_" + name)

        def sb(name, shape, dt=F32):
            return ctx.enter_context(nc.sbuf_tensor("un_" + name, shape, dt))

        U1_sb = sb("U1", [P, 2, D])
        U2_sb = sb("U2", [P, D])
        c1_col = sb("c1_col", [P, 1])
        c2_row = sb("c2_row", [P, D])
        b2_row = sb("b2_row", [P, D])
        WP = sb("WP", [P, 2, D])
        acc = sb("acc", [P, 2, BATCH, D + 1])
        x1 = sb("x1", [P, 2, BATCH, D])
        agg = sb("agg", [P, BATCH, D])
        deg = sb("deg", [P, 4, BATCH])
        has = sb("has", [P, BATCH])
        inT = sb("inT", [P, 2, BATCH, P])
        hidT = sb("hidT", [P, BATCH, P])
        y = sb("y", [P, 2, BATCH, D])
        square = sb("square", [P, BATCH, D])
        stats = sb("stats", [P, 5, BATCH])
        yT = sb("yT", [P, BATCH, P])
        O = sb("O", [P, 2, BATCH, 2 * D])
        left = ctx.enter_context(nc.psum_tensor("un_left", [P, 4, 512], F32))
        right = ctx.enter_context(nc.psum_tensor("un_right", [P, 4, 512], F32))
        s_zero = sem("s_zero")
        s_w = sem("s_w")
        s_scaled = sem("s_scaled")
        s_in = [sem(f"s_in{p}") for p in range(2)]
        s_dve = sem("s_dve")
        s_deg = sem("s_deg")
        s_root = sem("s_root")
        s_agg = sem("s_agg")
        s_turn = sem("s_turn")
        s_int = sem("s_int")
        s_hid = sem("s_hid")
        s_hidt = sem("s_hidt")
        s_upd = sem("s_upd")
        s_used = sem("s_used")
        s_var = sem("s_var")
        s_sd = sem("s_sd")
        s_y = sem("s_y")
        s_turn2 = sem("s_turn2")
        s_yt = sem("s_yt")
        s_prod = sem("s_prod")
        s_o = sem("s_o")
        s_out = [sem(f"s_out{p}") for p in range(2)]
        s_xout = [sem(f"s_xout{p}") for p in range(2)]
        WLOADS = 5 + 8

        with nc.Block() as block:
            @block.gpsimd
            def _(pool):
                pool.memset(WP[:, :, :], 0.0).then_inc(s_zero, 1)

            @block.sync
            def _(sp):
                sp.dma_start(U1_sb[:, :, :], U1.rearrange("(k p) n -> p k n", p=P)).then_inc(s_w, 16)
                sp.dma_start(U2_sb[:, :], U2).then_inc(s_w, 16)
                sp.dma_start(c1_col[:, :], c1.rearrange("(p o) -> p o", o=1)).then_inc(s_w, 16)
                sp.dma_start(c2_row[:, :], row(c2)).then_inc(s_w, 16)
                sp.dma_start(b2_row[:, :], row(b2)).then_inc(s_w, 16)
                sp.wait_ge(s_zero, 1)
                for k, (ws, wv) in enumerate(((W1_s, W1_v), (Ws_s, Ws_v))):
                    sp.dma_start(WP[0:32, k, 0:32], ws).then_inc(s_w, 16)
                    for d in range(3):
                        out = WP[32 + d:P:3, k, 32 + 32 * d:64 + 32 * d] if k == 0 else WP[32 + d:P:3, k, 32 + d:P:3]
                        sp.dma_start(out, wv, allow_slow_non_contiguous=True).then_inc(s_w, 16)

                def load(b):
                    p = b % 2
                    wait(sp, s_used, b - 1)
                    load_last(nc, sp, t, "B", b, t.slab_max, acc[:, p], s_in[p])
                    sp.dma_start(x1[:, p], node_batch(t.x1, b)).then_inc(s_in[p], 16)

                load(0)
                for b in range(NBATCH):
                    if b + 1 < NBATCH:
                        load(b + 1)
                    p = b % 2
                    sp.wait_ge(s_y, b + 1)
                    sp.dma_start(node_batch(t.x2, b), y[:, p]).then_inc(s_xout[p], 16)
                    sp.wait_ge(s_o, (b + 1) * BATCH)
                    sp.dma_start(node_batch(t.sv, b), O[:, p, :, 0:D]).then_inc(s_out[p], 16)
                    sp.dma_start(node_batch(t.skip, b), O[:, p, :, D:]).then_inc(s_out[p], 16)
                for p in range(2):
                    n = (NBATCH + 1 - p) // 2
                    sp.wait_ge(s_out[p], 32 * n)
                    sp.wait_ge(s_xout[p], 16 * n)

            @block.vector
            def _(dve):
                step = Chain(dve, s_dve)
                dve.wait_ge(s_w, 16 * WLOADS)
                dve.tensor_scalar(WP[:, :, :], WP[:, :, :], inv, None, ALU.mult).then_inc(s_scaled, 1)
                dve.wait_ge(s_scaled, 1)
                for b in range(NBATCH):
                    p = b % 2
                    dve.wait_ge(s_in[p], 16 * (BATCH + 1) * (b // 2 + 1))
                    filled = t.filled[:, b * BATCH:(b + 1) * BATCH]
                    step(dve.tensor_tensor(deg[:, 0, :], acc[:, p, :, D], filled, ALU.mult))
                    step(dve.tensor_scalar(has[:, :], deg[:, 0, :], 1.0, None, ALU.min))
                    dve.tensor_scalar(deg[:, 0, :], deg[:, 0, :], 1.0, None, ALU.max).then_inc(s_deg, 1)
                    dve.wait_ge(s_root, b + 1)
                    inverse_root(dve, step, deg[:, 0, :], deg[:, 1, :], deg[:, 2, :], deg[:, 3, :])
                    step(dve.tensor_tensor(t.dinv_sb[:, b * BATCH:(b + 1) * BATCH], deg[:, 2, :], has[:, :], ALU.mult))
                    step(dve.tensor_tensor(agg[:, :, :], acc[:, p, :, 0:D], bcast_mid(b2_row[:, :], BATCH), ALU.add))
                    dve.tensor_tensor(agg[:, :, :], agg[:, :, :], bcast_last(has[:, :], D), ALU.mult).then_inc(s_agg, 1)
                    dve.wait_ge(s_upd, b + 1)
                    wait(dve, s_xout[p], 16 * (b // 2))
                    step(dve.tensor_tensor(y[:, p], x1[:, p], bcast_mid(c2_row[:, :], BATCH), ALU.add))
                    step(dve.tensor_tensor(y[:, p, 0:4, :], y[:, p, 0:4, :], right[:, 2, :].rearrange("p (w n) -> p w n", w=4), ALU.add))
                    dve.tensor_tensor(y[:, p, 4:7, :], y[:, p, 4:7, :], right[:, 3, 0:3 * P].rearrange("p (w n) -> p w n", w=3),
                                      ALU.add).then_inc(s_used, 1)
                    dve.wait_ge(s_used, b + 1)
                    normalise(dve, step, y[:, p], stats, square[:, :, :], s_var, s_sd, b + 1)
                    dve.engine_nop().then_inc(s_y, 1)
                    wait(dve, s_out[p], 32 * (b // 2))
                    for w in range(BATCH):
                        n = b * BATCH + w
                        dve.wait_ge(s_prod, n + 1)
                        dve.tensor_copy(O[:, p, w, :], right[:, n % 2, 0:2 * D]).then_inc(s_o, 1)

            @block.scalar
            def _(act):
                for b in range(NBATCH):
                    act.wait_ge(s_deg, b + 1)
                    act.activation(deg[:, 1, :], deg[:, 0, :], ACT.Sqrt).then_inc(s_root, 1)
                    act.wait_ge(s_turn, b + 1)
                    copy_batch(act, inT[:, 0], left[:, 0:2])
                    copy_batch(act, inT[:, 1], left[:, 2:4]).then_inc(s_int, 1)
                    act.wait_ge(s_hid, b + 1)
                    act.activation(hidT[:, 0:4, :].rearrange("p w n -> p (w n)"), right[:, 0, :], ACT.Relu, bias=c1_col[:, :])
                    act.activation(hidT[:, 4:7, :].rearrange("p w n -> p (w n)"), right[:, 1, 0:3 * P], ACT.Relu,
                                   bias=c1_col[:, :]).then_inc(s_hidt, 1)
                    act.wait_ge(s_var, b + 1)
                    act.activation(stats[:, 2, :], stats[:, 1, :], ACT.Sqrt).then_inc(s_sd, 1)
                    act.wait_ge(s_turn2, b + 1)
                    copy_batch(act, yT, left[:, 0:2]).then_inc(s_yt, 1)

            @block.tensor
            def _(pe):
                pe.wait_ge(s_w, 16 * WLOADS)
                pe.wait_ge(s_scaled, 1)
                for b in range(NBATCH):
                    p = b % 2
                    pe.wait_ge(s_agg, b + 1)
                    wait(pe, s_yt, b)
                    turn_batch(pe, t, left[:, 0:2], x1[:, p])
                    turn_batch(pe, t, left[:, 2:4], agg).then_inc(s_turn, 1)
                    pe.wait_ge(s_int, b + 1)
                    wait(pe, s_o, b * BATCH)
                    for c, n in ((0, 4), (1, 3)):
                        for k in range(2):
                            last = pe.matmul(right[:, c, 0:n * P], U1_sb[:, k, :],
                                             inT[:, k, 4 * c:4 * c + n, :].rearrange("p w n -> p (w n)"), start=(k == 0), stop=(k == 1))
                    last.then_inc(s_hid, 1)
                    pe.wait_ge(s_hidt, b + 1)
                    for w in range(BATCH):
                        last = pe.matmul(right[:, 2 + w // 4, (w % 4) * P:(w % 4 + 1) * P], hidT[:, w, :], U2_sb[:, :], start=True, stop=True)
                    last.then_inc(s_upd, 1)
                    pe.wait_ge(s_y, b + 1)
                    turn_batch(pe, t, left[:, 0:2], y[:, p]).then_inc(s_turn2, 1)
                    pe.wait_ge(s_yt, b + 1)
                    for w in range(BATCH):
                        n = b * BATCH + w
                        wait(pe, s_o, n - 1)
                        pe.matmul(right[:, n % 2, 0:2 * D], yT[:, w, :], WP[:, :, :].rearrange("p k n -> p (k n)"),
                                  start=True, stop=True).then_inc(s_prod, 1)


def equi_sweep(nc, t, mW0, mb0, mW1, mb1, mW2, mb2):
    groups = TILES_B // GROUP
    E = GROUP * P
    M = 2 * D
    U = 32
    HID = 64
    with nc.cleanup_on_exit(), ExitStack() as ctx:
        def sem(name):
            return nc.alloc_semaphore("es_" + name)

        def sb(name, shape, dt=F32):
            return ctx.enter_context(nc.sbuf_tensor("es_" + name, shape, dt))

        def ps(name, shape):
            return ctx.enter_context(nc.psum_tensor("es_" + name, shape, F32))

        slots = sb("slots", [P, UNROLL, GROUP], I32)
        rows = sb("rows", [P, UNROLL, GROUP, D])
        W0 = sb("W0", [GROUP * 8, GROUP, HID])
        W1_sb = sb("W1", [HID, HID])
        W2_sb = sb("W2", [HID + 1, D])
        b0 = sb("b0", [HID, 1])
        b1 = sb("b1", [HID, 1])
        radial = sb("radial", [P, 2, GROUP, 8])
        radial_t = sb("radial_t", [GROUP * 8, 2, P])
        hid0 = sb("hid0", [HID, 2, E])
        hid1 = sb("hid1", [HID + 1, 2, E])
        scaled = sb("scaled", [P, 2, GROUP, D])
        q_s = sb("q_s", [P, 2, GROUP, U])
        dots = sb("dots", [P, 2, GROUP, 3, U])
        dot = sb("dot", [P, 2, GROUP, U])
        pick = sb("pick", [P, 2, GROUP, P])
        msg = sb("msg", [P, 2, GROUP, M])
        acc = sb("acc", [P, 4, GROUP, M])
        radial_ps = ps("radial_ps", [GROUP * 8, 2, 512])
        h0 = ps("h0", [HID, 512])
        h1 = ps("h1", [HID, 512])
        w = ps("w", [P, 2, GROUP, D])
        total = ps("total", [P, GROUP, M])

        s_w = sem("s_w")
        s_zero = sem("s_zero")
        s_init = sem("s_init")
        s_tick = sem("s_tick")
        s_pace = sem("s_pace")
        s_index = sem("s_index")
        s_gathered = [sem(f"s_gathered{q}") for q in range(UNROLL)]
        s_radial = sem("s_radial")
        s_turned = sem("s_turned")
        s_radial_t = sem("s_radial_t")
        s_h0 = sem("s_h0")
        s_hid0 = sem("s_hid0")
        s_h1 = sem("s_h1")
        s_hid1 = sem("s_hid1")
        s_weights = sem("s_weights")
        s_scaled = sem("s_scaled")
        s_pick = sem("s_pick")
        s_q = sem("s_q")
        s_dots = sem("s_dots")
        s_dot = sem("s_dot")
        s_msg = sem("s_msg")
        s_total = sem("s_total")
        s_acc = sem("s_acc")
        s_stored = [sem(f"s_stored{q}") for q in range(4)]

        with nc.Block() as block:
            @block.gpsimd
            def _(pool):
                pool.memset(W0[:, :, :], 0.0).then_inc(s_zero, 1)
                gather_rows(pool, t, "B", groups, t.sv, D, slots, rows, s_msg, 1, s_index, s_gathered, s_tick)

            @block.sync
            def _(sp):
                sp.wait_ge(s_zero, 1)
                for j in range(GROUP):
                    sp.dma_start(W0[8 * j:8 * j + 8, j, :], mW0).then_inc(s_w, 16)
                sp.dma_start(W1_sb[:, :], mW1).then_inc(s_w, 16)
                sp.dma_start(W2_sb[0:HID, :], mW2).then_inc(s_w, 16)
                sp.dma_start(W2_sb[HID:, :], mb2.rearrange("(o n) -> o n", o=1)).then_inc(s_w, 16)
                sp.dma_start(b0[:, :], mb0.rearrange("(p o) -> p o", o=1)).then_inc(s_w, 16)
                sp.dma_start(b1[:, :], mb1.rearrange("(p o) -> p o", o=1)).then_inc(s_w, 16)

                def store(g, q, r):
                    wait(sp, s_acc, GROUP * (g + 1))
                    sp.dma_start(t.slab_equi[bass.ds(g * GROUP, GROUP)].rearrange("j p c -> p j c"), acc[:, q % 4]).then_inc(s_stored[q % 4], 16)
                run_groups(sp, groups, [(0, store)])
                for q in range(4):
                    sp.wait_ge(s_stored[q], 16 * groups // 4)

            @block.scalar
            def _(act):
                act.wait_ge(s_w, 16 * 9)
                act.wait_ge(s_init, 1)

                def radial_g(g, q, r):
                    wait(act, s_turned, g - 1)
                    act.activation(radial[:, q % 2], t.ea8[:, bass.ds(g * GROUP, GROUP), :], ACT.Copy).then_inc(s_radial, 1)

                def radial_t_g(g, q, r):
                    wait(act, s_turned, g + 1)
                    wait(act, s_h0, g - 1)
                    act.activation(radial_t[:, q % 2, :], radial_ps[:, q % 2, 0:P], ACT.Copy).then_inc(s_radial_t, 1)

                def hid0_g(g, q, r):
                    wait(act, s_h0, g + 1)
                    wait(act, s_h1, g - 1)
                    act.activation(hid0[:, q % 2, :], h0[:, :], ACT.Silu, bias=b0[:, :]).then_inc(s_hid0, 1)

                def hid1_g(g, q, r):
                    wait(act, s_h1, g + 1)
                    wait(act, s_weights, g - 1)
                    act.activation(hid1[0:HID, q % 2, :], h1[:, :], ACT.Silu, bias=b1[:, :]).then_inc(s_hid1, 1)

                def scaled_g(g, q, r):
                    wait(act, s_gathered[q], 16 * GROUP * (r + 1))
                    wait(act, s_msg, g - 1)
                    for j in range(GROUP):
                        last = act.activation(scaled[:, q % 2, j, :], rows[:, q, j, :], ACT.Copy,
                                              scale=t.ea4[:, bass.ds(g * GROUP + j, 1), 0])
                    last.then_inc(s_scaled, 1)
                run_groups(act, groups, [(3, hid1_g), (0, radial_g), (1, radial_t_g), (2, hid0_g), (3, scaled_g)])

            @block.tensor
            def _(pe):
                pe.wait_ge(s_w, 16 * 9)
                pe.wait_ge(s_init, 1)

                def turn_g(g, q, r):
                    wait(pe, s_radial, g + 1)
                    wait(pe, s_radial_t, g - 1)
                    pe.transpose(radial_ps[:, q % 2, 0:P], radial[:, q % 2].rearrange("p j k -> p (j k)"), t.ident[:, :]).then_inc(s_turned, 1)

                def h0_g(g, q, r):
                    wait(pe, s_radial_t, g + 1)
                    wait(pe, s_hid0, g)
                    for j in range(GROUP):
                        last = pe.matmul(h0[:, j * P:(j + 1) * P], W0[:, j, :], radial_t[:, q % 2, :], start=True, stop=True)
                    last.then_inc(s_h0, 1)

                def h1_g(g, q, r):
                    wait(pe, s_hid0, g + 1)
                    wait(pe, s_hid1, g)
                    pe.sem_inc(s_pace, 1)
                    pe.matmul(h1[:, :], W1_sb[:, :], hid0[:, q % 2, :], start=True, stop=True).then_inc(s_h1, 1)

                def weights_g(g, q, r):
                    wait(pe, s_hid1, g + 1)
                    wait(pe, s_msg, g - 1)
                    pe.sem_inc(s_pace, 1)
                    for j in range(GROUP):
                        last = pe.matmul(w[:, q % 2, j, :], hid1[:, q % 2, j * P:(j + 1) * P], W2_sb[:, :], start=True, stop=True)
                    last.then_inc(s_weights, 1)

                def total_g(g, q, r):
                    wait(pe, s_pick, g + 1)
                    wait(pe, s_msg, g + 1)
                    wait(pe, s_acc, GROUP * g)
                    for j in range(GROUP):
                        last = pe.matmul(total[:, j, :], pick[:, q % 2, j, :], msg[:, q % 2, j, :], start=True, stop=True)
                    last.then_inc(s_total, 1)
                run_groups(pe, groups, [(0, turn_g), (1, h0_g), (2, h1_g), (3, weights_g), (4, total_g)])

            @block.vector
            def _(dve):
                dve.memset(hid1[HID:, :, :], 1.0)
                dve.memset(acc[:, 3, GROUP - 1, :], 0.0).then_inc(s_init, 1)
                dve.wait_ge(s_init, 1)

                def pick_g(g, q, r):
                    wait(dve, s_total, g - 1)
                    for j in range(GROUP):
                        last = dve.tensor_scalar(pick[:, q % 2, j, :], t.iota_f[:, :], t.dstrel["B"][:, bass.ds(g * GROUP + j, 1)],
                                                 None, ALU.is_equal)
                    last.then_inc(s_pick, 1)

                def part(g, q, i):
                    return w[:, q % 2, :, i * U:(i + 1) * U]

                def msg_g(g, q, r):
                    k = q % 2
                    sh = t.ea4[:, bass.ds(g * GROUP, GROUP), 1:4].unsqueeze(3).to_broadcast([P, GROUP, 3, U])
                    vectors = rows[:, q, :, U:].rearrange("p j (d u) -> p j d u", d=3)
                    wait(dve, s_gathered[q], 16 * GROUP * (r + 1))
                    wait(dve, s_weights, g + 1)
                    wait(dve, s_total, g - 1)
                    wait(dve, s_dot, 2 * (g - 1))
                    dve.tensor_tensor(dots[:, k], vectors, sh, ALU.mult).then_inc(s_dots, 1)
                    dve.tensor_tensor(q_s[:, k], part(g, q, 2), rows[:, q, :, 0:U], ALU.mult).then_inc(s_q, 1)
                    wait(dve, s_dots, g + 1)
                    dve.tensor_tensor(dot[:, k], dots[:, k, :, 0, :], dots[:, k, :, 1, :], ALU.add).then_inc(s_dot, 1)
                    wait(dve, s_scaled, g + 1)
                    dve.tensor_tensor(msg[:, k, :, 0:U], part(g, q, 0), scaled[:, k, :, 0:U], ALU.mult)
                    wait(dve, s_dot, 2 * g + 1)
                    dve.tensor_tensor(dot[:, k], dot[:, k], dots[:, k, :, 2, :], ALU.add).then_inc(s_dot, 1)
                    wait(dve, s_q, g + 1)
                    dve.tensor_tensor(msg[:, k, :, 2 * U:5 * U].rearrange("p j (d u) -> p j d u", d=3),
                                      q_s[:, k].unsqueeze(2).to_broadcast([P, GROUP, 3, U]), sh, ALU.mult)
                    wait(dve, s_dot, 2 * g + 2)
                    dve.tensor_tensor(msg[:, k, :, U:2 * U], part(g, q, 1), dot[:, k], ALU.mult)
                    dve.tensor_tensor(msg[:, k, :, 5 * U:].rearrange("p j (d u) -> p j d u", d=3),
                                      part(g, q, 3).unsqueeze(2).to_broadcast([P, GROUP, 3, U]),
                                      scaled[:, k, :, U:].rearrange("p j (d u) -> p j d u", d=3), ALU.mult).then_inc(s_msg, 1)

                def acc_g(g, q, r):
                    wait(dve, s_total, g + 1)
                    wait(dve, s_stored[q % 4], 16 * uses(q, r, 4))
                    for j in range(GROUP):
                        before = acc[:, q % 4, j - 1, :] if j else acc[:, (q - 1) % 4, GROUP - 1, :]
                        wait(dve, s_acc, g * GROUP + j)
                        dve.scalar_tensor_tensor(out=acc[:, q % 4, j, :], in0=before, scalar=t.same["B"][:, bass.ds(g * GROUP + j, 1)],
                                                 in1=total[:, j, :], op0=ALU.mult, op1=ALU.add).then_inc(s_acc, 1)
                run_groups(dve, groups, [(3, pick_g), (3, msg_g), (4, acc_g)])


def equi_nodes(nc, t, W2_s, W2_v):
    U = 32
    C = D + 1
    SILU_C = 1.6790524
    with nc.cleanup_on_exit(), ExitStack() as ctx:
        def sem(name):
            return nc.alloc_semaphore("en_" + name)

        def sb(name, shape, dt=F32):
            return ctx.enter_context(nc.sbuf_tensor("en_" + name, shape, dt))

        WB = sb("WB", [P, 2, 5 * U])
        acc = sb("acc", [P, 2, BATCH, 2 * D])
        skip = sb("skip", [P, 2, BATCH, D])
        x2 = sb("x2", [P, 2, BATCH, D])
        accT = sb("accT", [P, 2, BATCH, P])
        G = sb("G", [P, BATCH, 5 * U])
        gates = sb("gates", [P, BATCH, 2 * U])
        y = sb("y", [P, 2, BATCH, D])
        square = sb("square", [P, BATCH, D])
        stats = sb("stats", [P, 5, BATCH])
        O = sb("O", [P, 2, BATCH, C])
        turned = ctx.enter_context(nc.psum_tensor("en_turned", [P, 4, 512], F32))
        prod = ctx.enter_context(nc.psum_tensor("en_prod", [P, 4, 512], F32))
        s_zero = sem("s_zero")
        s_w = sem("s_w")
        s_in = [sem(f"s_in{p}") for p in range(2)]
        s_dve = sem("s_dve")
        s_turn = sem("s_turn")
        s_at = sem("s_at")
        s_prod = sem("s_prod")
        s_g = sem("s_g")
        s_gates = sem("s_gates")
        s_used = sem("s_used")
        s_var = sem("s_var")
        s_sd = sem("s_sd")
        s_y = sem("s_y")
        s_o = sem("s_o")
        s_out = [sem(f"s_out{p}") for p in range(2)]
        s_xout = [sem(f"s_xout{p}") for p in range(2)]
        vector_rows = [(0, 2 * U, 0, 0), (0, 3 * U, 0, 1), (1, 0, 0, 2), (1, U, U, 0), (1, 2 * U, U, 1), (1, 3 * U, U, 2)]
        WLOADS = 1 + len(vector_rows)

        with nc.Block() as block:
            @block.gpsimd
            def _(pool):
                pool.memset(WB[:, :, :], 0.0).then_inc(s_zero, 1)

            @block.sync
            def _(sp):
                sp.wait_ge(s_zero, 1)
                sp.dma_start(WB[0:2 * U, 0, 0:2 * U], W2_s).then_inc(s_w, 16)
                for half, row0, source, d in vector_rows:
                    sp.dma_start(WB[row0:row0 + U, half, 2 * U + d::3], W2_v[source:source + U, :],
                                 allow_slow_non_contiguous=True).then_inc(s_w, 16)

                def load(b):
                    p = b % 2
                    wait(sp, s_used, b - 1)
                    wait(sp, s_turn, b - 1)
                    load_last(nc, sp, t, "B", b, t.slab_equi, acc[:, p], s_in[p])
                    sp.dma_start(skip[:, p], node_batch(t.skip, b)).then_inc(s_in[p], 16)
                    sp.dma_start(x2[:, p], node_batch(t.x2, b)).then_inc(s_in[p], 16)

                load(0)
                for b in range(NBATCH):
                    if b + 1 < NBATCH:
                        load(b + 1)
                    p = b % 2
                    sp.wait_ge(s_y, b + 1)
                    sp.dma_start(node_batch(t.x3, b), y[:, p]).then_inc(s_xout[p], 16)
                    sp.wait_ge(s_o, b + 1)
                    sp.dma_start(node_batch(t.xd, b), O[:, p]).then_inc(s_out[p], 16)
                for p in range(2):
                    n = (NBATCH + 1 - p) // 2
                    sp.wait_ge(s_out[p], 16 * n)
                    sp.wait_ge(s_xout[p], 16 * n)

            @block.vector
            def _(dve):
                step = Chain(dve, s_dve)
                dve.wait_ge(s_w, 16 * WLOADS)
                step(dve.tensor_scalar(WB[:, :, :], WB[:, :, :], 1.0 / 32, None, ALU.mult))
                step(dve.tensor_scalar(WB[U:2 * U, 0, :], WB[U:2 * U, 0, :], 1.0 / 3 ** 0.5, None, ALU.mult))
                for b in range(NBATCH):
                    p = b % 2
                    filled = t.filled[:, b * BATCH:(b + 1) * BATCH]
                    dinv = t.dinv_sb[:, b * BATCH:(b + 1) * BATCH]
                    dve.wait_ge(s_in[p], 16 * (BATCH + 2) * (b // 2 + 1))
                    wait(dve, s_gates, b)
                    for c, n in ((0, 3), (3, 3), (6, 1)):
                        dve.wait_ge(s_prod, b * BATCH + c + n)
                        last = dve.tensor_tensor(G[:, c:c + n, :], prod[:, c // 3, 0:n * 5 * U].rearrange("p (w c) -> p w c", w=n),
                                                 bcast_last(filled[:, c:c + n], 5 * U), ALU.mult)
                    last.then_inc(s_g, 1)
                    wait(dve, s_xout[p], 16 * (b // 2))
                    dve.tensor_tensor(y[:, p], x2[:, p], skip[:, p], ALU.add).then_inc(s_used, 1)
                    dve.wait_ge(s_gates, b + 1)
                    step(dve.tensor_scalar(gates[:, :, :], gates[:, :, :], SILU_C, None, ALU.mult))
                    vectors = G[:, :, 2 * U:].rearrange("p w (u d) -> p w u d", d=3)
                    step(dve.tensor_tensor(vectors, vectors, gates[:, :, U:].unsqueeze(3).to_broadcast([P, BATCH, U, 3]), ALU.mult))
                    step(dve.tensor_tensor(y[:, p, :, 0:U], y[:, p, :, 0:U], gates[:, :, 0:U], ALU.add))
                    step(dve.tensor_tensor(y[:, p, :, U:], y[:, p, :, U:], G[:, :, 2 * U:], ALU.add))
                    normalise(dve, step, y[:, p], stats, square[:, :, :], s_var, s_sd, b + 1)
                    dve.engine_nop().then_inc(s_y, 1)
                    wait(dve, s_out[p], 16 * (b // 2))
                    step(dve.tensor_tensor(O[:, p, :, 0:D], y[:, p], bcast_last(dinv, D), ALU.mult))
                    dve.tensor_copy(O[:, p, :, D], dinv).then_inc(s_o, 1)

            @block.scalar
            def _(act):
                for b in range(NBATCH):
                    act.wait_ge(s_turn, b + 1)
                    wait(act, s_prod, b * BATCH)
                    copy_batch(act, accT[:, 0], turned[:, 0:2])
                    copy_batch(act, accT[:, 1], turned[:, 2:4]).then_inc(s_at, 1)
                    act.wait_ge(s_g, b + 1)
                    wait(act, s_used, b)
                    wait(act, s_y, b)
                    act.activation(gates[:, :, :], G[:, :, 0:2 * U], ACT.Silu).then_inc(s_gates, 1)
                    act.wait_ge(s_var, b + 1)
                    act.activation(stats[:, 2, :], stats[:, 1, :], ACT.Sqrt).then_inc(s_sd, 1)

            @block.tensor
            def _(pe):
                pe.wait_ge(s_dve, 2)
                for b in range(NBATCH):
                    p = b % 2
                    pe.wait_ge(s_in[p], 16 * (BATCH + 2) * (b // 2 + 1))
                    wait(pe, s_at, b)
                    turn_batch(pe, t, turned[:, 0:2], acc[:, p, :, 0:D])
                    turn_batch(pe, t, turned[:, 2:4], acc[:, p, :, D:]).then_inc(s_turn, 1)
                    pe.wait_ge(s_at, b + 1)
                    wait(pe, s_g, b)
                    for w in range(BATCH):
                        for k in range(2):
                            last = pe.matmul(prod[:, w // 3, (w % 3) * 5 * U:(w % 3 + 1) * 5 * U], accT[:, k, w, :], WB[:, k, :],
                                             start=(k == 0), stop=(k == 1))
                        last.then_inc(s_prod, 1)


def norm_sweep(nc, t):
    groups = TILES_B // GROUP
    C = D + 1
    with nc.cleanup_on_exit(), ExitStack() as ctx:
        def sem(name):
            return nc.alloc_semaphore("ns_" + name)

        def sb(name, shape, dt=F32):
            return ctx.enter_context(nc.sbuf_tensor("ns_" + name, shape, dt))

        slots = sb("slots", [P, UNROLL, GROUP], I32)
        rows = sb("rows", [P, UNROLL, GROUP, C])
        pick = sb("pick", [P, 2, GROUP, P])
        acc = sb("acc", [P, 4, GROUP, C])
        total = ctx.enter_context(nc.psum_tensor("ns_total", [P, 2, 2, 512], F32))
        s_init = sem("s_init")
        s_tick = sem("s_tick")
        s_index = sem("s_index")
        s_gathered = [sem(f"s_gathered{q}") for q in range(UNROLL)]
        s_pick = sem("s_pick")
        s_total = sem("s_total")
        s_acc = sem("s_acc")
        s_stored = [sem(f"s_stored{q}") for q in range(4)]

        with nc.Block() as block:
            @block.gpsimd
            def _(pool):
                gather_rows(pool, t, "B", groups, t.xd, C, slots, rows, s_total, 1, s_index, s_gathered, s_tick)

            @block.sync
            def _(sp):
                def store(g, q, r):
                    wait(sp, s_acc, GROUP * (g + 1))
                    sp.dma_start(t.slab_norm[bass.ds(g * GROUP, GROUP)].rearrange("j p c -> p j c"), acc[:, q % 4]).then_inc(s_stored[q % 4], 16)
                run_groups(sp, groups, [(0, store)])
                for q in range(4):
                    sp.wait_ge(s_stored[q], 16 * groups // 4)

            @block.tensor
            def _(pe):
                def total_g(g, q, r):
                    wait(pe, s_gathered[q], 16 * GROUP * (r + 1))
                    wait(pe, s_pick, g + 1)
                    wait(pe, s_acc, GROUP * (g - 1))
                    for j in range(GROUP):
                        last = pe.matmul(total[:, q % 2, j // 2, (j % 2) * C:(j % 2 + 1) * C], pick[:, q % 2, j, :], rows[:, q, j, :],
                                         start=True, stop=True)
                    last.then_inc(s_total, 1)
                run_groups(pe, groups, [(0, total_g)])

            @block.vector
            def _(dve):
                dve.memset(acc[:, 3, GROUP - 1, :], 0.0).then_inc(s_init, 1)
                dve.wait_ge(s_init, 1)

                def pick_g(g, q, r):
                    wait(dve, s_total, g - 1)
                    for j in range(GROUP):
                        last = dve.tensor_scalar(pick[:, q % 2, j, :], t.iota_f[:, :], t.dstrel["B"][:, bass.ds(g * GROUP + j, 1)],
                                                 None, ALU.is_equal)
                    last.then_inc(s_pick, 1)

                def acc_g(g, q, r):
                    wait(dve, s_total, g + 1)
                    wait(dve, s_stored[q % 4], 16 * uses(q, r, 4))
                    for j in range(GROUP):
                        before = acc[:, q % 4, j - 1, :] if j else acc[:, (q - 1) % 4, GROUP - 1, :]
                        wait(dve, s_acc, g * GROUP + j)
                        dve.scalar_tensor_tensor(out=acc[:, q % 4, j, :], in0=before, scalar=t.same["B"][:, bass.ds(g * GROUP + j, 1)],
                                                 in1=total[:, q % 2, j // 2, (j % 2) * C:(j % 2 + 1) * C], op0=ALU.mult,
                                                 op1=ALU.add).then_inc(s_acc, 1)
                run_groups(dve, groups, [(0, pick_g), (1, acc_g)])


def norm_nodes(nc, t, W1_w, W1_b, out):
    C = D + 1
    with nc.cleanup_on_exit(), ExitStack() as ctx:
        def sem(name):
            return nc.alloc_semaphore("nn_" + name)

        def sb(name, shape, dt=F32):
            return ctx.enter_context(nc.sbuf_tensor("nn_" + name, shape, dt))

        W = sb("W", [P, P])
        WT = sb("WT", [P, P])
        bias = sb("bias", [P, D])
        acc = sb("acc", [P, 2, BATCH, C])
        x3 = sb("x3", [P, 2, BATCH, D])
        prod_in = sb("prod_in", [P, BATCH, D])
        prod_inT = sb("prod_inT", [P, BATCH, P])
        r = sb("r", [P, BATCH, D])
        coef = sb("coef", [P, BATCH])
        y = sb("y", [P, 2, BATCH, D])
        square = sb("square", [P, BATCH, D])
        stats = sb("stats", [P, 5, BATCH])
        turned = ctx.enter_context(nc.psum_tensor("nn_turned", [P, 2, 512], F32))
        prod = ctx.enter_context(nc.psum_tensor("nn_prod", [P, 2, 512], F32))
        s_w = sem("s_w")
        s_wturn = sem("s_wturn")
        s_in = [sem(f"s_in{p}") for p in range(2)]
        s_dve = sem("s_dve")
        s_wt = sem("s_wt")
        s_pin = sem("s_pin")
        s_turn = sem("s_turn")
        s_pt = sem("s_pt")
        s_prod = sem("s_prod")
        s_used = sem("s_used")
        s_var = sem("s_var")
        s_sd = sem("s_sd")
        s_y = sem("s_y")
        s_out = [sem(f"s_out{p}") for p in range(2)]

        with nc.Block() as block:
            @block.sync
            def _(sp):
                sp.dma_start(W[:, :], W1_w).then_inc(s_w, 16)
                sp.dma_start(bias[:, :], row(W1_b)).then_inc(s_w, 16)

                def load(b):
                    p = b % 2
                    wait(sp, s_used, b - 1)
                    load_last(nc, sp, t, "B", b, t.slab_norm, acc[:, p], s_in[p])
                    sp.dma_start(x3[:, p], node_batch(t.x3, b)).then_inc(s_in[p], 16)

                load(0)
                for b in range(NBATCH):
                    if b + 1 < NBATCH:
                        load(b + 1)
                    p = b % 2
                    sp.wait_ge(s_y, b + 1)
                    if b < NBATCH - 1:
                        sp.dma_start(node_batch(out, b), y[:, p]).then_inc(s_out[p], 16)
                    else:
                        full = NODES // P * P
                        n = BATCH - 1
                        sp.dma_start(out[b * BATCH * P:full, :].rearrange("(w p) d -> p w d", p=P), y[:, p, 0:n, :]).then_inc(s_out[p], 16)
                        sp.dma_start(out[full:NODES, :], y[0:NODES - full, p, n, :]).then_inc(s_out[p], 16)
                sp.wait_ge(s_out[0], 16 * ((NBATCH + 1) // 2 + 1))
                sp.wait_ge(s_out[1], 16 * (NBATCH // 2))

            @block.vector
            def _(dve):
                step = Chain(dve, s_dve)
                dve.wait_ge(s_wturn, 1)
                dve.tensor_copy(WT[:, :], prod[:, 0, 0:P]).then_inc(s_wt, 1)
                dve.wait_ge(s_wt, 1)
                for b in range(NBATCH):
                    p = b % 2
                    windows = slice(b * BATCH, (b + 1) * BATCH)
                    dve.wait_ge(s_in[p], 16 * (BATCH + 1) * (b // 2 + 1))
                    wait(dve, s_turn, b)
                    dve.tensor_tensor(prod_in[:, :, :], acc[:, p, :, 0:D], x3[:, p], ALU.mult).then_inc(s_pin, 1)
                    step(dve.tensor_tensor(coef[:, :], t.dinv_sb[:, windows], t.filled[:, windows], ALU.mult))
                    step(dve.tensor_tensor(r[:, :, :], x3[:, p], bcast_mid(bias[:, :], BATCH), ALU.add))
                    step(dve.tensor_tensor(r[:, :, :], r[:, :, :], acc[:, p, :, D:].to_broadcast([P, BATCH, D]), ALU.mult))
                    dve.wait_ge(s_prod, b + 1)
                    step(dve.tensor_tensor(r[:, 0:4, :], r[:, 0:4, :], prod[:, 0, :].rearrange("p (w n) -> p w n", w=4), ALU.add))
                    step(dve.tensor_tensor(r[:, 4:7, :], r[:, 4:7, :], prod[:, 1, 0:3 * P].rearrange("p (w n) -> p w n", w=3), ALU.add))
                    step(dve.tensor_tensor(r[:, :, :], r[:, :, :], bcast_last(coef[:, :], D), ALU.mult))
                    step(dve.scalar_tensor_tensor(out=r[:, :, :], in0=r[:, :, :], scalar=0.01, in1=r[:, :, :], op0=ALU.mult, op1=ALU.max))
                    wait(dve, s_out[p], 16 * (b // 2))
                    dve.tensor_tensor(y[:, p], x3[:, p], r[:, :, :], ALU.add).then_inc(s_used, 1)
                    dve.wait_ge(s_used, b + 1)
                    normalise(dve, step, y[:, p], stats, square[:, :, :], s_var, s_sd, b + 1)
                    dve.engine_nop().then_inc(s_y, 1)

            @block.scalar
            def _(act):
                for b in range(NBATCH):
                    act.wait_ge(s_turn, b + 1)
                    wait(act, s_prod, b)
                    copy_batch(act, prod_inT, turned).then_inc(s_pt, 1)
                    act.wait_ge(s_var, b + 1)
                    act.activation(stats[:, 2, :], stats[:, 1, :], ACT.Sqrt).then_inc(s_sd, 1)

            @block.tensor
            def _(pe):
                pe.wait_ge(s_w, 32)
                pe.transpose(prod[:, 0, 0:P], W[:, :], t.ident[:, :]).then_inc(s_wturn, 1)
                pe.wait_ge(s_wt, 1)
                for b in range(NBATCH):
                    pe.wait_ge(s_pin, b + 1)
                    wait(pe, s_pt, b)
                    turn_batch(pe, t, turned, prod_in).then_inc(s_turn, 1)
                    pe.wait_ge(s_pt, b + 1)
                    wait(pe, s_used, b)
                    for w in range(BATCH):
                        last = pe.matmul(prod[:, w // 4, (w % 4) * P:(w % 4 + 1) * P], prod_inT[:, w, :], WT[:, :], start=True, stop=True)
                    last.then_inc(s_prod, 1)


def graph_layers(nc, a, out):
    with ExitStack() as ctx:
        t = Store()
        allocate(nc, ctx, t)

        def layer(prefix, names):
            return [a[f"{prefix}_{n}"] for n in names.split()]

        prepare_schedule(nc, t, a["x"], a["src"], a["dst"], a["edge_weight"], a["edge_attr_4"], a["edge_attr_8"])
        prepare_tables(nc, t)
        for i in range(2):
            attention_nodes(nc, t, i, *layer(f"L0_gnn_l{i + 1}", "Wl bl Wr br att Wres bias"))
            attention_sweep(nc, t, i, a[f"L0_gnn_l{i + 1}_att"])
        max_nodes(nc, t, *layer("L1_gnn", "W1 b1"))
        max_sweep(nc, t, *layer("L1_gnn", "W1 W2"))
        update_nodes(nc, t, *layer("L1_gnn", "b2 U1 c1 U2 c2"), *layer("L2_gnn", "W1_s W1_v Ws_s Ws_v"))
        equi_sweep(nc, t, *layer("L2_gnn", "mW0 mb0 mW1 mb1 mW2 mb2"))
        equi_nodes(nc, t, *layer("L2_gnn", "W2_s W2_v"))
        norm_sweep(nc, t)
        norm_nodes(nc, t, *layer("L3_gnn", "W1_w W1_b"), out)


_INS = ['x', 'src', 'dst', 'edge_attr_4', 'edge_attr_8', 'edge_weight',
        'L0_gnn_l1_Wl', 'L0_gnn_l1_bl', 'L0_gnn_l1_Wr', 'L0_gnn_l1_br', 'L0_gnn_l1_att', 'L0_gnn_l1_Wres', 'L0_gnn_l1_bias',
        'L0_gnn_l2_Wl', 'L0_gnn_l2_bl', 'L0_gnn_l2_Wr', 'L0_gnn_l2_br', 'L0_gnn_l2_att', 'L0_gnn_l2_Wres', 'L0_gnn_l2_bias',
        'L1_gnn_W1', 'L1_gnn_b1', 'L1_gnn_W2', 'L1_gnn_b2', 'L1_gnn_U1', 'L1_gnn_c1', 'L1_gnn_U2', 'L1_gnn_c2',
        'L2_gnn_W1_s', 'L2_gnn_W1_v', 'L2_gnn_mW0', 'L2_gnn_mb0', 'L2_gnn_mW1', 'L2_gnn_mb1', 'L2_gnn_mW2', 'L2_gnn_mb2',
        'L2_gnn_W2_s', 'L2_gnn_W2_v', 'L2_gnn_Ws_s', 'L2_gnn_Ws_v', 'L3_gnn_W1_w', 'L3_gnn_W1_b']
_OUTS = [((6250, 128), 'float32')]


def kernel(**inputs):
    import numpy as _np
    import concourse.bacc as _bacc
    from concourse import mybir as _mybir
    from concourse.bass_utils import run_bass_kernel_spmd as _run

    nc = _bacc.Bacc("TRN2", target_bir_lowering=False, num_devices=1)
    arrays, args = {}, {}
    for name in _INS:
        a = _np.ascontiguousarray(inputs[name])
        arrays[f"in_{name}_dram"] = a
        args[name] = nc.dram_tensor(f"in_{name}_dram", a.shape, _mybir.dt.from_np(a.dtype), kind="ExternalInput").ap()
    outs = []
    for i, (shape, dtype) in enumerate(_OUTS):
        dt = _mybir.dt.from_np(_np.dtype(dtype))
        outs.append(nc.dram_tensor(f"out_{i}_dram", shape, dt, kind="ExternalOutput").ap())
    graph_layers(nc, args, *outs)
    r = _run(nc, [arrays], core_ids=[0])
    got = tuple(r.results[0][f"out_{i}_dram"] for i in range(len(_OUTS)))
    return got[0]
```

```python
from contextlib import ExitStack

import concourse.bass as bass
from concourse import mybir

P = 128
NODES = 6250
EDGES = 100000
D = 128
WINDOWS = -(-NODES // P)
NPAD = WINDOWS * P
GROUP = 4
UNROLL = 8
STEP = GROUP * UNROLL
BLOCKS = 7
TABLE = BLOCKS * P
TILES_B = -(-(EDGES // P + WINDOWS + 1) // STEP) * STEP
TILES_A = -(-(EDGES // P + 2 * WINDOWS + 1) // STEP) * STEP
TAIL = P * 116
EDGE0 = NPAD
BATCH = 7
NBATCH = WINDOWS // BATCH
COUNT_P = 125
BIG = 1e30
FAR = 1000000
EPS = 1e-5

F32 = mybir.dt.float32
I32 = mybir.dt.int32
ALU = mybir.AluOpType
ACT = mybir.ActivationFunctionType
AX = mybir.AxisListType
assert TILES_A <= TABLE and NBATCH * BATCH == WINDOWS and COUNT_P * 800 == EDGES


def wait(eng, sem, value):
    if isinstance(value, int) and value <= 0:
        return
    eng.wait_ge(sem, value)


def uses(q, r, ring):
    return r * (UNROLL // ring) + q // ring


def run_groups(eng, groups, stages):
    last = max(lag for entry in stages for lag, _ in (entry if isinstance(entry, list) else [entry]))

    def step(place):
        for entry in stages:
            if isinstance(entry, list):
                for j in range(GROUP):
                    for lag, f in entry:
                        if place(lag):
                            f(*place(lag), j)
            elif place(entry[0]):
                entry[1](*place(entry[0]))

    def peeled(g):
        step(lambda lag: (g - lag, (g - lag) % UNROLL, (g - lag) // UNROLL) if 0 <= g - lag < groups else None)

    head = 2 * UNROLL
    for g in range(head):
        peeled(g)
    with eng.Fori(head // UNROLL, groups // UNROLL) as r:
        for q in range(UNROLL):
            step(lambda lag: (r * UNROLL + (q - lag), (q - lag) % UNROLL, r + (q - lag) // UNROLL))
    for g in range(groups, groups + last):
        peeled(g)


class Chain:

    def __init__(self, eng, sem, start=0):
        self.eng, self.sem, self.start, self.n = eng, sem, start, 0

    def __call__(self, instruction):
        self.n += 1
        instruction.then_inc(self.sem, 1)
        self.eng.wait_ge(self.sem, self.start + self.n)


def bcast_mid(ap, n):
    return ap.unsqueeze(1).to_broadcast([ap.shape[0], n, ap.shape[1]])


def bcast_last(ap, n):
    return ap.unsqueeze(2).to_broadcast([ap.shape[0], ap.shape[1], n])


class Store:
    pass


def allocate(nc, ctx, t):
    def sb(name, shape, dt=F32):
        return ctx.enter_context(nc.sbuf_tensor(name, shape, dt))

    def dram(name, shape, dt=F32):
        return nc.dram_tensor(name, shape, dt, kind="Internal").ap()

    t.iota_f = sb("iota_f", [P, P])
    t.iota_p = sb("iota_p", [P, 1])
    t.ident = sb("ident", [P, P])
    t.ones = sb("ones", [P, P])
    t.window = {x: sb(f"window_{x}", [P, BLOCKS]) for x in "AB"}
    t.start = {x: sb(f"start_{x}", [P, BLOCKS]) for x in "AB"}
    t.offsets = {n: sb(f"offsets_{n}", [P, BLOCKS], I32) for n in ("A", "B", "Bprev", "ew", "ea4", "ea8")}
    t.last_tile = {x: sb(f"last_tile_{x}", [P, WINDOWS], I32) for x in "AB"}
    t.filled = sb("filled", [P, WINDOWS])
    t.window_row = {x: sb(f"window_row_{x}", [1, TABLE], I32) for x in "AB"}
    t.same = {x: sb(f"same_{x}", [P, TABLE]) for x in "AB"}
    t.newwin = sb("newwin", [P, TABLE])
    t.src = {x: sb(f"src_{x}", [P, TABLE], I32) for x in "AB"}
    t.dstrel = {x: sb(f"dstrel_{x}", [P, TABLE]) for x in "AB"}
    t.lastrel = sb("lastrel", [P, TABLE])
    t.dinv_sb = sb("dinv_sb", [P, WINDOWS])
    t.ea4 = sb("ea4", [P, TABLE, 4])
    t.ea8 = sb("ea8", [P, TABLE, 8])

    t.dst_all = dram("dst_all", [EDGE0 + EDGES + TAIL], I32)
    t.src_all = dram("src_all", [EDGE0 + EDGES + TAIL], I32)
    t.ew_all = dram("ew_all", [EDGES + TAIL])
    t.ea4_all = dram("ea4_all", [(EDGES + TAIL) * 4])
    t.ea8_all = dram("ea8_all", [(EDGES + TAIL) * 8])
    t.x_pad = dram("x_pad", [NPAD, D])
    t.win_f = {x: dram(f"win_f_{x}", [TABLE]) for x in "AB"}
    t.win_i = {x: dram(f"win_i_{x}", [TABLE], I32) for x in "AB"}
    t.dst_rows = {x: dram(f"dst_rows_{x}", [TABLE, P]) for x in "AB"}
    t.seg_rows = dram("seg_rows", [TABLE, P])
    t.ew_rows = dram("ew_rows", [TABLE, P])
    t.xl = [dram(f"xl{i}", [NPAD, D]) for i in range(2)]
    t.xr = [dram(f"xr{i}", [NPAD, D]) for i in range(2)]
    t.res = [dram(f"res{i}", [NPAD, D]) for i in range(2)]
    t.x1 = dram("x1", [NPAD, D])
    t.ha = dram("ha", [NPAD, D])
    t.hb = dram("hb", [NPAD, D])
    t.x2 = dram("x2", [NPAD, D])
    t.sv = dram("sv", [NPAD, D])
    t.skip = dram("skip", [NPAD, D])
    t.x3 = dram("x3", [NPAD, D])
    t.xd = dram("xd", [NPAD, D + 1])
    t.slab_att = [dram(f"slab_att{i}", [TILES_A, P, D + 1]) for i in range(2)]
    t.slab_max = dram("slab_max", [TILES_B, P, D + 1])
    t.slab_equi = dram("slab_equi", [TILES_B, P, 2 * D])
    t.slab_norm = dram("slab_norm", [TILES_B, P, D + 1])


def prepare_schedule(nc, t, x, src, dst, edge_weight, edge_attr_4, edge_attr_8):
    with nc.cleanup_on_exit(), ExitStack() as ctx:
        def sem(name):
            return nc.alloc_semaphore("ps" + "_" + name)

        def sb(name, shape, dt=F32):
            return ctx.enter_context(nc.sbuf_tensor("ps_" + name, shape, dt))

        iota_fi = sb("iota_fi", [P, P], I32)
        iota_pi = sb("iota_pi", [P, 1], I32)
        self_id = sb("self_id", [P, WINDOWS], I32)
        tile_i = sb("tile_i", [P, BLOCKS], I32)
        zeros = sb("zeros", [P, 8 * TAIL // P])
        zeros_i = sb("zeros_i", [P, TAIL // P], I32)
        far = sb("far", [P, TAIL // P], I32)
        dst_i = sb("dst_i", [COUNT_P, 800], I32)
        dst_f = sb("dst_f", [COUNT_P, 800])
        junk = sb("junk", [P, 800])
        below = sb("below", [P, WINDOWS - 1])
        first = sb("first", [P, WINDOWS + 1])
        count = sb("count", [P, WINDOWS])
        rounded = sb("rounded", [P, WINDOWS])
        tiles_i = sb("tiles_i", [P, WINDOWS], I32)
        tiles_s = sb("tiles_s", [P, WINDOWS], I32)
        tiles = sb("tiles", [P, WINDOWS])
        tile0 = {k: sb(f"tile0_{k}", [P, WINDOWS + 1]) for k in "AB"}
        shift = {k: sb(f"shift_{k}", [P, WINDOWS]) for k in "AB"}
        last_f = {k: sb(f"last_f_{k}", [P, WINDOWS]) for k in "AB"}
        tile_f = sb("tile_f", [P, BLOCKS])
        ssum = {k: sb(f"ssum_{k}", [P, BLOCKS]) for k in "AB"}
        isself = sb("isself", [P, BLOCKS])
        pos = sb("pos", [P, BLOCKS])
        gap = sb("gap", [P, BLOCKS])
        edge_f = sb("edge_f", [P, BLOCKS])
        win_i = {k: sb(f"win_i_{k}", [P, BLOCKS], I32) for k in "AB"}
        total = ctx.enter_context(nc.psum_tensor("ps_total", [P, 512], F32))

        s_iota = sem("s_iota")
        s_fill = sem("s_fill")
        s_copy = sem("s_copy")
        s_dst = sem("s_dst")
        s_dve = sem("s_dve")
        s_counted = sem("s_counted")
        s_total = sem("s_total")
        s_windows = sem("s_windows")
        s_lists = sem("s_lists")

        with nc.Block() as block:
            @block.gpsimd
            def _(pool):
                pool.iota(iota_fi[:, :], pattern=[[1, P]], base=0, channel_multiplier=0).then_inc(s_iota, 1)
                pool.iota(iota_pi[:, :], pattern=[[0, 1]], base=0, channel_multiplier=1).then_inc(s_iota, 1)
                pool.iota(tile_i[:, :], pattern=[[P, BLOCKS]], base=0, channel_multiplier=1).then_inc(s_iota, 1)
                pool.iota(self_id[:, :], pattern=[[1, WINDOWS]], base=0, channel_multiplier=WINDOWS).then_inc(s_fill, 1)
                pool.memset(zeros[:, :], 0.0).then_inc(s_fill, 1)
                pool.memset(zeros_i[:, :], 0).then_inc(s_fill, 1)
                pool.memset(far[:, :], FAR).then_inc(s_fill, 1)

            @block.sync
            def _(sp):
                sp.dma_start(dst_i[:, :], dst.rearrange("(p j) -> p j", p=COUNT_P)).then_inc(s_dst, 16)
                sp.dma_start(t.dst_all[EDGE0:EDGE0 + EDGES].rearrange("(p j) -> p j", p=P // 4),
                             dst.rearrange("(p j) -> p j", p=P // 4)).then_inc(s_copy, 16)
                sp.dma_start(t.src_all[EDGE0:EDGE0 + EDGES].rearrange("(p j) -> p j", p=P // 4),
                             src.rearrange("(p j) -> p j", p=P // 4)).then_inc(s_copy, 16)
                sp.dma_start(t.ew_all[0:EDGES].rearrange("(p j) -> p j", p=P // 4),
                             edge_weight.rearrange("(p j) -> p j", p=P // 4)).then_inc(s_copy, 16)
                sp.dma_start(t.ea4_all[0:EDGES * 4].rearrange("(p j) -> p j", p=P // 4),
                             edge_attr_4.rearrange("(p j) k -> p (j k)", p=P // 4)).then_inc(s_copy, 16)
                sp.dma_start(t.ea8_all[0:EDGES * 8].rearrange("(p j) -> p j", p=P // 4),
                             edge_attr_8.rearrange("(p j) k -> p (j k)", p=P // 4)).then_inc(s_copy, 16)
                sp.dma_start(t.x_pad[0:NODES, :], x).then_inc(s_copy, 16)
                sp.wait_ge(s_fill, 4)
                for a in (t.dst_all, t.src_all):
                    sp.dma_start(a[0:NPAD].rearrange("(p j) -> p j", p=P), self_id[:, :]).then_inc(s_copy, 16)
                sp.dma_start(t.dst_all[EDGE0 + EDGES:].rearrange("(p j) -> p j", p=P), far[:, :]).then_inc(s_copy, 16)
                sp.dma_start(t.src_all[EDGE0 + EDGES:].rearrange("(p j) -> p j", p=P), zeros_i[:, :]).then_inc(s_copy, 16)
                for a, k in ((t.ew_all, 1), (t.ea4_all, 4), (t.ea8_all, 8)):
                    sp.dma_start(a[k * EDGES:].rearrange("(p j) -> p j", p=P), zeros[:, 0:k * TAIL // P]).then_inc(s_copy, 16)
                sp.dma_start(t.x_pad[NODES:NPAD, :], zeros[0:NPAD - NODES, 0:D]).then_inc(s_copy, 16)
                sp.wait_ge(s_copy, 16 * 14)
                sp.wait_ge(s_windows, 1)
                for k in "AB":
                    sp.dma_start(t.win_f[k].rearrange("(b p) -> p b", p=P), t.window[k][:, :],
                                 allow_slow_non_contiguous=True).then_inc(s_lists, 16)
                    sp.dma_start(t.win_i[k].rearrange("(b p) -> p b", p=P), win_i[k][:, :],
                                 allow_slow_non_contiguous=True).then_inc(s_lists, 16)
                sp.wait_ge(s_lists, 64)

            @block.tensor
            def _(pe):
                pe.wait_ge(s_counted, 1)
                pe.matmul(total[:, 0:WINDOWS - 1], t.ones[0:COUNT_P, :], below[0:COUNT_P, :],
                          start=True, stop=True).then_inc(s_total, 1)

            @block.vector
            def _(dve):
                step = Chain(dve, s_dve)
                dve.wait_ge(s_iota, 3)
                step(dve.tensor_copy(t.iota_f[:, :], iota_fi[:, :]))
                step(dve.tensor_copy(t.iota_p[:, :], iota_pi[:, :]))
                step(dve.tensor_copy(tile_f[:, :], tile_i[:, :]))
                step(dve.memset(t.ones[:, :], 1.0))
                step(dve.tensor_scalar(t.ident[:, :], t.iota_f[:, :], t.iota_p[:, :], None, ALU.is_equal))
                dve.wait_ge(s_dst, 16)
                step(dve.tensor_copy(dst_f[:, :], dst_i[:, :]))
                for w in range(1, WINDOWS):
                    step(dve.tensor_scalar(junk[0:COUNT_P, :], dst_f[:, :], float(P * w), 0.0, ALU.is_lt, ALU.add,
                                           accum_out=below[0:COUNT_P, w - 1:w]))
                dve.engine_nop().then_inc(s_counted, 1)
                dve.wait_ge(s_total, 1)
                step(dve.memset(first[:, 0:1], 0.0))
                step(dve.tensor_copy(first[:, 1:WINDOWS], total[:, 0:WINDOWS - 1]))
                step(dve.memset(first[:, WINDOWS:], float(EDGES)))
                step(dve.tensor_tensor(count[:, :], first[:, 1:], first[:, 0:WINDOWS], ALU.subtract))
                step(dve.tensor_scalar(rounded[:, :], count[:, :], float(P - 1), None, ALU.add))
                step(dve.tensor_copy(tiles_i[:, :], rounded[:, :]))
                step(dve.tensor_scalar(tiles_s[:, :], tiles_i[:, :], 7, None, ALU.logical_shift_right))
                step(dve.tensor_copy(tiles[:, :], tiles_s[:, :]))
                step(dve.tensor_scalar(t.filled[:, :], tiles[:, :], 1.0, None, ALU.min))
                step(dve.memset(tile0["B"][:, 0:1], 0.0))
                step(dve.tensor_tensor_scan(tile0["B"][:, 1:], t.ones[:, 0:WINDOWS], tiles[:, :], 0.0, ALU.mult, ALU.add))
                step(dve.tensor_tensor(tile0["A"][:, :], tile0["B"][:, :], t.iota_f[:, 0:WINDOWS + 1], ALU.add))
                step(dve.scalar_tensor_tensor(out=shift["B"][:, :], in0=tiles[:, :], scalar=-float(P), in1=count[:, :],
                                              op0=ALU.mult, op1=ALU.add))
                step(dve.tensor_scalar(shift["A"][:, :], shift["B"][:, :], -float(P), None, ALU.add))
                step(dve.tensor_scalar(shift["A"][:, WINDOWS - 1:], shift["A"][:, WINDOWS - 1:], float(P), None, ALU.add))
                for k in "AB":
                    step(dve.tensor_scalar(last_f[k][:, :], tile0[k][:, 1:], -1.0, 0.0, ALU.add, ALU.max))
                    step(dve.tensor_copy(t.last_tile[k][:, :], last_f[k][:, :]))
                    for b in range(BLOCKS):
                        tile = tile_f[:, b:b + 1]
                        step(dve.tensor_scalar(junk[:, 0:WINDOWS - 1], tile0[k][:, 1:WINDOWS], tile, 0.0, ALU.is_le, ALU.add,
                                               accum_out=t.window[k][:, b:b + 1]))
                        step(dve.scalar_tensor_tensor(out=junk[:, 0:WINDOWS], in0=tile0[k][:, 1:], scalar=tile, in1=shift[k][:, :],
                                                      op0=ALU.is_le, op1=ALU.mult, accum_out=ssum[k][:, b:b + 1]))
                        if k == "A":
                            step(dve.tensor_scalar(junk[:, 0:WINDOWS], tile0["A"][:, 0:WINDOWS], tile, 0.0, ALU.is_equal, ALU.add,
                                                   accum_out=isself[:, b:b + 1]))
                    step(dve.tensor_copy(win_i[k][:, :], t.window[k][:, :]))
                    step(dve.scalar_tensor_tensor(out=pos[:, :], in0=tile_f[:, :], scalar=float(P), in1=ssum[k][:, :],
                                                  op0=ALU.mult, op1=ALU.add))
                    if k == "B":
                        step(dve.tensor_scalar(t.start["B"][:, :], pos[:, :], float(EDGE0), None, ALU.add))
                    else:
                        step(dve.tensor_scalar(t.start["A"][:, :], pos[:, :], float(EDGE0 - P), None, ALU.add))
                        step(dve.scalar_tensor_tensor(out=gap[:, :], in0=t.window["A"][:, :], scalar=float(P), in1=t.start["A"][:, :],
                                                      op0=ALU.mult, op1=ALU.subtract))
                        step(dve.tensor_tensor(gap[:, :], gap[:, :], isself[:, :], ALU.mult))
                        step(dve.tensor_tensor(t.start["A"][:, :], t.start["A"][:, :], gap[:, :], ALU.add))
                    step(dve.tensor_copy(t.offsets[k][:, :], t.start[k][:, :]))
                dve.engine_nop().then_inc(s_windows, 1)
                step(dve.tensor_scalar(edge_f[:, :], t.start["B"][:, :], -1.0, None, ALU.add))
                step(dve.tensor_copy(t.offsets["Bprev"][:, :], edge_f[:, :]))
                for name, k in (("ew", 1), ("ea4", 4), ("ea8", 8)):
                    step(dve.tensor_scalar(edge_f[:, :], t.start["B"][:, :], -float(EDGE0), float(k), ALU.add, ALU.mult))
                    step(dve.tensor_copy(t.offsets[name][:, :], edge_f[:, :]))


def prepare_tables(nc, t):
    with nc.cleanup_on_exit(), ExitStack() as ctx:
        def sem(name):
            return nc.alloc_semaphore("pt" + "_" + name)

        def sb(name, shape, dt=F32):
            return ctx.enter_context(nc.sbuf_tensor("pt_" + name, shape, dt))

        src_i = {k: sb(f"src_i_{k}", [P, BLOCKS, P], I32) for k in "AB"}
        src_f = {k: sb(f"src_f_{k}", [P, BLOCKS, P]) for k in "AB"}
        width = {"A": P, "B": P + 2}
        dst_i = {k: sb(f"dst_i_{k}", [P, BLOCKS, width[k]], I32) for k in "AB"}
        dst_f = {k: sb(f"dst_f_{k}", [P, BLOCKS, width[k]]) for k in "AB"}
        rel = {k: sb(f"rel_{k}", [P, BLOCKS, P]) for k in "AB"}
        w128 = {k: sb(f"w128_{k}", [P, BLOCKS]) for k in "AB"}
        seg = sb("seg", [P, BLOCKS, P])
        last = sb("last", [P, BLOCKS, P])
        ew = sb("ew", [P, BLOCKS, P])
        ea4 = sb("ea4", [P, 1, P * 4])
        ea8 = sb("ea8", [P, 1, P * 8])
        wrow = {k: sb(f"wrow_{k}", [P, TABLE]) for k in "AB"}
        bank = ctx.enter_context(nc.psum_tensor("pt_bank", [P, 4, 512], F32))

        s_rows = sem("s_rows")
        s_ew = sem("s_ew")
        s_attr = sem("s_attr")
        s_wrow = sem("s_wrow")
        s_dve = sem("s_dve2")
        s_ready = sem("s_ready")
        s_turned = sem("s_turned")
        s_taken = sem("s_taken")
        s_saved = sem("s_saved")

        turns = []
        for k in "AB":
            for b in range(BLOCKS):
                turns.append((rel[k][:, b, :], t.dstrel[k][:, b * P:(b + 1) * P]))
                turns.append((src_f[k][:, b, :], t.src[k][:, b * P:(b + 1) * P]))
        for b in range(BLOCKS):
            turns.append((last[:, b, :], t.lastrel[:, b * P:(b + 1) * P]))
        plain = len(turns)
        a4 = ea4[:, 0, :].rearrange("p (e k) -> p k e", k=4)
        a8 = ea8[:, 0, :].rearrange("p (e k) -> p k e", k=8)
        for b in range(BLOCKS):
            turns += [(a4[:, k, :], t.ea4[:, b * P:(b + 1) * P, k]) for k in range(4)]
            turns += [(a8[:, k, :], t.ea8[:, b * P:(b + 1) * P, k]) for k in range(8)]

        def gather(pool, out, source, name, b):
            return pool.indirect_dma_start(
                out=out, out_offset=None, in_=source.rearrange("(n o) -> n o", o=1),
                in_offset=bass.IndirectOffsetOnAxis(ap=t.offsets[name][:, b:b + 1], axis=0))

        with nc.Block() as block:
            @block.gpsimd
            def _(pool):
                for b in range(BLOCKS):
                    for k in "AB":
                        gather(pool, src_i[k][:, b, :], t.src_all, k, b).then_inc(s_rows, 16)
                        gather(pool, dst_i[k][:, b, :], t.dst_all, "A" if k == "A" else "Bprev", b).then_inc(s_rows, 16)
                    gather(pool, ew[:, b, :], t.ew_all, "ew", b).then_inc(s_ew, 16)
                for b in range(BLOCKS):
                    wait(pool, s_turned, plain + 12 * b if b else 0)
                    gather(pool, ea4[:, 0, :], t.ea4_all, "ea4", b).then_inc(s_attr, 16)
                    gather(pool, ea8[:, 0, :], t.ea8_all, "ea8", b).then_inc(s_attr, 16)

            @block.sync
            def _(sp):
                for k in "AB":
                    sp.dma_start(wrow[k][:, :], t.win_f[k].rearrange("(o n) -> o n", o=1).to_broadcast([P, TABLE])).then_inc(s_wrow, 16)
                    sp.dma_start(t.window_row[k][:, :], t.win_i[k].rearrange("(o n) -> o n", o=1)).then_inc(s_wrow, 16)
                sp.wait_ge(s_wrow, 64)
                sp.wait_ge(s_ew, 16 * BLOCKS)
                sp.dma_start(t.ew_rows.rearrange("(b p) e -> p b e", p=P), ew[:, :, :]).then_inc(s_saved, 16)
                sp.wait_ge(s_ready, 3)
                for k in "AB":
                    sp.dma_start(t.dst_rows[k].rearrange("(b p) e -> p b e", p=P), rel[k][:, :, :]).then_inc(s_saved, 16)
                sp.dma_start(t.seg_rows.rearrange("(b p) e -> p b e", p=P), seg[:, :, :]).then_inc(s_saved, 16)
                sp.wait_ge(s_saved, 64)

            @block.vector
            def _(dve):
                step = Chain(dve, s_dve)
                dve.wait_ge(s_rows, 16 * 4 * BLOCKS)
                for k in "AB":
                    step(dve.tensor_scalar(w128[k][:, :], t.window[k][:, :], float(P), None, ALU.mult))
                    step(dve.tensor_copy(src_f[k][:, :, :], src_i[k][:, :, :]))
                    step(dve.tensor_copy(dst_f[k][:, :, :], dst_i[k][:, :, :]))
                    o = 0 if k == "A" else 1
                    step(dve.tensor_tensor(rel[k][:, :, :], dst_f[k][:, :, o:o + P], bcast_last(w128[k][:, :], P), ALU.subtract))
                    dve.engine_nop().then_inc(s_ready, 1)
                f = dst_f["B"]
                step(dve.tensor_tensor(seg[:, :, :], f[:, :, 1:P + 1], f[:, :, 0:P], ALU.not_equal))
                step(dve.tensor_scalar(seg[:, :, :], seg[:, :, :], -BIG, None, ALU.mult))
                step(dve.tensor_tensor(last[:, :, :], f[:, :, 1:P + 1], f[:, :, 2:P + 2], ALU.is_equal))
                step(dve.scalar_tensor_tensor(out=last[:, :, :].rearrange("p b e -> p (b e)"), in0=last[:, :, :].rearrange("p b e -> p (b e)"),
                                              scalar=float(FAR), in1=rel["B"][:, :, :].rearrange("p b e -> p (b e)"), op0=ALU.mult, op1=ALU.add))
                dve.engine_nop().then_inc(s_ready, 1)
                dve.wait_ge(s_wrow, 64)
                for k in "AB":
                    step(dve.memset(t.same[k][:, 0:1], 0.0))
                    step(dve.tensor_tensor(t.same[k][:, 1:], wrow[k][:, 1:], wrow[k][:, 0:TABLE - 1], ALU.is_equal))
                step(dve.tensor_scalar(t.newwin[:, :], t.same["A"][:, :], -1.0, BIG, ALU.add, ALU.mult))
                for n, (_, out) in enumerate(turns):
                    dve.wait_ge(s_turned, n + 1)
                    dve.tensor_copy(out, bank[:, n % 4, 0:P]).then_inc(s_taken, 1)

            @block.tensor
            def _(pe):
                pe.wait_ge(s_ready, 3)
                for n, (source, _) in enumerate(turns):
                    if n >= 4:
                        pe.wait_ge(s_taken, n - 3)
                    if n >= plain and (n - plain) % 12 == 0:
                        pe.wait_ge(s_attr, 32 * ((n - plain) // 12 + 1))
                    pe.transpose(bank[:, n % 4, 0:P], source, t.ident[:, :]).then_inc(s_turned, 1)


def gather_rows(pool, t, sched, groups, table, width, slots, rows, s_rows_used, used_per_group, s_index, s_gathered, s_tick):
    def index_g(g, q, r):
        wait(pool, s_gathered[q], 16 * GROUP * r)
        pool.sem_inc(s_tick, 1)
        pool.tensor_copy(slots[:, q, :], t.src[sched][:, bass.ds(g * GROUP, GROUP)]).then_inc(s_index, 1)

    def gather_g(g, q, r):
        wait(pool, s_rows_used, (g - UNROLL + 1) * used_per_group)
        wait(pool, s_index, g + 1)
        pool.sem_inc(s_tick, 1)
        for j in range(GROUP):
            pool.indirect_dma_start(out=rows[:, q, j, 0:width], out_offset=None, in_=table,
                                    in_offset=bass.IndirectOffsetOnAxis(ap=slots[:, q, j:j + 1], axis=0)).then_inc(s_gathered[q], 16)
    run_groups(pool, groups, [(0, index_g), (3, gather_g)])


def load_windows(nc, sp, t, sched, g, table, out, sem):
    _, windows = nc.values_load_multi_w_load_instructions(
        t.window_row[sched][0:1, bass.ds(g * GROUP, GROUP)], engines=[mybir.EngineType.SP], min_val=0, max_val=WINDOWS - 1)
    for j in range(GROUP):
        sp.dma_start(out[:, j, :], table.rearrange("(w p) d -> w p d", p=P)[bass.ds(windows[j], 1)]
                     .rearrange("w p d -> p (w d)")).then_inc(sem, 16)


def node_batch(ap, b):
    return ap[b * BATCH * P:(b + 1) * BATCH * P, :].rearrange("(w p) d -> p w d", p=P)


def load_last(nc, sp, t, sched, b, slab, out, sem):
    _, tiles = nc.values_load_multi_w_load_instructions(
        t.last_tile[sched][0:1, b * BATCH:(b + 1) * BATCH], engines=[mybir.EngineType.SP], min_val=0,
        max_val=(TILES_A if sched == "A" else TILES_B) - 1)
    for w in range(BATCH):
        sp.dma_start(out[:, w, :], slab[bass.ds(tiles[w], 1)].rearrange("w p d -> p (w d)")).then_inc(sem, 16)


def row(ap):
    return ap.rearrange("(o n) -> o n", o=1).to_broadcast([P, ap.shape[0]])


def attention_nodes(nc, t, layer, Wl, bl, Wr, br, Wres, bias):
    with nc.cleanup_on_exit(), ExitStack() as ctx:
        def sem(name):
            return nc.alloc_semaphore(f"an{layer}" + "_" + name)

        def sb(name, shape, dt=F32):
            return ctx.enter_context(nc.sbuf_tensor(f"an{layer}_" + name, shape, dt))

        W = sb("W", [P, 3, P])
        WT = sb("WT", [P, 3, P])
        biases = sb("biases", [P, 3, P])
        H = sb("H", [P, 2, BATCH, D])
        acc = sb("acc", [P, 2, BATCH, D + 1])
        res = sb("res", [P, 2, BATCH, D])
        rec = sb("rec", [P, BATCH])
        HT = sb("HT", [P, BATCH, P])
        O = sb("O", [P, 2, BATCH, 3 * D])
        turned = ctx.enter_context(nc.psum_tensor(f"an{layer}_turned", [P, 2, 512], F32))
        prod = ctx.enter_context(nc.psum_tensor(f"an{layer}_prod", [P, 4, 512], F32))

        s_w = sem("s_w")
        s_wturn = sem("s_wturn")
        s_wt = sem("s_wt")
        s_in = [sem(f"s_in{p}") for p in range(2)]
        s_dve = sem("s_dve")
        s_h = sem("s_h")
        s_turn = sem("s_turn")
        s_ht = sem("s_ht")
        s_prod = sem("s_prod")
        s_o = sem("s_o")
        s_out = [sem(f"s_out{p}") for p in range(2)]
        loads = 1 if layer == 0 else BATCH + 1

        with nc.Block() as block:
            @block.sync
            def _(sp):
                for i, m in enumerate((Wl, Wr, Wres)):
                    sp.dma_start(W[:, i, :], m).then_inc(s_w, 16)
                for i, v in enumerate((bl, br, bias)):
                    sp.dma_start(biases[:, i, :], row(v)).then_inc(s_w, 16)

                def load(b):
                    p = b % 2
                    wait(sp, s_turn, b - 1)
                    if layer == 0:
                        sp.dma_start(H[:, p, :, :], node_batch(t.x_pad, b)).then_inc(s_in[p], 16)
                    else:
                        load_last(nc, sp, t, "A", b, t.slab_att[0], acc[:, p], s_in[p])
                        sp.dma_start(res[:, p, :, :], node_batch(t.res[0], b)).then_inc(s_in[p], 16)

                load(0)
                for b in range(NBATCH):
                    if b + 1 < NBATCH:
                        load(b + 1)
                    p = b % 2
                    sp.wait_ge(s_o, (b + 1) * BATCH)
                    for k, table in enumerate((t.xl[layer], t.xr[layer], t.res[layer])):
                        sp.dma_start(node_batch(table, b), O[:, p, :, k * D:(k + 1) * D]).then_inc(s_out[p], 16)
                for p in range(2):
                    sp.wait_ge(s_out[p], 48 * ((NBATCH + 1 - p) // 2))

            @block.vector
            def _(dve):
                step = Chain(dve, s_dve)
                dve.wait_ge(s_wturn, 1)
                dve.tensor_copy(WT[:, :, :].rearrange("k m n -> k (m n)"), prod[:, 0, 0:3 * P]).then_inc(s_wt, 1)
                dve.wait_ge(s_w, 16 * 6)
                for b in range(NBATCH):
                    p = b % 2
                    if layer > 0:
                        dve.wait_ge(s_in[p], 16 * loads * (b // 2 + 1))
                        step(dve.reciprocal(rec[:, :], acc[:, p, :, D]))
                        step(dve.tensor_tensor(H[:, p], acc[:, p, :, 0:D], bcast_last(rec[:, :], D), ALU.mult))
                        step(dve.tensor_tensor(H[:, p], H[:, p], res[:, p], ALU.add))
                        dve.tensor_scalar(H[:, p], H[:, p], 0.0, None, ALU.max).then_inc(s_h, 1)
                    wait(dve, s_out[p], 48 * (b // 2))
                    for w in range(BATCH):
                        n = b * BATCH + w
                        dve.wait_ge(s_prod, n + 1)
                        dve.tensor_tensor(O[:, p, w, :], prod[:, n % 4, 0:3 * P], biases[:, :, :].rearrange("p k c -> p (k c)"),
                                          ALU.add).then_inc(s_o, 1)

            @block.scalar
            def _(act):
                for b in range(NBATCH):
                    act.wait_ge(s_turn, b + 1)
                    wait(act, s_prod, b * BATCH)
                    act.activation(HT[:, 0:4, :], turned[:, 0, :].rearrange("p (w n) -> p w n", w=4), ACT.Copy)
                    act.activation(HT[:, 4:7, :], turned[:, 1, 0:3 * P].rearrange("p (w n) -> p w n", w=3), ACT.Copy).then_inc(s_ht, 1)

            @block.tensor
            def _(pe):
                pe.wait_ge(s_w, 16 * 6)
                for i in range(3):
                    last = pe.transpose(prod[:, 0, i * P:(i + 1) * P], W[:, i, :], t.ident[:, :])
                last.then_inc(s_wturn, 1)
                pe.wait_ge(s_wt, 1)
                for b in range(NBATCH):
                    p = b % 2
                    if layer == 0:
                        pe.wait_ge(s_in[p], 16 * (b // 2 + 1))
                    else:
                        pe.wait_ge(s_h, b + 1)
                    wait(pe, s_ht, b)
                    for w in range(BATCH):
                        last = pe.transpose(turned[:, w // 4, (w % 4) * P:(w % 4 + 1) * P], H[:, p, w, :], t.ident[:, :])
                    last.then_inc(s_turn, 1)
                    pe.wait_ge(s_ht, b + 1)
                    for w in range(BATCH):
                        n = b * BATCH + w
                        wait(pe, s_o, n - 3)
                        pe.matmul(prod[:, n % 4, 0:3 * P], HT[:, w, :], WT[:, :, :].rearrange("k m n -> k (m n)"),
                                  start=True, stop=True).then_inc(s_prod, 1)


def attention_sweep(nc, t, layer, att):
    groups = TILES_A // GROUP
    C = D + 1
    E = GROUP * P
    with nc.cleanup_on_exit(), ExitStack() as ctx:
        def sem(name):
            return nc.alloc_semaphore(f"as{layer}" + "_" + name)

        def sb(name, shape, dt=F32):
            return ctx.enter_context(nc.sbuf_tensor(f"as{layer}_" + name, shape, dt))

        def ps(name, shape):
            return ctx.enter_context(nc.psum_tensor(f"as{layer}_" + name, shape, F32))

        slots = sb("slots", [P, UNROLL, GROUP], I32)
        rows = sb("rows", [P, UNROLL, GROUP, C])
        xr = sb("xr", [P, 4, GROUP, D])
        dst_row = sb("dst_row", [P, 4, E])
        hot_t = sb("hot_t", [P, 4, GROUP, P])
        masked = sb("masked", [P, 2, GROUP, P])
        leaky = sb("leaky", [P, 2, E])
        att_col = sb("att_col", [P, 1])
        att_all = sb("att_all", [P, P])
        tile_max = sb("tile_max", [P, 2, GROUP])
        run_max = sb("run_max", [P, TILES_A + 1])
        minus_max = sb("minus_max", [P, 4, GROUP])
        step_down = sb("step_down", [P, 4, GROUP])
        rescale = sb("rescale", [P, 4, GROUP])
        weight_t = sb("weight_t", [P, 2, GROUP, P])
        weight = sb("weight", [P, 2, GROUP, P])
        acc = sb("acc", [P, 4, GROUP, C])
        z = ps("z", [P, 2, E])
        score = ps("score", [P, 2, GROUP, P])
        turned = ps("turned", [P, 2, GROUP, P])
        total = ps("total", [P, 2, 512])

        s_att = sem("s_att")
        s_init = sem("s_init")
        s_tick = sem("s_tick")
        s_index = sem("s_index")
        s_pace = sem("s_pace")
        s_gathered = [sem(f"s_gathered{q}") for q in range(UNROLL)]
        s_window = [sem(f"s_window{q}") for q in range(4)]
        s_hot = sem("s_hot")
        s_z = sem("s_z")
        s_relu = sem("s_relu")
        s_leaky = sem("s_leaky")
        s_score = sem("s_score")
        s_outside = sem("s_outside")
        s_tmax = sem("s_tmax")
        s_run = sem("s_run")
        s_max = sem("s_max")
        s_exps = sem("s_exps")
        s_turned = sem("s_turned")
        s_weight = sem("s_weight")
        s_total = sem("s_total")
        s_acc = sem("s_acc")
        s_stored = [sem(f"s_stored{q}") for q in range(4)]

        with nc.Block() as block:
            @block.gpsimd
            def _(pool):
                gather_rows(pool, t, "A", groups, t.xl[layer], D, slots, rows, s_total, 1, s_index, s_gathered, s_tick)

            @block.sync
            def _(sp):
                sp.dma_start(att_col[:, :], att.rearrange("(p o) -> p o", o=1)).then_inc(s_att, 16)

                def stage(g, q, r):
                    wait(sp, s_z, g - 3)
                    wait(sp, s_hot, g - 3)
                    load_windows(nc, sp, t, "A", g, t.xr[layer], xr[:, q % 4], s_window[q % 4])
                    sp.dma_start(dst_row[:, q % 4, :], t.dst_rows["A"].rearrange("(g j) e -> g (j e)", j=GROUP)[bass.ds(g, 1)]
                                 .to_broadcast([P, E])).then_inc(s_window[q % 4], 16)
                run_groups(sp, groups, [(0, stage)])
                for q in range(4):
                    sp.wait_ge(s_stored[q], 16 * groups // 4)

            @block.scalar
            def _(act):
                def store(g, q, r):
                    wait(act, s_acc, GROUP * (g + 1))
                    act.dma_start(t.slab_att[layer][bass.ds(g * GROUP, GROUP)].rearrange("j p c -> p j c"), acc[:, q % 4]).then_inc(s_stored[q % 4], 16)

                def relu_g(g, q, r):
                    wait(act, s_z, g + 1)
                    wait(act, s_score, g - 1)
                    act.activation(leaky[:, q % 2, :], z[:, q % 2, :], ACT.Relu, scale=0.8).then_inc(s_relu, 1)

                def outside_t(g, q, r):
                    wait(act, s_hot, g + 1)
                    wait(act, s_exps, g - 1)
                    act.activation(masked[:, q % 2], hot_t[:, q % 4], ACT.Copy, scale=BIG, bias=-BIG).then_inc(s_outside, 1)

                def weight_g(g, q, r):
                    wait(act, s_turned, g + 1)
                    wait(act, s_total, g - 1)
                    act.activation(weight[:, q % 2], turned[:, q % 2], ACT.Copy).then_inc(s_weight, 1)

                def exps_g(g, q, r):
                    wait(act, s_max, g + 1)
                    wait(act, s_turned, g - 1)
                    wait(act, s_acc, GROUP * (g - 3))
                    act.activation(rescale[:, q % 4, :], step_down[:, q % 4, :], ACT.Exp)
                    for j in range(GROUP):
                        last = act.activation(weight_t[:, q % 2, j, :], masked[:, q % 2, j, :], ACT.Exp, bias=minus_max[:, q % 4, j:j + 1])
                    last.then_inc(s_exps, 1)
                run_groups(act, groups, [(2, outside_t), (1, relu_g), (4, weight_g), (3, exps_g), (7, store)])

            @block.tensor
            def _(pe):
                pe.wait_ge(s_init, 2)

                def z_g(g, q, r):
                    wait(pe, s_gathered[q], 16 * GROUP * (r + 1))
                    wait(pe, s_window[q % 4], 16 * (GROUP + 1) * (uses(q, r, 4) + 1))
                    wait(pe, s_hot, g + 1)
                    wait(pe, s_leaky, g - 1)
                    for j in range(GROUP):
                        out = z[:, q % 2, j * P:(j + 1) * P]
                        pe.matmul(out, rows[:, q, j, 0:D], t.ident[:, :], start=True, stop=False, skip_group_check=True)
                        last = pe.matmul(out, xr[:, q % 4, j, :], hot_t[:, q % 4, j, :], start=False, stop=True, skip_group_check=True)
                    last.then_inc(s_z, 1)

                def score_g(g, q, r):
                    wait(pe, s_leaky, g + 1)
                    wait(pe, s_tmax, g - 1)
                    pe.matmul(score[:, q % 2].rearrange("p j e -> p (j e)"), att_all[:, :], leaky[:, q % 2, :],
                              start=True, stop=True).then_inc(s_score, 1)

                def turn_g(g, q, r):
                    wait(pe, s_exps, g + 1)
                    wait(pe, s_weight, g - 1)
                    for j in range(GROUP):
                        last = pe.transpose(turned[:, q % 2, j, :], weight_t[:, q % 2, j, :], t.ident[:, :])
                    last.then_inc(s_turned, 1)

                def total_g(g, q, r):
                    wait(pe, s_weight, g + 1)
                    wait(pe, s_acc, GROUP * g)
                    for j in range(GROUP):
                        last = pe.matmul(total[:, j // 2, (j % 2) * C:(j % 2 + 1) * C], weight[:, q % 2, j, :], rows[:, q, j, :],
                                         start=True, stop=True)
                    last.then_inc(s_total, 1)
                run_groups(pe, groups, [(1, z_g), (4, turn_g), (2, score_g), (5, total_g)])

            @block.vector
            def _(dve):
                dve.memset(rows[:, :, :, D:], 1.0)
                dve.memset(run_max[:, 0:1], -BIG)
                dve.memset(acc[:, 3, GROUP - 1, :], 0.0).then_inc(s_init, 1)
                dve.wait_ge(s_init, 1)
                dve.wait_ge(s_att, 16)
                dve.tensor_copy(att_all[:, :], att_col[:, :].to_broadcast([P, P])).then_inc(s_init, 1)

                def leaky_g(g, q, r):
                    wait(dve, s_relu, g + 1)
                    dve.scalar_tensor_tensor(out=leaky[:, q % 2, :], in0=z[:, q % 2, :], scalar=0.2, in1=leaky[:, q % 2, :],
                                             op0=ALU.mult, op1=ALU.add).then_inc(s_leaky, 1)

                def tile_max_g(g, q, r):
                    wait(dve, s_score, g + 1)
                    wait(dve, s_outside, g + 1)
                    dve.sem_inc(s_pace, 1)
                    for j in range(GROUP):
                        last = dve.tensor_tensor_reduce(masked[:, q % 2, j, :], score[:, q % 2, j, :], masked[:, q % 2, j, :], 1.0, -BIG,
                                                        ALU.add, ALU.max, tile_max[:, q % 2, j:j + 1])
                    last.then_inc(s_tmax, 1)

                def max_g(g, q, r, j):
                    old, new = run_max[:, bass.ds(g * GROUP, GROUP)], run_max[:, bass.ds(g * GROUP + 1, GROUP)]
                    newwin = t.newwin[:, bass.ds(g * GROUP, GROUP)]
                    if j == 0:
                        wait(dve, s_tmax, g + 1)
                        dve.tensor_tensor_scan(new, newwin, tile_max[:, q % 2, :], run_max[:, bass.ds(g * GROUP, 1)],
                                               ALU.add, ALU.max).then_inc(s_run, 1)
                    elif j == 1:
                        wait(dve, s_run, 2 * g + 1)
                        wait(dve, s_exps, g - 3)
                        dve.tensor_scalar(minus_max[:, q % 4, :], new, -1.0, None, ALU.mult)
                        dve.tensor_tensor(step_down[:, q % 4, :], old, newwin, ALU.add).then_inc(s_run, 1)
                    elif j == 2:
                        wait(dve, s_run, 2 * g + 2)
                        dve.tensor_tensor(step_down[:, q % 4, :], step_down[:, q % 4, :], new, ALU.subtract).then_inc(s_max, 1)

                def hot_g(g, q, r):
                    wait(dve, s_window[q % 4], 16 * (GROUP + 1) * (uses(q, r, 4) + 1))
                    wait(dve, s_z, g - 3)
                    wait(dve, s_outside, g - 3)
                    dve.tensor_scalar(hot_t[:, q % 4].rearrange("p j e -> p (j e)"), dst_row[:, q % 4, :], t.iota_p[:, :], None,
                                      ALU.is_equal).then_inc(s_hot, 1)

                def acc_g(g, q, r, j):
                    wait(dve, s_total, g + 1)
                    wait(dve, s_stored[q % 4], 16 * uses(q, r, 4))
                    before = acc[:, q % 4, j - 1, :] if j else acc[:, (q - 1) % 4, GROUP - 1, :]
                    wait(dve, s_acc, g * GROUP + j)
                    dve.scalar_tensor_tensor(out=acc[:, q % 4, j, :], in0=before, scalar=rescale[:, q % 4, j:j + 1],
                                             in1=total[:, j // 2, (j % 2) * C:(j % 2 + 1) * C], op0=ALU.mult, op1=ALU.add).then_inc(s_acc, 1)
                run_groups(dve, groups, [(2, leaky_g), (3, tile_max_g), [(6, acc_g), (3, max_g)], (0, hot_g)])


def normalise(dve, step, y, stats, square, s_var, s_sd, n):
    mean, var, dev, inv, tmp = (stats[:, i, :] for i in range(5))
    step(dve.tensor_reduce(mean, y, AX.X, ALU.add))
    step(dve.tensor_scalar(mean, mean, 1.0 / D, None, ALU.mult))
    step(dve.tensor_tensor(y, y, bcast_last(mean, D), ALU.subtract))
    step(dve.tensor_tensor(square, y, y, ALU.mult))
    step(dve.tensor_reduce(var, square, AX.X, ALU.add))
    dve.tensor_scalar(var, var, 1.0 / D, EPS, ALU.mult, ALU.add).then_inc(s_var, 1)
    dve.wait_ge(s_sd, n)
    inverse_root(dve, step, var, dev, inv, tmp)
    step(dve.tensor_tensor(y, y, bcast_last(inv, D), ALU.mult))


def inverse_root(dve, step, value, root, inv, tmp):
    step(dve.reciprocal(inv, root))
    step(dve.tensor_tensor(tmp, inv, inv, ALU.mult))
    step(dve.tensor_tensor(tmp, tmp, value, ALU.mult))
    step(dve.tensor_scalar(tmp, tmp, -0.5, 1.5, ALU.mult, ALU.add))
    step(dve.tensor_tensor(inv, inv, tmp, ALU.mult))


def turn_batch(pe, t, bank, source):
    for w in range(BATCH):
        last = pe.transpose(bank[:, w // 4, (w % 4) * P:(w % 4 + 1) * P], source[:, w, :], t.ident[:, :])
    return last


def copy_batch(act, out, bank):
    act.activation(out[:, 0:4, :], bank[:, 0, :].rearrange("p (w n) -> p w n", w=4), ACT.Copy)
    return act.activation(out[:, 4:7, :], bank[:, 1, 0:3 * P].rearrange("p (w n) -> p w n", w=3), ACT.Copy)


def max_nodes(nc, t, W1, b1):
    with nc.cleanup_on_exit(), ExitStack() as ctx:
        def sem(name):
            return nc.alloc_semaphore("mn_" + name)

        def sb(name, shape, dt=F32):
            return ctx.enter_context(nc.sbuf_tensor("mn_" + name, shape, dt))

        W = sb("W", [P, 2, P])
        bias = sb("bias", [P, P])
        acc = sb("acc", [P, 2, BATCH, D + 1])
        res = sb("res", [P, 2, BATCH, D])
        x = sb("x", [P, 2, BATCH, D])
        y = sb("y", [P, 2, BATCH, D])
        square = sb("square", [P, BATCH, D])
        rec = sb("rec", [P, BATCH])
        stats = sb("stats", [P, 5, BATCH])
        yT = sb("yT", [P, BATCH, P])
        O = sb("O", [P, 2, BATCH, 2 * D])
        turned = ctx.enter_context(nc.psum_tensor("mn_turned", [P, 2, 512], F32))
        prod = ctx.enter_context(nc.psum_tensor("mn_prod", [P, 4, 512], F32))
        s_w = sem("s_w")
        s_in = [sem(f"s_in{p}") for p in range(2)]
        s_dve = sem("s_dve")
        s_used = sem("s_used")
        s_var = sem("s_var")
        s_sd = sem("s_sd")
        s_y = sem("s_y")
        s_turn = sem("s_turn")
        s_yt = sem("s_yt")
        s_prod = sem("s_prod")
        s_o = sem("s_o")
        s_out = [sem(f"s_out{p}") for p in range(2)]
        s_xout = [sem(f"s_xout{p}") for p in range(2)]

        with nc.Block() as block:
            @block.sync
            def _(sp):
                sp.dma_start(W[:, :, :], W1[0:2 * D, :].rearrange("(k p) n -> p k n", p=P)).then_inc(s_w, 16)
                sp.dma_start(bias[:, :], row(b1)).then_inc(s_w, 16)

                def load(b):
                    p = b % 2
                    wait(sp, s_used, b - 1)
                    load_last(nc, sp, t, "A", b, t.slab_att[1], acc[:, p], s_in[p])
                    sp.dma_start(res[:, p], node_batch(t.res[1], b)).then_inc(s_in[p], 16)
                    sp.dma_start(x[:, p], node_batch(t.x_pad, b)).then_inc(s_in[p], 16)

                load(0)
                for b in range(NBATCH):
                    if b + 1 < NBATCH:
                        load(b + 1)
                    p = b % 2
                    sp.wait_ge(s_y, b + 1)
                    sp.dma_start(node_batch(t.x1, b), y[:, p]).then_inc(s_xout[p], 16)
                    sp.wait_ge(s_o, (b + 1) * BATCH)
                    sp.dma_start(node_batch(t.ha, b), O[:, p, :, 0:D]).then_inc(s_out[p], 16)
                    sp.dma_start(node_batch(t.hb, b), O[:, p, :, D:]).then_inc(s_out[p], 16)
                for p in range(2):
                    n = (NBATCH + 1 - p) // 2
                    sp.wait_ge(s_out[p], 32 * n)
                    sp.wait_ge(s_xout[p], 16 * n)

            @block.vector
            def _(dve):
                step = Chain(dve, s_dve)
                dve.wait_ge(s_w, 32)
                for b in range(NBATCH):
                    p = b % 2
                    dve.wait_ge(s_in[p], 16 * (BATCH + 2) * (b // 2 + 1))
                    step(dve.reciprocal(rec[:, :], acc[:, p, :, D]))
                    wait(dve, s_xout[p], 16 * (b // 2))
                    wait(dve, s_turn, b - 1)
                    step(dve.tensor_tensor(y[:, p], acc[:, p, :, 0:D], bcast_last(rec[:, :], D), ALU.mult))
                    step(dve.tensor_tensor(y[:, p], y[:, p], res[:, p], ALU.add))
                    dve.tensor_tensor(y[:, p], y[:, p], x[:, p], ALU.add).then_inc(s_used, 1)
                    dve.wait_ge(s_used, b + 1)
                    normalise(dve, step, y[:, p], stats, square[:, :, :], s_var, s_sd, b + 1)
                    dve.engine_nop().then_inc(s_y, 1)
                    wait(dve, s_out[p], 32 * (b // 2))
                    for w in range(BATCH):
                        n = b * BATCH + w
                        dve.wait_ge(s_prod, n + 1)
                        dve.tensor_copy(O[:, p, w, 0:D], prod[:, n % 4, 0:D])
                        dve.tensor_tensor(O[:, p, w, D:], prod[:, n % 4, D:2 * D], bias[:, :], ALU.add).then_inc(s_o, 1)

            @block.scalar
            def _(act):
                for b in range(NBATCH):
                    act.wait_ge(s_var, b + 1)
                    act.activation(stats[:, 2, :], stats[:, 1, :], ACT.Sqrt).then_inc(s_sd, 1)
                    act.wait_ge(s_turn, b + 1)
                    wait(act, s_prod, b * BATCH)
                    copy_batch(act, yT, turned).then_inc(s_yt, 1)

            @block.tensor
            def _(pe):
                pe.wait_ge(s_w, 32)
                for b in range(NBATCH):
                    pe.wait_ge(s_y, b + 1)
                    wait(pe, s_yt, b)
                    turn_batch(pe, t, turned, y[:, b % 2]).then_inc(s_turn, 1)
                    pe.wait_ge(s_yt, b + 1)
                    for w in range(BATCH):
                        n = b * BATCH + w
                        wait(pe, s_o, n - 3)
                        pe.matmul(prod[:, n % 4, 0:2 * D], yT[:, w, :], W[:, :, :].rearrange("p k n -> p (k n)"),
                                  start=True, stop=True).then_inc(s_prod, 1)


def max_sweep(nc, t, W1, W2):
    groups = TILES_B // GROUP
    E = GROUP * P
    with nc.cleanup_on_exit(), ExitStack() as ctx:
        def sem(name):
            return nc.alloc_semaphore("ms_" + name)

        def sb(name, shape, dt=F32):
            return ctx.enter_context(nc.sbuf_tensor("ms_" + name, shape, dt))

        def ps(name, shape):
            return ctx.enter_context(nc.psum_tensor("ms_" + name, shape, F32))

        slots = sb("slots", [P, UNROLL, GROUP], I32)
        rows = sb("rows", [P, UNROLL, GROUP, D])
        hb = sb("hb", [P, 4, GROUP, D])
        dst_row = sb("dst_row", [P, 4, E])
        seg_row = sb("seg_row", [P, UNROLL, E])
        ew_row = sb("ew_row", [1, 4, E])
        W1c = sb("W1c", [1, D])
        W2_sb = sb("W2", [P, D])
        hot_t = sb("hot_t", [P, 2, GROUP, P])
        hidden_sb = sb("hidden", [P, 2, E])
        running = sb("running", [P, 2, E])
        edge_major = sb("edge_major", [P, 2, GROUP, P])
        pick = sb("pick", [P, 2, GROUP, P])
        degree = sb("degree", [P, UNROLL, GROUP])
        acc = sb("acc", [P, 4, GROUP, D + 1])
        hidden = ps("hidden_ps", [P, 2, E])
        message = ps("message", [P, 2, E])
        turned = ps("turned", [P, 2, E])
        total = ps("total", [P, 2, GROUP, P])

        s_w = sem("s_w")
        s_init = sem("s_init")
        s_tick = sem("s_tick")
        s_index = sem("s_index")
        s_gathered = [sem(f"s_gathered{q}") for q in range(UNROLL)]
        s_window = [sem(f"s_window{q}") for q in range(4)]
        s_hot = sem("s_hot")
        s_degree = sem("s_degree")
        s_hidden = sem("s_hidden")
        s_relu = sem("s_relu")
        s_message = sem("s_message")
        s_running = sem("s_running")
        s_turned = sem("s_turned")
        s_edge = sem("s_edge")
        s_pick = sem("s_pick")
        s_total = sem("s_total")
        s_acc = sem("s_acc")
        s_summed = sem("s_summed")
        s_stored = [sem(f"s_stored{q}") for q in range(4)]
        LOADS = GROUP + 3

        with nc.Block() as block:
            @block.gpsimd
            def _(pool):
                gather_rows(pool, t, "B", groups, t.ha, D, slots, rows, s_hidden, 1, s_index, s_gathered, s_tick)

            @block.sync
            def _(sp):
                sp.dma_start(W1c[:, :], W1[2 * D:2 * D + 1, :]).then_inc(s_w, 16)
                sp.dma_start(W2_sb[:, :], W2).then_inc(s_w, 16)

                def stage(g, q, r):
                    k = q % 4
                    wait(sp, s_hidden, g - 3)
                    load_windows(nc, sp, t, "B", g, t.hb, hb[:, k], s_window[k])
                run_groups(sp, groups, [(0, stage)])
                for q in range(4):
                    sp.wait_ge(s_stored[q], 16 * groups // 4)

            @block.scalar
            def _(act):
                def store(g, q, r):
                    wait(act, s_acc, GROUP * (g + 1))
                    wait(act, s_summed, g + 1)
                    act.dma_start(t.slab_max[bass.ds(g * GROUP, GROUP)].rearrange("j p c -> p j c"), acc[:, q % 4]).then_inc(s_stored[q % 4], 16)

                def rows_g(g, q, r):
                    k = q % 4
                    wait(act, s_hidden, g - 3)
                    wait(act, s_hot, g - 3)
                    wait(act, s_running, g - 7)
                    for out, table in ((dst_row[:, k], t.dst_rows["B"]), (seg_row[:, q], t.seg_rows)):
                        act.dma_start(out, table.rearrange("(g j) e -> g (j e)", j=GROUP)[bass.ds(g, 1)]
                                      .to_broadcast([P, E])).then_inc(s_window[k], 16)
                    act.dma_start(ew_row[:, k, :], t.ew_rows.rearrange("(g j) e -> g (j e)", j=GROUP)[bass.ds(g, 1)]).then_inc(s_window[k], 16)

                def relu_g(g, q, r):
                    wait(act, s_hidden, g + 1)
                    wait(act, s_message, g - 1)
                    act.activation(hidden_sb[:, q % 2, :], hidden[:, q % 2, :], ACT.Relu).then_inc(s_relu, 1)

                def edge_g(g, q, r):
                    wait(act, s_turned, g + 1)
                    wait(act, s_total, g - 1)
                    act.activation(edge_major[:, q % 2].rearrange("p j e -> p (j e)"), turned[:, q % 2, :], ACT.Copy).then_inc(s_edge, 1)
                run_groups(act, groups, [(0, rows_g), (2, relu_g), (5, edge_g), (8, store)])

            @block.tensor
            def _(pe):
                pe.wait_ge(s_w, 32)

                def message_g(g, q, r):
                    wait(pe, s_relu, g + 1)
                    wait(pe, s_running, g - 1)
                    pe.matmul(message[:, q % 2, :], W2_sb[:, :], hidden_sb[:, q % 2, :], start=True, stop=True).then_inc(s_message, 1)

                def hidden_g(g, q, r):
                    wait(pe, s_gathered[q], 16 * GROUP * (r + 1))
                    wait(pe, s_window[q % 4], 16 * LOADS * (uses(q, r, 4) + 1))
                    wait(pe, s_hot, g + 1)
                    wait(pe, s_relu, g - 1)
                    pe.matmul(hidden[:, q % 2, :], W1c[:, :], ew_row[:, q % 4, :], start=True, stop=False, skip_group_check=True)
                    for j in range(GROUP):
                        out = hidden[:, q % 2, j * P:(j + 1) * P]
                        pe.matmul(out, rows[:, q, j, :], t.ident[:, :], start=False, stop=False, skip_group_check=True)
                        last = pe.matmul(out, hb[:, q % 4, j, :], hot_t[:, q % 2, j, :], start=False, stop=True, skip_group_check=True)
                    last.then_inc(s_hidden, 1)

                def turn_g(g, q, r):
                    wait(pe, s_running, g + 1)
                    wait(pe, s_edge, g - 1)
                    for j in range(GROUP):
                        last = pe.transpose(turned[:, q % 2, j * P:(j + 1) * P], running[:, q % 2, j * P:(j + 1) * P], t.ident[:, :])
                    last.then_inc(s_turned, 1)

                def total_g(g, q, r):
                    wait(pe, s_pick, GROUP * (g + 1))
                    wait(pe, s_edge, g + 1)
                    wait(pe, s_acc, GROUP * (g - 1))
                    for j in range(GROUP):
                        last = pe.matmul(total[:, q % 2, j, :], pick[:, q % 2, j, :], edge_major[:, q % 2, j, :], start=True, stop=True)
                    last.then_inc(s_total, 1)
                run_groups(pe, groups, [(2, hidden_g), (3, message_g), (5, turn_g), (6, total_g)])

            @block.vector
            def _(dve):
                dve.memset(running[:, 1, E - 1:E], 0.0)
                dve.memset(acc[:, 3, GROUP - 1, :], 0.0).then_inc(s_init, 1)
                dve.wait_ge(s_init, 1)

                def hot_g(g, q, r):
                    wait(dve, s_window[q % 4], 16 * LOADS * (uses(q, r, 4) + 1))
                    wait(dve, s_hidden, g - 1)
                    dve.tensor_scalar(hot_t[:, q % 2].rearrange("p j e -> p (j e)"), dst_row[:, q % 4, :], t.iota_p[:, :], None,
                                      ALU.is_equal).then_inc(s_hot, 1)
                    wait(dve, s_hot, g + 1)
                    wait(dve, s_summed, g - 7)
                    dve.tensor_reduce(degree[:, q, :], hot_t[:, q % 2], AX.X, ALU.add).then_inc(s_degree, 1)

                def running_g(g, q, r):
                    wait(dve, s_message, g + 1)
                    wait(dve, s_turned, g - 1)
                    wait(dve, s_running, g)
                    dve.tensor_tensor_scan(running[:, q % 2, :], seg_row[:, q, :], message[:, q % 2, :],
                                           running[:, (q - 1) % 2, E - 1:E], ALU.add, ALU.max).then_inc(s_running, 1)

                def pick_g(g, q, r, j):
                    wait(dve, s_total, g - 1)
                    dve.tensor_scalar(pick[:, q % 2, j, :], t.iota_f[:, :], t.lastrel[:, bass.ds(g * GROUP + j, 1)],
                                      None, ALU.is_equal).then_inc(s_pick, 1)

                def degree_g(g, q, r):
                    wait(dve, s_stored[q % 4], 16 * uses(q, r, 4))
                    wait(dve, s_degree, g + 1)
                    wait(dve, s_summed, g)
                    dve.tensor_tensor_scan(acc[:, q % 4, :, D], t.same["B"][:, bass.ds(g * GROUP, GROUP)], degree[:, q, :],
                                           acc[:, (q - 1) % 4, GROUP - 1, D:], ALU.mult, ALU.add).then_inc(s_summed, 1)

                def acc_g(g, q, r, j):
                    wait(dve, s_total, g + 1)
                    wait(dve, s_stored[q % 4], 16 * uses(q, r, 4))
                    before = acc[:, q % 4, j - 1, 0:D] if j else acc[:, (q - 1) % 4, GROUP - 1, 0:D]
                    wait(dve, s_acc, g * GROUP + j)
                    dve.scalar_tensor_tensor(out=acc[:, q % 4, j, 0:D], in0=before, scalar=t.same["B"][:, bass.ds(g * GROUP + j, 1)],
                                             in1=total[:, q % 2, j, :], op0=ALU.mult, op1=ALU.add).then_inc(s_acc, 1)
                run_groups(dve, groups, [(4, running_g), (7, degree_g), [(5, pick_g), (7, acc_g)], (1, hot_g)])


def update_nodes(nc, t, b2, U1, c1, U2, c2, W1_s, W1_v, Ws_s, Ws_v):
    inv = 1.0 / 32 ** 0.5
    with nc.cleanup_on_exit(), ExitStack() as ctx:
        def sem(name):
            return nc.alloc_semaphore("un_" + name)

        def sb(name, shape, dt=F32):
            return ctx.enter_context(nc.sbuf_tensor("un_" + name, shape, dt))

        U1_sb = sb("U1", [P, 2, D])
        U2_sb = sb("U2", [P, D])
        c1_col = sb("c1_col", [P, 1])
        c2_row = sb("c2_row", [P, D])
        b2_row = sb("b2_row", [P, D])
        WP = sb("WP", [P, 2, D])
        acc = sb("acc", [P, 2, BATCH, D + 1])
        x1 = sb("x1", [P, 2, BATCH, D])
        agg = sb("agg", [P, BATCH, D])
        deg = sb("deg", [P, 4, BATCH])
        has = sb("has", [P, BATCH])
        inT = sb("inT", [P, 2, BATCH, P])
        hidT = sb("hidT", [P, BATCH, P])
        y = sb("y", [P, 2, BATCH, D])
        square = sb("square", [P, BATCH, D])
        stats = sb("stats", [P, 5, BATCH])
        yT = sb("yT", [P, BATCH, P])
        O = sb("O", [P, 2, BATCH, 2 * D])
        left = ctx.enter_context(nc.psum_tensor("un_left", [P, 4, 512], F32))
        right = ctx.enter_context(nc.psum_tensor("un_right", [P, 4, 512], F32))
        s_zero = sem("s_zero")
        s_w = sem("s_w")
        s_scaled = sem("s_scaled")
        s_in = [sem(f"s_in{p}") for p in range(2)]
        s_dve = sem("s_dve")
        s_deg = sem("s_deg")
        s_root = sem("s_root")
        s_agg = sem("s_agg")
        s_turn = sem("s_turn")
        s_int = sem("s_int")
        s_hid = sem("s_hid")
        s_hidt = sem("s_hidt")
        s_upd = sem("s_upd")
        s_used = sem("s_used")
        s_var = sem("s_var")
        s_sd = sem("s_sd")
        s_y = sem("s_y")
        s_turn2 = sem("s_turn2")
        s_yt = sem("s_yt")
        s_prod = sem("s_prod")
        s_o = sem("s_o")
        s_out = [sem(f"s_out{p}") for p in range(2)]
        s_xout = [sem(f"s_xout{p}") for p in range(2)]
        WLOADS = 5 + 8

        with nc.Block() as block:
            @block.gpsimd
            def _(pool):
                pool.memset(WP[:, :, :], 0.0).then_inc(s_zero, 1)

            @block.sync
            def _(sp):
                sp.dma_start(U1_sb[:, :, :], U1.rearrange("(k p) n -> p k n", p=P)).then_inc(s_w, 16)
                sp.dma_start(U2_sb[:, :], U2).then_inc(s_w, 16)
                sp.dma_start(c1_col[:, :], c1.rearrange("(p o) -> p o", o=1)).then_inc(s_w, 16)
                sp.dma_start(c2_row[:, :], row(c2)).then_inc(s_w, 16)
                sp.dma_start(b2_row[:, :], row(b2)).then_inc(s_w, 16)
                sp.wait_ge(s_zero, 1)
                for k, (ws, wv) in enumerate(((W1_s, W1_v), (Ws_s, Ws_v))):
                    sp.dma_start(WP[0:32, k, 0:32], ws).then_inc(s_w, 16)
                    for d in range(3):
                        out = WP[32 + d:P:3, k, 32 + 32 * d:64 + 32 * d] if k == 0 else WP[32 + d:P:3, k, 32 + d:P:3]
                        sp.dma_start(out, wv, allow_slow_non_contiguous=True).then_inc(s_w, 16)

                def load(b):
                    p = b % 2
                    wait(sp, s_used, b - 1)
                    load_last(nc, sp, t, "B", b, t.slab_max, acc[:, p], s_in[p])
                    sp.dma_start(x1[:, p], node_batch(t.x1, b)).then_inc(s_in[p], 16)

                load(0)
                for b in range(NBATCH):
                    if b + 1 < NBATCH:
                        load(b + 1)
                    p = b % 2
                    sp.wait_ge(s_y, b + 1)
                    sp.dma_start(node_batch(t.x2, b), y[:, p]).then_inc(s_xout[p], 16)
                    sp.wait_ge(s_o, (b + 1) * BATCH)
                    sp.dma_start(node_batch(t.sv, b), O[:, p, :, 0:D]).then_inc(s_out[p], 16)
                    sp.dma_start(node_batch(t.skip, b), O[:, p, :, D:]).then_inc(s_out[p], 16)
                for p in range(2):
                    n = (NBATCH + 1 - p) // 2
                    sp.wait_ge(s_out[p], 32 * n)
                    sp.wait_ge(s_xout[p], 16 * n)

            @block.vector
            def _(dve):
                step = Chain(dve, s_dve)
                dve.wait_ge(s_w, 16 * WLOADS)
                dve.tensor_scalar(WP[:, :, :], WP[:, :, :], inv, None, ALU.mult).then_inc(s_scaled, 1)
                dve.wait_ge(s_scaled, 1)
                for b in range(NBATCH):
                    p = b % 2
                    dve.wait_ge(s_in[p], 16 * (BATCH + 1) * (b // 2 + 1))
                    filled = t.filled[:, b * BATCH:(b + 1) * BATCH]
                    step(dve.tensor_tensor(deg[:, 0, :], acc[:, p, :, D], filled, ALU.mult))
                    step(dve.tensor_scalar(has[:, :], deg[:, 0, :], 1.0, None, ALU.min))
                    dve.tensor_scalar(deg[:, 0, :], deg[:, 0, :], 1.0, None, ALU.max).then_inc(s_deg, 1)
                    dve.wait_ge(s_root, b + 1)
                    inverse_root(dve, step, deg[:, 0, :], deg[:, 1, :], deg[:, 2, :], deg[:, 3, :])
                    step(dve.tensor_tensor(t.dinv_sb[:, b * BATCH:(b + 1) * BATCH], deg[:, 2, :], has[:, :], ALU.mult))
                    step(dve.tensor_tensor(agg[:, :, :], acc[:, p, :, 0:D], bcast_mid(b2_row[:, :], BATCH), ALU.add))
                    dve.tensor_tensor(agg[:, :, :], agg[:, :, :], bcast_last(has[:, :], D), ALU.mult).then_inc(s_agg, 1)
                    dve.wait_ge(s_upd, b + 1)
                    wait(dve, s_xout[p], 16 * (b // 2))
                    step(dve.tensor_tensor(y[:, p], x1[:, p], bcast_mid(c2_row[:, :], BATCH), ALU.add))
                    step(dve.tensor_tensor(y[:, p, 0:4, :], y[:, p, 0:4, :], right[:, 2, :].rearrange("p (w n) -> p w n", w=4), ALU.add))
                    dve.tensor_tensor(y[:, p, 4:7, :], y[:, p, 4:7, :], right[:, 3, 0:3 * P].rearrange("p (w n) -> p w n", w=3),
                                      ALU.add).then_inc(s_used, 1)
                    dve.wait_ge(s_used, b + 1)
                    normalise(dve, step, y[:, p], stats, square[:, :, :], s_var, s_sd, b + 1)
                    dve.engine_nop().then_inc(s_y, 1)
                    wait(dve, s_out[p], 32 * (b // 2))
                    for w in range(BATCH):
                        n = b * BATCH + w
                        dve.wait_ge(s_prod, n + 1)
                        dve.tensor_copy(O[:, p, w, :], right[:, n % 2, 0:2 * D]).then_inc(s_o, 1)

            @block.scalar
            def _(act):
                for b in range(NBATCH):
                    act.wait_ge(s_deg, b + 1)
                    act.activation(deg[:, 1, :], deg[:, 0, :], ACT.Sqrt).then_inc(s_root, 1)
                    act.wait_ge(s_turn, b + 1)
                    copy_batch(act, inT[:, 0], left[:, 0:2])
                    copy_batch(act, inT[:, 1], left[:, 2:4]).then_inc(s_int, 1)
                    act.wait_ge(s_hid, b + 1)
                    act.activation(hidT[:, 0:4, :].rearrange("p w n -> p (w n)"), right[:, 0, :], ACT.Relu, bias=c1_col[:, :])
                    act.activation(hidT[:, 4:7, :].rearrange("p w n -> p (w n)"), right[:, 1, 0:3 * P], ACT.Relu,
                                   bias=c1_col[:, :]).then_inc(s_hidt, 1)
                    act.wait_ge(s_var, b + 1)
                    act.activation(stats[:, 2, :], stats[:, 1, :], ACT.Sqrt).then_inc(s_sd, 1)
                    act.wait_ge(s_turn2, b + 1)
                    copy_batch(act, yT, left[:, 0:2]).then_inc(s_yt, 1)

            @block.tensor
            def _(pe):
                pe.wait_ge(s_w, 16 * WLOADS)
                pe.wait_ge(s_scaled, 1)
                for b in range(NBATCH):
                    p = b % 2
                    pe.wait_ge(s_agg, b + 1)
                    wait(pe, s_yt, b)
                    turn_batch(pe, t, left[:, 0:2], x1[:, p])
                    turn_batch(pe, t, left[:, 2:4], agg).then_inc(s_turn, 1)
                    pe.wait_ge(s_int, b + 1)
                    wait(pe, s_o, b * BATCH)
                    for c, n in ((0, 4), (1, 3)):
                        for k in range(2):
                            last = pe.matmul(right[:, c, 0:n * P], U1_sb[:, k, :],
                                             inT[:, k, 4 * c:4 * c + n, :].rearrange("p w n -> p (w n)"), start=(k == 0), stop=(k == 1))
                    last.then_inc(s_hid, 1)
                    pe.wait_ge(s_hidt, b + 1)
                    for w in range(BATCH):
                        last = pe.matmul(right[:, 2 + w // 4, (w % 4) * P:(w % 4 + 1) * P], hidT[:, w, :], U2_sb[:, :], start=True, stop=True)
                    last.then_inc(s_upd, 1)
                    pe.wait_ge(s_y, b + 1)
                    turn_batch(pe, t, left[:, 0:2], y[:, p]).then_inc(s_turn2, 1)
                    pe.wait_ge(s_yt, b + 1)
                    for w in range(BATCH):
                        n = b * BATCH + w
                        wait(pe, s_o, n - 1)
                        pe.matmul(right[:, n % 2, 0:2 * D], yT[:, w, :], WP[:, :, :].rearrange("p k n -> p (k n)"),
                                  start=True, stop=True).then_inc(s_prod, 1)


def equi_sweep(nc, t, mW0, mb0, mW1, mb1, mW2, mb2):
    groups = TILES_B // GROUP
    E = GROUP * P
    M = 2 * D
    U = 32
    HID = 64
    with nc.cleanup_on_exit(), ExitStack() as ctx:
        def sem(name):
            return nc.alloc_semaphore("es_" + name)

        def sb(name, shape, dt=F32):
            return ctx.enter_context(nc.sbuf_tensor("es_" + name, shape, dt))

        def ps(name, shape):
            return ctx.enter_context(nc.psum_tensor("es_" + name, shape, F32))

        slots = sb("slots", [P, UNROLL, GROUP], I32)
        rows = sb("rows", [P, UNROLL, GROUP, D])
        W0 = sb("W0", [GROUP * 8, GROUP, HID])
        W1_sb = sb("W1", [HID, HID])
        W2_sb = sb("W2", [HID + 1, D])
        b0 = sb("b0", [HID, 1])
        b1 = sb("b1", [HID, 1])
        radial = sb("radial", [P, 2, GROUP, 8])
        radial_t = sb("radial_t", [GROUP * 8, 2, P])
        hid0 = sb("hid0", [HID, 2, E])
        hid1 = sb("hid1", [HID + 1, 2, E])
        scaled = sb("scaled", [P, 4, GROUP, D])
        q_s = sb("q_s", [P, 2, GROUP, U])
        dots = sb("dots", [P, 2, GROUP, 3, U])
        dot = sb("dot", [P, 2, GROUP, U])
        pick = sb("pick", [P, 4, GROUP, P])
        msg = sb("msg", [P, 4, GROUP, M])
        acc = sb("acc", [P, 4, GROUP, M])
        radial_ps = ps("radial_ps", [GROUP * 8, 2, 512])
        h0 = ps("h0", [HID, 512])
        h1 = ps("h1", [HID, 512])
        w = ps("w", [P, 2, GROUP, D])
        total = ps("total", [P, GROUP, M])

        s_w = sem("s_w")
        s_zero = sem("s_zero")
        s_init = sem("s_init")
        s_tick = sem("s_tick")
        s_pace = sem("s_pace")
        s_index = sem("s_index")
        s_gathered = [sem(f"s_gathered{q}") for q in range(UNROLL)]
        s_radial = sem("s_radial")
        s_turned = sem("s_turned")
        s_radial_t = sem("s_radial_t")
        s_h0 = sem("s_h0")
        s_hid0 = sem("s_hid0")
        s_h1 = sem("s_h1")
        s_hid1 = sem("s_hid1")
        s_weights = sem("s_weights")
        s_scaled = sem("s_scaled")
        s_pick = sem("s_pick")
        s_q = sem("s_q")
        s_dots = sem("s_dots")
        s_dot = sem("s_dot")
        s_msg = sem("s_msg")
        s_total = sem("s_total")
        s_acc = sem("s_acc")
        s_stored = [sem(f"s_stored{q}") for q in range(4)]

        with nc.Block() as block:
            @block.gpsimd
            def _(pool):
                pool.memset(W0[:, :, :], 0.0).then_inc(s_zero, 1)
                gather_rows(pool, t, "B", groups, t.sv, D, slots, rows, s_msg, 1, s_index, s_gathered, s_tick)

            @block.sync
            def _(sp):
                sp.wait_ge(s_zero, 1)
                for j in range(GROUP):
                    sp.dma_start(W0[8 * j:8 * j + 8, j, :], mW0).then_inc(s_w, 16)
                sp.dma_start(W1_sb[:, :], mW1).then_inc(s_w, 16)
                sp.dma_start(W2_sb[0:HID, :], mW2).then_inc(s_w, 16)
                sp.dma_start(W2_sb[HID:, :], mb2.rearrange("(o n) -> o n", o=1)).then_inc(s_w, 16)
                sp.dma_start(b0[:, :], mb0.rearrange("(p o) -> p o", o=1)).then_inc(s_w, 16)
                sp.dma_start(b1[:, :], mb1.rearrange("(p o) -> p o", o=1)).then_inc(s_w, 16)

                def store(g, q, r):
                    wait(sp, s_acc, GROUP * (g + 1))
                    sp.dma_start(t.slab_equi[bass.ds(g * GROUP, GROUP)].rearrange("j p c -> p j c"), acc[:, q % 4]).then_inc(s_stored[q % 4], 16)
                run_groups(sp, groups, [(0, store)])
                for q in range(4):
                    sp.wait_ge(s_stored[q], 16 * groups // 4)

            @block.scalar
            def _(act):
                act.wait_ge(s_w, 16 * 9)
                act.wait_ge(s_init, 1)

                def radial_g(g, q, r):
                    wait(act, s_turned, g - 1)
                    act.activation(radial[:, q % 2], t.ea8[:, bass.ds(g * GROUP, GROUP), :], ACT.Copy).then_inc(s_radial, 1)

                def radial_t_g(g, q, r):
                    wait(act, s_turned, g + 1)
                    wait(act, s_h0, g - 1)
                    act.activation(radial_t[:, q % 2, :], radial_ps[:, q % 2, 0:P], ACT.Copy).then_inc(s_radial_t, 1)

                def hid0_g(g, q, r):
                    wait(act, s_h0, g + 1)
                    wait(act, s_h1, g - 1)
                    act.activation(hid0[:, q % 2, :], h0[:, :], ACT.Silu, bias=b0[:, :]).then_inc(s_hid0, 1)

                def hid1_g(g, q, r):
                    wait(act, s_h1, g + 1)
                    wait(act, s_weights, g - 1)
                    act.activation(hid1[0:HID, q % 2, :], h1[:, :], ACT.Silu, bias=b1[:, :]).then_inc(s_hid1, 1)

                def scaled_g(g, q, r):
                    wait(act, s_gathered[q], 16 * GROUP * (r + 1))
                    wait(act, s_msg, g - 3)
                    for j in range(GROUP):
                        last = act.activation(scaled[:, q % 4, j, :], rows[:, q, j, :], ACT.Copy,
                                              scale=t.ea4[:, bass.ds(g * GROUP + j, 1), 0])
                    last.then_inc(s_scaled, 1)
                run_groups(act, groups, [(0, radial_g), (2, hid0_g), (1, radial_t_g), (3, hid1_g), (3, scaled_g)])

            @block.tensor
            def _(pe):
                pe.wait_ge(s_w, 16 * 9)
                pe.wait_ge(s_init, 1)

                def turn_g(g, q, r):
                    wait(pe, s_radial, g + 1)
                    wait(pe, s_radial_t, g - 1)
                    pe.transpose(radial_ps[:, q % 2, 0:P], radial[:, q % 2].rearrange("p j k -> p (j k)"), t.ident[:, :]).then_inc(s_turned, 1)

                def h0_g(g, q, r):
                    wait(pe, s_radial_t, g + 1)
                    wait(pe, s_hid0, g)
                    for j in range(GROUP):
                        last = pe.matmul(h0[:, j * P:(j + 1) * P], W0[:, j, :], radial_t[:, q % 2, :], start=True, stop=True)
                    last.then_inc(s_h0, 1)

                def h1_g(g, q, r):
                    wait(pe, s_hid0, g + 1)
                    wait(pe, s_hid1, g)
                    pe.sem_inc(s_pace, 1)
                    pe.matmul(h1[:, :], W1_sb[:, :], hid0[:, q % 2, :], start=True, stop=True).then_inc(s_h1, 1)

                def weights_g(g, q, r):
                    wait(pe, s_hid1, g + 1)
                    wait(pe, s_msg, g - 1)
                    pe.sem_inc(s_pace, 1)
                    for j in range(GROUP):
                        last = pe.matmul(w[:, q % 2, j, :], hid1[:, q % 2, j * P:(j + 1) * P], W2_sb[:, :], start=True, stop=True)
                    last.then_inc(s_weights, 1)

                def total_first(g, q, r):
                    wait(pe, s_pick, GROUP * (g + 1))
                    wait(pe, s_msg, g + 1)
                    wait(pe, s_acc, GROUP * g - 2)
                    for j in (0, 1):
                        last = pe.matmul(total[:, j, :], pick[:, q % 4, j, :], msg[:, q % 4, j, :], start=True, stop=True)
                    last.then_inc(s_total, 1)

                def total_second(g, q, r):
                    wait(pe, s_acc, GROUP * g)
                    for j in (2, 3):
                        last = pe.matmul(total[:, j, :], pick[:, q % 4, j, :], msg[:, q % 4, j, :], start=True, stop=True)
                    last.then_inc(s_total, 1)
                run_groups(pe, groups, [(6, total_second), (0, turn_g), (1, h0_g), (2, h1_g), (3, weights_g), (5, total_first)])

            @block.vector
            def _(dve):
                dve.memset(hid1[HID:, :, :], 1.0)
                dve.memset(acc[:, 3, GROUP - 1, :], 0.0).then_inc(s_init, 1)
                dve.wait_ge(s_init, 1)

                def pick_g(g, q, r, j):
                    wait(dve, s_total, 2 * (g - 3))
                    dve.tensor_scalar(pick[:, q % 4, j, :], t.iota_f[:, :], t.dstrel["B"][:, bass.ds(g * GROUP + j, 1)],
                                      None, ALU.is_equal).then_inc(s_pick, 1)

                def part(g, q, i):
                    return w[:, q % 2, :, i * U:(i + 1) * U]

                def msg_g(g, q, r, j):
                    k = q % 2
                    m = q % 4
                    sh = t.ea4[:, bass.ds(g * GROUP, GROUP), 1:4].unsqueeze(3).to_broadcast([P, GROUP, 3, U])
                    vectors = rows[:, q, :, U:].rearrange("p j (d u) -> p j d u", d=3)
                    if j == 0:
                        wait(dve, s_gathered[q], 16 * GROUP * (r + 1))
                        wait(dve, s_weights, g + 1)
                        wait(dve, s_dot, 2 * (g - 1))
                        dve.tensor_tensor(dots[:, k], vectors, sh, ALU.mult).then_inc(s_dots, 1)
                        dve.tensor_tensor(q_s[:, k], part(g, q, 2), rows[:, q, :, 0:U], ALU.mult).then_inc(s_q, 1)
                    elif j == 1:
                        wait(dve, s_dots, g + 1)
                        dve.tensor_tensor(dot[:, k], dots[:, k, :, 0, :], dots[:, k, :, 1, :], ALU.add).then_inc(s_dot, 1)
                        wait(dve, s_scaled, g + 1)
                        wait(dve, s_total, 2 * (g - 3))
                        dve.tensor_tensor(msg[:, m, :, 0:U], part(g, q, 0), scaled[:, m, :, 0:U], ALU.mult)
                    elif j == 2:
                        wait(dve, s_dot, 2 * g + 1)
                        dve.tensor_tensor(dot[:, k], dot[:, k], dots[:, k, :, 2, :], ALU.add).then_inc(s_dot, 1)
                        wait(dve, s_q, g + 1)
                        dve.tensor_tensor(msg[:, m, :, 2 * U:5 * U].rearrange("p j (d u) -> p j d u", d=3),
                                          q_s[:, k].unsqueeze(2).to_broadcast([P, GROUP, 3, U]), sh, ALU.mult)
                    else:
                        wait(dve, s_dot, 2 * g + 2)
                        dve.tensor_tensor(msg[:, m, :, U:2 * U], part(g, q, 1), dot[:, k], ALU.mult)
                        dve.tensor_tensor(msg[:, m, :, 5 * U:].rearrange("p j (d u) -> p j d u", d=3),
                                          part(g, q, 3).unsqueeze(2).to_broadcast([P, GROUP, 3, U]),
                                          scaled[:, m, :, U:].rearrange("p j (d u) -> p j d u", d=3), ALU.mult).then_inc(s_msg, 1)

                def acc_g(g, q, r, j):
                    wait(dve, s_total, 2 * g + 1 + j // 2)
                    wait(dve, s_stored[q % 4], 16 * uses(q, r, 4))
                    before = acc[:, q % 4, j - 1, :] if j else acc[:, (q - 1) % 4, GROUP - 1, :]
                    wait(dve, s_acc, g * GROUP + j)
                    dve.scalar_tensor_tensor(out=acc[:, q % 4, j, :], in0=before, scalar=t.same["B"][:, bass.ds(g * GROUP + j, 1)],
                                             in1=total[:, j, :], op0=ALU.mult, op1=ALU.add).then_inc(s_acc, 1)
                run_groups(dve, groups, [[(6, acc_g), (4, pick_g), (4, msg_g)]])


def equi_nodes(nc, t, W2_s, W2_v):
    U = 32
    C = D + 1
    SILU_C = 1.6790524
    with nc.cleanup_on_exit(), ExitStack() as ctx:
        def sem(name):
            return nc.alloc_semaphore("en_" + name)

        def sb(name, shape, dt=F32):
            return ctx.enter_context(nc.sbuf_tensor("en_" + name, shape, dt))

        WB = sb("WB", [P, 2, 5 * U])
        acc = sb("acc", [P, 2, BATCH, 2 * D])
        skip = sb("skip", [P, 2, BATCH, D])
        x2 = sb("x2", [P, 2, BATCH, D])
        accT = sb("accT", [P, 2, BATCH, P])
        G = sb("G", [P, BATCH, 5 * U])
        gates = sb("gates", [P, BATCH, 2 * U])
        y = sb("y", [P, 2, BATCH, D])
        square = sb("square", [P, BATCH, D])
        stats = sb("stats", [P, 5, BATCH])
        O = sb("O", [P, 2, BATCH, C])
        turned = ctx.enter_context(nc.psum_tensor("en_turned", [P, 4, 512], F32))
        prod = ctx.enter_context(nc.psum_tensor("en_prod", [P, 4, 512], F32))
        s_zero = sem("s_zero")
        s_w = sem("s_w")
        s_in = [sem(f"s_in{p}") for p in range(2)]
        s_dve = sem("s_dve")
        s_turn = sem("s_turn")
        s_at = sem("s_at")
        s_prod = sem("s_prod")
        s_g = sem("s_g")
        s_gates = sem("s_gates")
        s_used = sem("s_used")
        s_var = sem("s_var")
        s_sd = sem("s_sd")
        s_y = sem("s_y")
        s_o = sem("s_o")
        s_out = [sem(f"s_out{p}") for p in range(2)]
        s_xout = [sem(f"s_xout{p}") for p in range(2)]
        vector_rows = [(0, 2 * U, 0, 0), (0, 3 * U, 0, 1), (1, 0, 0, 2), (1, U, U, 0), (1, 2 * U, U, 1), (1, 3 * U, U, 2)]
        WLOADS = 1 + len(vector_rows)

        with nc.Block() as block:
            @block.gpsimd
            def _(pool):
                pool.memset(WB[:, :, :], 0.0).then_inc(s_zero, 1)

            @block.sync
            def _(sp):
                sp.wait_ge(s_zero, 1)
                sp.dma_start(WB[0:2 * U, 0, 0:2 * U], W2_s).then_inc(s_w, 16)
                for half, row0, source, d in vector_rows:
                    sp.dma_start(WB[row0:row0 + U, half, 2 * U + d::3], W2_v[source:source + U, :],
                                 allow_slow_non_contiguous=True).then_inc(s_w, 16)

                def load(b):
                    p = b % 2
                    wait(sp, s_used, b - 1)
                    wait(sp, s_turn, b - 1)
                    load_last(nc, sp, t, "B", b, t.slab_equi, acc[:, p], s_in[p])
                    sp.dma_start(skip[:, p], node_batch(t.skip, b)).then_inc(s_in[p], 16)
                    sp.dma_start(x2[:, p], node_batch(t.x2, b)).then_inc(s_in[p], 16)

                load(0)
                for b in range(NBATCH):
                    if b + 1 < NBATCH:
                        load(b + 1)
                    p = b % 2
                    sp.wait_ge(s_y, b + 1)
                    sp.dma_start(node_batch(t.x3, b), y[:, p]).then_inc(s_xout[p], 16)
                    sp.wait_ge(s_o, b + 1)
                    sp.dma_start(node_batch(t.xd, b), O[:, p]).then_inc(s_out[p], 16)
                for p in range(2):
                    n = (NBATCH + 1 - p) // 2
                    sp.wait_ge(s_out[p], 16 * n)
                    sp.wait_ge(s_xout[p], 16 * n)

            @block.vector
            def _(dve):
                step = Chain(dve, s_dve)
                dve.wait_ge(s_w, 16 * WLOADS)
                step(dve.tensor_scalar(WB[:, :, :], WB[:, :, :], 1.0 / 32, None, ALU.mult))
                step(dve.tensor_scalar(WB[U:2 * U, 0, :], WB[U:2 * U, 0, :], 1.0 / 3 ** 0.5, None, ALU.mult))
                for b in range(NBATCH):
                    p = b % 2
                    filled = t.filled[:, b * BATCH:(b + 1) * BATCH]
                    dinv = t.dinv_sb[:, b * BATCH:(b + 1) * BATCH]
                    dve.wait_ge(s_in[p], 16 * (BATCH + 2) * (b // 2 + 1))
                    wait(dve, s_gates, b)
                    for c, n in ((0, 3), (3, 3), (6, 1)):
                        dve.wait_ge(s_prod, b * BATCH + c + n)
                        last = dve.tensor_tensor(G[:, c:c + n, :], prod[:, c // 3, 0:n * 5 * U].rearrange("p (w c) -> p w c", w=n),
                                                 bcast_last(filled[:, c:c + n], 5 * U), ALU.mult)
                    last.then_inc(s_g, 1)
                    wait(dve, s_xout[p], 16 * (b // 2))
                    dve.tensor_tensor(y[:, p], x2[:, p], skip[:, p], ALU.add).then_inc(s_used, 1)
                    dve.wait_ge(s_gates, b + 1)
                    step(dve.tensor_scalar(gates[:, :, :], gates[:, :, :], SILU_C, None, ALU.mult))
                    vectors = G[:, :, 2 * U:].rearrange("p w (u d) -> p w u d", d=3)
                    step(dve.tensor_tensor(vectors, vectors, gates[:, :, U:].unsqueeze(3).to_broadcast([P, BATCH, U, 3]), ALU.mult))
                    step(dve.tensor_tensor(y[:, p, :, 0:U], y[:, p, :, 0:U], gates[:, :, 0:U], ALU.add))
                    step(dve.tensor_tensor(y[:, p, :, U:], y[:, p, :, U:], G[:, :, 2 * U:], ALU.add))
                    normalise(dve, step, y[:, p], stats, square[:, :, :], s_var, s_sd, b + 1)
                    dve.engine_nop().then_inc(s_y, 1)
                    wait(dve, s_out[p], 16 * (b // 2))
                    step(dve.tensor_tensor(O[:, p, :, 0:D], y[:, p], bcast_last(dinv, D), ALU.mult))
                    dve.tensor_copy(O[:, p, :, D], dinv).then_inc(s_o, 1)

            @block.scalar
            def _(act):
                for b in range(NBATCH):
                    act.wait_ge(s_turn, b + 1)
                    wait(act, s_prod, b * BATCH)
                    copy_batch(act, accT[:, 0], turned[:, 0:2])
                    copy_batch(act, accT[:, 1], turned[:, 2:4]).then_inc(s_at, 1)
                    act.wait_ge(s_g, b + 1)
                    wait(act, s_used, b)
                    wait(act, s_y, b)
                    act.activation(gates[:, :, :], G[:, :, 0:2 * U], ACT.Silu).then_inc(s_gates, 1)
                    act.wait_ge(s_var, b + 1)
                    act.activation(stats[:, 2, :], stats[:, 1, :], ACT.Sqrt).then_inc(s_sd, 1)

            @block.tensor
            def _(pe):
                pe.wait_ge(s_dve, 2)
                for b in range(NBATCH):
                    p = b % 2
                    pe.wait_ge(s_in[p], 16 * (BATCH + 2) * (b // 2 + 1))
                    wait(pe, s_at, b)
                    turn_batch(pe, t, turned[:, 0:2], acc[:, p, :, 0:D])
                    turn_batch(pe, t, turned[:, 2:4], acc[:, p, :, D:]).then_inc(s_turn, 1)
                    pe.wait_ge(s_at, b + 1)
                    wait(pe, s_g, b)
                    for w in range(BATCH):
                        for k in range(2):
                            last = pe.matmul(prod[:, w // 3, (w % 3) * 5 * U:(w % 3 + 1) * 5 * U], accT[:, k, w, :], WB[:, k, :],
                                             start=(k == 0), stop=(k == 1))
                        last.then_inc(s_prod, 1)


def norm_sweep(nc, t):
    groups = TILES_B // GROUP
    C = D + 1
    with nc.cleanup_on_exit(), ExitStack() as ctx:
        def sem(name):
            return nc.alloc_semaphore("ns_" + name)

        def sb(name, shape, dt=F32):
            return ctx.enter_context(nc.sbuf_tensor("ns_" + name, shape, dt))

        slots = sb("slots", [P, UNROLL, GROUP], I32)
        rows = sb("rows", [P, UNROLL, GROUP, C])
        pick = sb("pick", [P, 2, GROUP, P])
        acc = sb("acc", [P, 4, GROUP, C])
        total = ctx.enter_context(nc.psum_tensor("ns_total", [P, 2, 2, 512], F32))
        s_init = sem("s_init")
        s_tick = sem("s_tick")
        s_index = sem("s_index")
        s_gathered = [sem(f"s_gathered{q}") for q in range(UNROLL)]
        s_pick = sem("s_pick")
        s_total = sem("s_total")
        s_acc = sem("s_acc")
        s_stored = [sem(f"s_stored{q}") for q in range(4)]

        with nc.Block() as block:
            @block.gpsimd
            def _(pool):
                gather_rows(pool, t, "B", groups, t.xd, C, slots, rows, s_total, 1, s_index, s_gathered, s_tick)

            @block.sync
            def _(sp):
                def store(g, q, r):
                    wait(sp, s_acc, GROUP * (g + 1))
                    sp.dma_start(t.slab_norm[bass.ds(g * GROUP, GROUP)].rearrange("j p c -> p j c"), acc[:, q % 4]).then_inc(s_stored[q % 4], 16)
                run_groups(sp, groups, [(0, store)])
                for q in range(4):
                    sp.wait_ge(s_stored[q], 16 * groups // 4)

            @block.tensor
            def _(pe):
                def total_g(g, q, r):
                    wait(pe, s_gathered[q], 16 * GROUP * (r + 1))
                    wait(pe, s_pick, GROUP * (g + 1))
                    wait(pe, s_acc, GROUP * (g - 1))
                    for j in range(GROUP):
                        last = pe.matmul(total[:, q % 2, j // 2, (j % 2) * C:(j % 2 + 1) * C], pick[:, q % 2, j, :], rows[:, q, j, :],
                                         start=True, stop=True)
                    last.then_inc(s_total, 1)
                run_groups(pe, groups, [(1, total_g)])

            @block.vector
            def _(dve):
                dve.memset(acc[:, 3, GROUP - 1, :], 0.0).then_inc(s_init, 1)
                dve.wait_ge(s_init, 1)

                def pick_g(g, q, r, j):
                    wait(dve, s_total, g - 1)
                    dve.tensor_scalar(pick[:, q % 2, j, :], t.iota_f[:, :], t.dstrel["B"][:, bass.ds(g * GROUP + j, 1)],
                                      None, ALU.is_equal).then_inc(s_pick, 1)

                def acc_g(g, q, r, j):
                    wait(dve, s_total, g + 1)
                    wait(dve, s_stored[q % 4], 16 * uses(q, r, 4))
                    before = acc[:, q % 4, j - 1, :] if j else acc[:, (q - 1) % 4, GROUP - 1, :]
                    wait(dve, s_acc, g * GROUP + j)
                    dve.scalar_tensor_tensor(out=acc[:, q % 4, j, :], in0=before, scalar=t.same["B"][:, bass.ds(g * GROUP + j, 1)],
                                             in1=total[:, q % 2, j // 2, (j % 2) * C:(j % 2 + 1) * C], op0=ALU.mult,
                                             op1=ALU.add).then_inc(s_acc, 1)
                run_groups(dve, groups, [[(0, pick_g), (2, acc_g)]])


def norm_nodes(nc, t, W1_w, W1_b, out):
    C = D + 1
    with nc.cleanup_on_exit(), ExitStack() as ctx:
        def sem(name):
            return nc.alloc_semaphore("nn_" + name)

        def sb(name, shape, dt=F32):
            return ctx.enter_context(nc.sbuf_tensor("nn_" + name, shape, dt))

        W = sb("W", [P, P])
        WT = sb("WT", [P, P])
        bias = sb("bias", [P, D])
        acc = sb("acc", [P, 2, BATCH, C])
        x3 = sb("x3", [P, 2, BATCH, D])
        prod_in = sb("prod_in", [P, BATCH, D])
        prod_inT = sb("prod_inT", [P, BATCH, P])
        r = sb("r", [P, BATCH, D])
        coef = sb("coef", [P, BATCH])
        y = sb("y", [P, 2, BATCH, D])
        square = sb("square", [P, BATCH, D])
        stats = sb("stats", [P, 5, BATCH])
        turned = ctx.enter_context(nc.psum_tensor("nn_turned", [P, 2, 512], F32))
        prod = ctx.enter_context(nc.psum_tensor("nn_prod", [P, 2, 512], F32))
        s_w = sem("s_w")
        s_wturn = sem("s_wturn")
        s_in = [sem(f"s_in{p}") for p in range(2)]
        s_dve = sem("s_dve")
        s_wt = sem("s_wt")
        s_pin = sem("s_pin")
        s_turn = sem("s_turn")
        s_pt = sem("s_pt")
        s_prod = sem("s_prod")
        s_used = sem("s_used")
        s_var = sem("s_var")
        s_sd = sem("s_sd")
        s_y = sem("s_y")
        s_out = [sem(f"s_out{p}") for p in range(2)]

        with nc.Block() as block:
            @block.sync
            def _(sp):
                sp.dma_start(W[:, :], W1_w).then_inc(s_w, 16)
                sp.dma_start(bias[:, :], row(W1_b)).then_inc(s_w, 16)

                def load(b):
                    p = b % 2
                    wait(sp, s_used, b - 1)
                    load_last(nc, sp, t, "B", b, t.slab_norm, acc[:, p], s_in[p])
                    sp.dma_start(x3[:, p], node_batch(t.x3, b)).then_inc(s_in[p], 16)

                load(0)
                for b in range(NBATCH):
                    if b + 1 < NBATCH:
                        load(b + 1)
                    p = b % 2
                    sp.wait_ge(s_y, b + 1)
                    if b < NBATCH - 1:
                        sp.dma_start(node_batch(out, b), y[:, p]).then_inc(s_out[p], 16)
                    else:
                        full = NODES // P * P
                        n = BATCH - 1
                        sp.dma_start(out[b * BATCH * P:full, :].rearrange("(w p) d -> p w d", p=P), y[:, p, 0:n, :]).then_inc(s_out[p], 16)
                        sp.dma_start(out[full:NODES, :], y[0:NODES - full, p, n, :]).then_inc(s_out[p], 16)
                sp.wait_ge(s_out[0], 16 * ((NBATCH + 1) // 2 + 1))
                sp.wait_ge(s_out[1], 16 * (NBATCH // 2))

            @block.vector
            def _(dve):
                step = Chain(dve, s_dve)
                dve.wait_ge(s_wturn, 1)
                dve.tensor_copy(WT[:, :], prod[:, 0, 0:P]).then_inc(s_wt, 1)
                dve.wait_ge(s_wt, 1)
                for b in range(NBATCH):
                    p = b % 2
                    windows = slice(b * BATCH, (b + 1) * BATCH)
                    dve.wait_ge(s_in[p], 16 * (BATCH + 1) * (b // 2 + 1))
                    wait(dve, s_turn, b)
                    dve.tensor_tensor(prod_in[:, :, :], acc[:, p, :, 0:D], x3[:, p], ALU.mult).then_inc(s_pin, 1)
                    step(dve.tensor_tensor(coef[:, :], t.dinv_sb[:, windows], t.filled[:, windows], ALU.mult))
                    step(dve.tensor_tensor(r[:, :, :], x3[:, p], bcast_mid(bias[:, :], BATCH), ALU.add))
                    step(dve.tensor_tensor(r[:, :, :], r[:, :, :], acc[:, p, :, D:].to_broadcast([P, BATCH, D]), ALU.mult))
                    dve.wait_ge(s_prod, b + 1)
                    step(dve.tensor_tensor(r[:, 0:4, :], r[:, 0:4, :], prod[:, 0, :].rearrange("p (w n) -> p w n", w=4), ALU.add))
                    step(dve.tensor_tensor(r[:, 4:7, :], r[:, 4:7, :], prod[:, 1, 0:3 * P].rearrange("p (w n) -> p w n", w=3), ALU.add))
                    step(dve.tensor_tensor(r[:, :, :], r[:, :, :], bcast_last(coef[:, :], D), ALU.mult))
                    step(dve.scalar_tensor_tensor(out=r[:, :, :], in0=r[:, :, :], scalar=0.01, in1=r[:, :, :], op0=ALU.mult, op1=ALU.max))
                    wait(dve, s_out[p], 16 * (b // 2))
                    dve.tensor_tensor(y[:, p], x3[:, p], r[:, :, :], ALU.add).then_inc(s_used, 1)
                    dve.wait_ge(s_used, b + 1)
                    normalise(dve, step, y[:, p], stats, square[:, :, :], s_var, s_sd, b + 1)
                    dve.engine_nop().then_inc(s_y, 1)

            @block.scalar
            def _(act):
                for b in range(NBATCH):
                    act.wait_ge(s_turn, b + 1)
                    wait(act, s_prod, b)
                    copy_batch(act, prod_inT, turned).then_inc(s_pt, 1)
                    act.wait_ge(s_var, b + 1)
                    act.activation(stats[:, 2, :], stats[:, 1, :], ACT.Sqrt).then_inc(s_sd, 1)

            @block.tensor
            def _(pe):
                pe.wait_ge(s_w, 32)
                pe.transpose(prod[:, 0, 0:P], W[:, :], t.ident[:, :]).then_inc(s_wturn, 1)
                pe.wait_ge(s_wt, 1)
                for b in range(NBATCH):
                    pe.wait_ge(s_pin, b + 1)
                    wait(pe, s_pt, b)
                    turn_batch(pe, t, turned, prod_in).then_inc(s_turn, 1)
                    pe.wait_ge(s_pt, b + 1)
                    wait(pe, s_used, b)
                    for w in range(BATCH):
                        last = pe.matmul(prod[:, w // 4, (w % 4) * P:(w % 4 + 1) * P], prod_inT[:, w, :], WT[:, :], start=True, stop=True)
                    last.then_inc(s_prod, 1)


def graph_layers(nc, a, out):
    with ExitStack() as ctx:
        t = Store()
        allocate(nc, ctx, t)

        def layer(prefix, names):
            return [a[f"{prefix}_{n}"] for n in names.split()]

        prepare_schedule(nc, t, a["x"], a["src"], a["dst"], a["edge_weight"], a["edge_attr_4"], a["edge_attr_8"])
        prepare_tables(nc, t)
        for i in range(2):
            attention_nodes(nc, t, i, *layer(f"L0_gnn_l{i + 1}", "Wl bl Wr br Wres bias"))
            attention_sweep(nc, t, i, a[f"L0_gnn_l{i + 1}_att"])
        max_nodes(nc, t, *layer("L1_gnn", "W1 b1"))
        max_sweep(nc, t, *layer("L1_gnn", "W1 W2"))
        update_nodes(nc, t, *layer("L1_gnn", "b2 U1 c1 U2 c2"), *layer("L2_gnn", "W1_s W1_v Ws_s Ws_v"))
        equi_sweep(nc, t, *layer("L2_gnn", "mW0 mb0 mW1 mb1 mW2 mb2"))
        equi_nodes(nc, t, *layer("L2_gnn", "W2_s W2_v"))
        norm_sweep(nc, t)
        norm_nodes(nc, t, *layer("L3_gnn", "W1_w W1_b"), out)


_INS = ['x', 'src', 'dst', 'edge_attr_4', 'edge_attr_8', 'edge_weight',
        'L0_gnn_l1_Wl', 'L0_gnn_l1_bl', 'L0_gnn_l1_Wr', 'L0_gnn_l1_br', 'L0_gnn_l1_att', 'L0_gnn_l1_Wres', 'L0_gnn_l1_bias',
        'L0_gnn_l2_Wl', 'L0_gnn_l2_bl', 'L0_gnn_l2_Wr', 'L0_gnn_l2_br', 'L0_gnn_l2_att', 'L0_gnn_l2_Wres', 'L0_gnn_l2_bias',
        'L1_gnn_W1', 'L1_gnn_b1', 'L1_gnn_W2', 'L1_gnn_b2', 'L1_gnn_U1', 'L1_gnn_c1', 'L1_gnn_U2', 'L1_gnn_c2',
        'L2_gnn_W1_s', 'L2_gnn_W1_v', 'L2_gnn_mW0', 'L2_gnn_mb0', 'L2_gnn_mW1', 'L2_gnn_mb1', 'L2_gnn_mW2', 'L2_gnn_mb2',
        'L2_gnn_W2_s', 'L2_gnn_W2_v', 'L2_gnn_Ws_s', 'L2_gnn_Ws_v', 'L3_gnn_W1_w', 'L3_gnn_W1_b']
_OUTS = [((6250, 128), 'float32')]


def kernel(**inputs):
    import numpy as _np
    import concourse.bacc as _bacc
    from concourse import mybir as _mybir
    from concourse.bass_utils import run_bass_kernel_spmd as _run

    nc = _bacc.Bacc("TRN2", target_bir_lowering=False, num_devices=1)
    arrays, args = {}, {}
    for name in _INS:
        a = _np.ascontiguousarray(inputs[name])
        arrays[f"in_{name}_dram"] = a
        args[name] = nc.dram_tensor(f"in_{name}_dram", a.shape, _mybir.dt.from_np(a.dtype), kind="ExternalInput").ap()
    outs = []
    for i, (shape, dtype) in enumerate(_OUTS):
        dt = _mybir.dt.from_np(_np.dtype(dtype))
        outs.append(nc.dram_tensor(f"out_{i}_dram", shape, dt, kind="ExternalOutput").ap())
    graph_layers(nc, args, *outs)
    r = _run(nc, [arrays], core_ids=[0])
    got = tuple(r.results[0][f"out_{i}_dram"] for i in range(len(_OUTS)))
    return got[0]
```

```python
from contextlib import ExitStack

import concourse.bass as bass
from concourse import mybir

P = 128
NODES = 6250
EDGES = 100000
D = 128
WINDOWS = -(-NODES // P)
NPAD = WINDOWS * P
GROUP = 4
UNROLL = 8
STEP = GROUP * UNROLL
BLOCKS = 7
TABLE = BLOCKS * P
TILES_B = -(-(EDGES // P + WINDOWS + 1) // STEP) * STEP
TILES_A = -(-(EDGES // P + 2 * WINDOWS + 1) // STEP) * STEP
TAIL = P * 116
EDGE0 = NPAD
BATCH = 7
NBATCH = WINDOWS // BATCH
COUNT_P = 125
BIG = 1e30
FAR = 1000000
EPS = 1e-5

F32 = mybir.dt.float32
I32 = mybir.dt.int32
BF16 = mybir.dt.bfloat16
ALU = mybir.AluOpType
ACT = mybir.ActivationFunctionType
AX = mybir.AxisListType
assert TILES_A <= TABLE and NBATCH * BATCH == WINDOWS and COUNT_P * 800 == EDGES


def wait(eng, sem, value):
    if isinstance(value, int) and value <= 0:
        return
    eng.wait_ge(sem, value)


def uses(q, r, ring):
    return r * (UNROLL // ring) + q // ring


def run_groups(eng, groups, stages):
    last = max(lag for entry in stages for lag, _ in (entry if isinstance(entry, list) else [entry]))

    def step(place):
        for entry in stages:
            if isinstance(entry, list):
                for j in range(GROUP):
                    for lag, f in entry:
                        if place(lag):
                            f(*place(lag), j)
            elif place(entry[0]):
                entry[1](*place(entry[0]))

    def peeled(g):
        step(lambda lag: (g - lag, (g - lag) % UNROLL, (g - lag) // UNROLL) if 0 <= g - lag < groups else None)

    head = 2 * UNROLL
    for g in range(head):
        peeled(g)
    with eng.Fori(head // UNROLL, groups // UNROLL) as r:
        for q in range(UNROLL):
            step(lambda lag: (r * UNROLL + (q - lag), (q - lag) % UNROLL, r + (q - lag) // UNROLL))
    for g in range(groups, groups + last):
        peeled(g)


def run_batches(stages):
    for step in range(NBATCH + max(lag for lag, _ in stages)):
        for lag, f in stages:
            if 0 <= step - lag < NBATCH:
                f(step - lag)


def split_bf16(dve, step, value, parts, rest):
    step(dve.tensor_copy(parts[0], value))
    step(dve.tensor_tensor(rest, value, parts[0], ALU.subtract))
    step(dve.tensor_copy(parts[1], rest))
    step(dve.tensor_tensor(rest, rest, parts[1], ALU.subtract))
    step(dve.tensor_copy(parts[2], rest))


class Chain:

    def __init__(self, eng, sem, start=0):
        self.eng, self.sem, self.start, self.n = eng, sem, start, 0

    def __call__(self, instruction):
        self.n += 1
        instruction.then_inc(self.sem, 1)
        self.eng.wait_ge(self.sem, self.start + self.n)


def bcast_mid(ap, n):
    return ap.unsqueeze(1).to_broadcast([ap.shape[0], n, ap.shape[1]])


def bcast_last(ap, n):
    return ap.unsqueeze(2).to_broadcast([ap.shape[0], ap.shape[1], n])


class Store:
    pass


def allocate(nc, ctx, t):
    def sb(name, shape, dt=F32):
        return ctx.enter_context(nc.sbuf_tensor(name, shape, dt))

    def dram(name, shape, dt=F32):
        return nc.dram_tensor(name, shape, dt, kind="Internal").ap()

    t.iota_f = sb("iota_f", [P, P])
    t.iota_p = sb("iota_p", [P, 1])
    t.ident = sb("ident", [P, P])
    t.ones = sb("ones", [P, P])
    t.window = {x: sb(f"window_{x}", [P, BLOCKS]) for x in "AB"}
    t.start = {x: sb(f"start_{x}", [P, BLOCKS]) for x in "AB"}
    t.offsets = {n: sb(f"offsets_{n}", [P, BLOCKS], I32) for n in ("A", "B", "Bprev", "ew", "ea4", "ea8")}
    t.last_tile = {x: sb(f"last_tile_{x}", [P, WINDOWS], I32) for x in "AB"}
    t.filled = sb("filled", [P, WINDOWS])
    t.window_row = {x: sb(f"window_row_{x}", [1, TABLE], I32) for x in "AB"}
    t.same = {x: sb(f"same_{x}", [P, TABLE]) for x in "AB"}
    t.newwin = sb("newwin", [P, TABLE])
    t.src = {x: sb(f"src_{x}", [P, TABLE], I32) for x in "AB"}
    t.dstrel = {x: sb(f"dstrel_{x}", [P, TABLE]) for x in "AB"}
    t.lastrel = sb("lastrel", [P, TABLE])
    t.dinv_sb = sb("dinv_sb", [P, WINDOWS])
    t.ea4 = sb("ea4", [P, TABLE, 4])
    t.ea8 = sb("ea8", [P, TABLE, 8])

    t.dst_all = dram("dst_all", [EDGE0 + EDGES + TAIL], I32)
    t.src_all = dram("src_all", [EDGE0 + EDGES + TAIL], I32)
    t.ew_all = dram("ew_all", [EDGES + TAIL])
    t.ea4_all = dram("ea4_all", [(EDGES + TAIL) * 4])
    t.ea8_all = dram("ea8_all", [(EDGES + TAIL) * 8])
    t.x_pad = dram("x_pad", [NPAD, D])
    t.win_f = {x: dram(f"win_f_{x}", [TABLE]) for x in "AB"}
    t.win_i = {x: dram(f"win_i_{x}", [TABLE], I32) for x in "AB"}
    t.dst_rows = {x: dram(f"dst_rows_{x}", [TABLE, P]) for x in "AB"}
    t.seg_rows = dram("seg_rows", [TABLE, P])
    t.ew_rows = dram("ew_rows", [TABLE, 9, P], BF16)
    t.xl = [dram(f"xl{i}", [NPAD, D]) for i in range(2)]
    t.xr = [dram(f"xr{i}", [NPAD, D]) for i in range(2)]
    t.res = [dram(f"res{i}", [NPAD, D]) for i in range(2)]
    t.x1 = dram("x1", [NPAD, D])
    t.ha = dram("ha", [NPAD, D])
    t.hb = dram("hb", [NPAD, D])
    t.x2 = dram("x2", [NPAD, D])
    t.sv = dram("sv", [NPAD, D])
    t.skip = dram("skip", [NPAD, D])
    t.x3 = dram("x3", [NPAD, D])
    t.xd = dram("xd", [NPAD, D + 1])
    t.slab_att = [dram(f"slab_att{i}", [TILES_A, P, D + 1]) for i in range(2)]
    t.slab_max = dram("slab_max", [TILES_B, P, D + 1])
    t.slab_equi = dram("slab_equi", [TILES_B, P, 2 * D])
    t.slab_norm = dram("slab_norm", [TILES_B, P, D + 1])


def prepare_schedule(nc, t, x, src, dst, edge_weight, edge_attr_4, edge_attr_8):
    with nc.cleanup_on_exit(), ExitStack() as ctx:
        def sem(name):
            return nc.alloc_semaphore("ps" + "_" + name)

        def sb(name, shape, dt=F32):
            return ctx.enter_context(nc.sbuf_tensor("ps_" + name, shape, dt))

        iota_fi = sb("iota_fi", [P, P], I32)
        iota_pi = sb("iota_pi", [P, 1], I32)
        self_id = sb("self_id", [P, WINDOWS], I32)
        tile_i = sb("tile_i", [P, BLOCKS], I32)
        zeros = sb("zeros", [P, 8 * TAIL // P])
        zeros_i = sb("zeros_i", [P, TAIL // P], I32)
        far = sb("far", [P, TAIL // P], I32)
        dst_i = sb("dst_i", [COUNT_P, 800], I32)
        dst_w = sb("dst_w", [COUNT_P, 800], I32)
        dst_f = sb("dst_f", [COUNT_P, 800], BF16)
        below_junk = sb("below_junk", [COUNT_P, 800], BF16)
        junk = sb("junk", [P, P])
        below = sb("below", [P, WINDOWS - 1])
        first = sb("first", [P, WINDOWS + 1])
        count = sb("count", [P, WINDOWS])
        rounded = sb("rounded", [P, WINDOWS])
        tiles_i = sb("tiles_i", [P, WINDOWS], I32)
        tiles_s = sb("tiles_s", [P, WINDOWS], I32)
        tiles = sb("tiles", [P, WINDOWS])
        tile0 = {k: sb(f"tile0_{k}", [P, WINDOWS + 1]) for k in "AB"}
        shift = {k: sb(f"shift_{k}", [P, WINDOWS]) for k in "AB"}
        last_f = {k: sb(f"last_f_{k}", [P, WINDOWS]) for k in "AB"}
        tile_f = sb("tile_f", [P, BLOCKS])
        ssum = {k: sb(f"ssum_{k}", [P, BLOCKS]) for k in "AB"}
        isself = sb("isself", [P, BLOCKS])
        pos = sb("pos", [P, BLOCKS])
        gap = sb("gap", [P, BLOCKS])
        edge_f = sb("edge_f", [P, BLOCKS])
        win_i = {k: sb(f"win_i_{k}", [P, BLOCKS], I32) for k in "AB"}
        total = ctx.enter_context(nc.psum_tensor("ps_total", [P, 512], F32))

        s_iota = sem("s_iota")
        s_fill = sem("s_fill")
        s_copy = sem("s_copy")
        s_dst = sem("s_dst")
        s_dve = sem("s_dve")
        s_counted = sem("s_counted")
        s_total = sem("s_total")
        s_windows = sem("s_windows")
        s_lists = sem("s_lists")

        with nc.Block() as block:
            @block.gpsimd
            def _(pool):
                pool.iota(iota_fi[:, :], pattern=[[1, P]], base=0, channel_multiplier=0).then_inc(s_iota, 1)
                pool.iota(iota_pi[:, :], pattern=[[0, 1]], base=0, channel_multiplier=1).then_inc(s_iota, 1)
                pool.iota(tile_i[:, :], pattern=[[P, BLOCKS]], base=0, channel_multiplier=1).then_inc(s_iota, 1)
                pool.iota(self_id[:, :], pattern=[[1, WINDOWS]], base=0, channel_multiplier=WINDOWS).then_inc(s_fill, 1)
                pool.memset(zeros[:, :], 0.0).then_inc(s_fill, 1)
                pool.memset(zeros_i[:, :], 0).then_inc(s_fill, 1)
                pool.memset(far[:, :], FAR).then_inc(s_fill, 1)

            @block.sync
            def _(sp):
                sp.dma_start(dst_i[:, :], dst.rearrange("(p j) -> p j", p=COUNT_P)).then_inc(s_dst, 16)
                sp.dma_start(t.dst_all[EDGE0:EDGE0 + EDGES].rearrange("(p j) -> p j", p=P // 4),
                             dst.rearrange("(p j) -> p j", p=P // 4)).then_inc(s_copy, 16)
                sp.dma_start(t.src_all[EDGE0:EDGE0 + EDGES].rearrange("(p j) -> p j", p=P // 4),
                             src.rearrange("(p j) -> p j", p=P // 4)).then_inc(s_copy, 16)
                sp.dma_start(t.ew_all[0:EDGES].rearrange("(p j) -> p j", p=P // 4),
                             edge_weight.rearrange("(p j) -> p j", p=P // 4)).then_inc(s_copy, 16)
                sp.dma_start(t.ea4_all[0:EDGES * 4].rearrange("(p j) -> p j", p=P // 4),
                             edge_attr_4.rearrange("(p j) k -> p (j k)", p=P // 4)).then_inc(s_copy, 16)
                sp.dma_start(t.ea8_all[0:EDGES * 8].rearrange("(p j) -> p j", p=P // 4),
                             edge_attr_8.rearrange("(p j) k -> p (j k)", p=P // 4)).then_inc(s_copy, 16)
                sp.dma_start(t.x_pad[0:NODES, :], x).then_inc(s_copy, 16)
                sp.wait_ge(s_fill, 4)
                for a in (t.dst_all, t.src_all):
                    sp.dma_start(a[0:NPAD].rearrange("(p j) -> p j", p=P), self_id[:, :]).then_inc(s_copy, 16)
                sp.dma_start(t.dst_all[EDGE0 + EDGES:].rearrange("(p j) -> p j", p=P), far[:, :]).then_inc(s_copy, 16)
                sp.dma_start(t.src_all[EDGE0 + EDGES:].rearrange("(p j) -> p j", p=P), zeros_i[:, :]).then_inc(s_copy, 16)
                for a, k in ((t.ew_all, 1), (t.ea4_all, 4), (t.ea8_all, 8)):
                    sp.dma_start(a[k * EDGES:].rearrange("(p j) -> p j", p=P), zeros[:, 0:k * TAIL // P]).then_inc(s_copy, 16)
                sp.dma_start(t.x_pad[NODES:NPAD, :], zeros[0:NPAD - NODES, 0:D]).then_inc(s_copy, 16)
                sp.wait_ge(s_copy, 16 * 14)
                sp.wait_ge(s_windows, 1)
                for k in "AB":
                    sp.dma_start(t.win_f[k].rearrange("(b p) -> p b", p=P), t.window[k][:, :],
                                 allow_slow_non_contiguous=True).then_inc(s_lists, 16)
                    sp.dma_start(t.win_i[k].rearrange("(b p) -> p b", p=P), win_i[k][:, :],
                                 allow_slow_non_contiguous=True).then_inc(s_lists, 16)
                sp.wait_ge(s_lists, 64)

            @block.tensor
            def _(pe):
                pe.wait_ge(s_counted, 1)
                pe.matmul(total[:, 0:WINDOWS - 1], t.ones[0:COUNT_P, :], below[0:COUNT_P, :],
                          start=True, stop=True).then_inc(s_total, 1)

            @block.vector
            def _(dve):
                step = Chain(dve, s_dve)
                dve.wait_ge(s_iota, 3)
                step(dve.tensor_copy(t.iota_f[:, :], iota_fi[:, :]))
                step(dve.tensor_copy(t.iota_p[:, :], iota_pi[:, :]))
                step(dve.tensor_copy(tile_f[:, :], tile_i[:, :]))
                step(dve.memset(t.ones[:, :], 1.0))
                step(dve.tensor_scalar(t.ident[:, :], t.iota_f[:, :], t.iota_p[:, :], None, ALU.is_equal))
                dve.wait_ge(s_dst, 16)
                step(dve.tensor_scalar(dst_w[:, :], dst_i[:, :], 7, None, ALU.logical_shift_right))
                step(dve.tensor_copy(dst_f[:, :], dst_w[:, :]))
                for w in range(1, WINDOWS):
                    step(dve.tensor_scalar(below_junk[:, :], dst_f[:, :], float(w), 0.0, ALU.is_lt, ALU.add,
                                           accum_out=below[0:COUNT_P, w - 1:w]))
                dve.engine_nop().then_inc(s_counted, 1)
                dve.wait_ge(s_total, 1)
                step(dve.memset(first[:, 0:1], 0.0))
                step(dve.tensor_copy(first[:, 1:WINDOWS], total[:, 0:WINDOWS - 1]))
                step(dve.memset(first[:, WINDOWS:], float(EDGES)))
                step(dve.tensor_tensor(count[:, :], first[:, 1:], first[:, 0:WINDOWS], ALU.subtract))
                step(dve.tensor_scalar(rounded[:, :], count[:, :], float(P - 1), None, ALU.add))
                step(dve.tensor_copy(tiles_i[:, :], rounded[:, :]))
                step(dve.tensor_scalar(tiles_s[:, :], tiles_i[:, :], 7, None, ALU.logical_shift_right))
                step(dve.tensor_copy(tiles[:, :], tiles_s[:, :]))
                step(dve.tensor_scalar(t.filled[:, :], tiles[:, :], 1.0, None, ALU.min))
                step(dve.memset(tile0["B"][:, 0:1], 0.0))
                step(dve.tensor_tensor_scan(tile0["B"][:, 1:], t.ones[:, 0:WINDOWS], tiles[:, :], 0.0, ALU.mult, ALU.add))
                step(dve.tensor_tensor(tile0["A"][:, :], tile0["B"][:, :], t.iota_f[:, 0:WINDOWS + 1], ALU.add))
                step(dve.scalar_tensor_tensor(out=shift["B"][:, :], in0=tiles[:, :], scalar=-float(P), in1=count[:, :],
                                              op0=ALU.mult, op1=ALU.add))
                step(dve.tensor_scalar(shift["A"][:, :], shift["B"][:, :], -float(P), None, ALU.add))
                step(dve.tensor_scalar(shift["A"][:, WINDOWS - 1:], shift["A"][:, WINDOWS - 1:], float(P), None, ALU.add))
                for k in "AB":
                    step(dve.tensor_scalar(last_f[k][:, :], tile0[k][:, 1:], -1.0, 0.0, ALU.add, ALU.max))
                    step(dve.tensor_copy(t.last_tile[k][:, :], last_f[k][:, :]))
                    for b in range(BLOCKS):
                        tile = tile_f[:, b:b + 1]
                        step(dve.tensor_scalar(junk[:, 0:WINDOWS - 1], tile0[k][:, 1:WINDOWS], tile, 0.0, ALU.is_le, ALU.add,
                                               accum_out=t.window[k][:, b:b + 1]))
                        step(dve.scalar_tensor_tensor(out=junk[:, 0:WINDOWS], in0=tile0[k][:, 1:], scalar=tile, in1=shift[k][:, :],
                                                      op0=ALU.is_le, op1=ALU.mult, accum_out=ssum[k][:, b:b + 1]))
                        if k == "A":
                            step(dve.tensor_scalar(junk[:, 0:WINDOWS], tile0["A"][:, 0:WINDOWS], tile, 0.0, ALU.is_equal, ALU.add,
                                                   accum_out=isself[:, b:b + 1]))
                    step(dve.tensor_copy(win_i[k][:, :], t.window[k][:, :]))
                    step(dve.scalar_tensor_tensor(out=pos[:, :], in0=tile_f[:, :], scalar=float(P), in1=ssum[k][:, :],
                                                  op0=ALU.mult, op1=ALU.add))
                    if k == "B":
                        step(dve.tensor_scalar(t.start["B"][:, :], pos[:, :], float(EDGE0), None, ALU.add))
                    else:
                        step(dve.tensor_scalar(t.start["A"][:, :], pos[:, :], float(EDGE0 - P), None, ALU.add))
                        step(dve.scalar_tensor_tensor(out=gap[:, :], in0=t.window["A"][:, :], scalar=float(P), in1=t.start["A"][:, :],
                                                      op0=ALU.mult, op1=ALU.subtract))
                        step(dve.tensor_tensor(gap[:, :], gap[:, :], isself[:, :], ALU.mult))
                        step(dve.tensor_tensor(t.start["A"][:, :], t.start["A"][:, :], gap[:, :], ALU.add))
                    step(dve.tensor_copy(t.offsets[k][:, :], t.start[k][:, :]))
                dve.engine_nop().then_inc(s_windows, 1)
                step(dve.tensor_scalar(edge_f[:, :], t.start["B"][:, :], -1.0, None, ALU.add))
                step(dve.tensor_copy(t.offsets["Bprev"][:, :], edge_f[:, :]))
                for name, k in (("ew", 1), ("ea4", 4), ("ea8", 8)):
                    step(dve.tensor_scalar(edge_f[:, :], t.start["B"][:, :], -float(EDGE0), float(k), ALU.add, ALU.mult))
                    step(dve.tensor_copy(t.offsets[name][:, :], edge_f[:, :]))


def prepare_tables(nc, t):
    with nc.cleanup_on_exit(), ExitStack() as ctx:
        def sem(name):
            return nc.alloc_semaphore("pt" + "_" + name)

        def sb(name, shape, dt=F32):
            return ctx.enter_context(nc.sbuf_tensor("pt_" + name, shape, dt))

        src_i = {k: sb(f"src_i_{k}", [P, BLOCKS, P], I32) for k in "AB"}
        src_f = {k: sb(f"src_f_{k}", [P, BLOCKS, P]) for k in "AB"}
        width = {"A": P, "B": P + 2}
        dst_i = {k: sb(f"dst_i_{k}", [P, BLOCKS, width[k]], I32) for k in "AB"}
        dst_f = {k: sb(f"dst_f_{k}", [P, BLOCKS, width[k]]) for k in "AB"}
        rel = {k: sb(f"rel_{k}", [P, BLOCKS, P]) for k in "AB"}
        w128 = {k: sb(f"w128_{k}", [P, BLOCKS]) for k in "AB"}
        seg = sb("seg", [P, BLOCKS, P])
        last = sb("last", [P, BLOCKS, P])
        ew = sb("ew", [P, BLOCKS, P])
        ew_parts = sb("ew_parts", [P, 3, BLOCKS, P], BF16)
        ew_rest = sb("ew_rest", [P, BLOCKS, P])
        ea4 = sb("ea4", [P, 1, P * 4])
        ea8 = sb("ea8", [P, 1, P * 8])
        wrow = {k: sb(f"wrow_{k}", [P, TABLE]) for k in "AB"}
        bank = ctx.enter_context(nc.psum_tensor("pt_bank", [P, 4, 512], F32))

        s_rows = sem("s_rows")
        s_ew = sem("s_ew")
        s_split = sem("s_split")
        s_attr = sem("s_attr")
        s_wrow = sem("s_wrow")
        s_dve = sem("s_dve2")
        s_ready = sem("s_ready")
        s_turned = sem("s_turned")
        s_taken = sem("s_taken")
        s_saved = sem("s_saved")

        turns = []
        for k in "AB":
            for b in range(BLOCKS):
                turns.append((rel[k][:, b, :], t.dstrel[k][:, b * P:(b + 1) * P]))
                turns.append((src_f[k][:, b, :], t.src[k][:, b * P:(b + 1) * P]))
        for b in range(BLOCKS):
            turns.append((last[:, b, :], t.lastrel[:, b * P:(b + 1) * P]))
        plain = len(turns)
        a4 = ea4[:, 0, :].rearrange("p (e k) -> p k e", k=4)
        a8 = ea8[:, 0, :].rearrange("p (e k) -> p k e", k=8)
        for b in range(BLOCKS):
            turns += [(a4[:, k, :], t.ea4[:, b * P:(b + 1) * P, k]) for k in range(4)]
            turns += [(a8[:, k, :], t.ea8[:, b * P:(b + 1) * P, k]) for k in range(8)]

        def gather(pool, out, source, name, b):
            return pool.indirect_dma_start(
                out=out, out_offset=None, in_=source.rearrange("(n o) -> n o", o=1),
                in_offset=bass.IndirectOffsetOnAxis(ap=t.offsets[name][:, b:b + 1], axis=0))

        with nc.Block() as block:
            @block.gpsimd
            def _(pool):
                for b in range(BLOCKS):
                    for k in "AB":
                        gather(pool, src_i[k][:, b, :], t.src_all, k, b).then_inc(s_rows, 16)
                        gather(pool, dst_i[k][:, b, :], t.dst_all, "A" if k == "A" else "Bprev", b).then_inc(s_rows, 16)
                    gather(pool, ew[:, b, :], t.ew_all, "ew", b).then_inc(s_ew, 16)
                for b in range(BLOCKS):
                    wait(pool, s_turned, plain + 12 * b if b else 0)
                    gather(pool, ea4[:, 0, :], t.ea4_all, "ea4", b).then_inc(s_attr, 16)
                    gather(pool, ea8[:, 0, :], t.ea8_all, "ea8", b).then_inc(s_attr, 16)

            @block.sync
            def _(sp):
                for k in "AB":
                    sp.dma_start(wrow[k][:, :], t.win_f[k].rearrange("(o n) -> o n", o=1).to_broadcast([P, TABLE])).then_inc(s_wrow, 16)
                    sp.dma_start(t.window_row[k][:, :], t.win_i[k].rearrange("(o n) -> o n", o=1)).then_inc(s_wrow, 16)
                sp.wait_ge(s_wrow, 64)
                sp.wait_ge(s_split, 1)
                for i in range(3):
                    for k in range(3):
                        sp.dma_start(t.ew_rows[:, 3 * i + k, :].rearrange("(b p) e -> p b e", p=P), ew_parts[:, i]).then_inc(s_saved, 16)
                sp.wait_ge(s_ready, 3)
                for k in "AB":
                    sp.dma_start(t.dst_rows[k].rearrange("(b p) e -> p b e", p=P), rel[k][:, :, :]).then_inc(s_saved, 16)
                sp.dma_start(t.seg_rows.rearrange("(b p) e -> p b e", p=P), seg[:, :, :]).then_inc(s_saved, 16)
                sp.wait_ge(s_saved, 16 * 12)

            @block.vector
            def _(dve):
                step = Chain(dve, s_dve)
                dve.wait_ge(s_rows, 16 * 4 * BLOCKS)
                for k in "AB":
                    step(dve.tensor_scalar(w128[k][:, :], t.window[k][:, :], float(P), None, ALU.mult))
                    step(dve.tensor_copy(src_f[k][:, :, :], src_i[k][:, :, :]))
                    step(dve.tensor_copy(dst_f[k][:, :, :], dst_i[k][:, :, :]))
                    o = 0 if k == "A" else 1
                    step(dve.tensor_tensor(rel[k][:, :, :], dst_f[k][:, :, o:o + P], bcast_last(w128[k][:, :], P), ALU.subtract))
                    dve.engine_nop().then_inc(s_ready, 1)
                f = dst_f["B"]
                step(dve.tensor_tensor(seg[:, :, :], f[:, :, 1:P + 1], f[:, :, 0:P], ALU.not_equal))
                step(dve.tensor_scalar(seg[:, :, :], seg[:, :, :], -BIG, None, ALU.mult))
                step(dve.tensor_tensor(last[:, :, :], f[:, :, 1:P + 1], f[:, :, 2:P + 2], ALU.is_equal))
                step(dve.scalar_tensor_tensor(out=last[:, :, :].rearrange("p b e -> p (b e)"), in0=last[:, :, :].rearrange("p b e -> p (b e)"),
                                              scalar=float(FAR), in1=rel["B"][:, :, :].rearrange("p b e -> p (b e)"), op0=ALU.mult, op1=ALU.add))
                dve.engine_nop().then_inc(s_ready, 1)
                dve.wait_ge(s_ew, 16 * BLOCKS)
                split_bf16(dve, step, ew[:, :, :], [ew_parts[:, i] for i in range(3)], ew_rest[:, :, :])
                dve.engine_nop().then_inc(s_split, 1)
                dve.wait_ge(s_wrow, 64)
                for k in "AB":
                    step(dve.memset(t.same[k][:, 0:1], 0.0))
                    step(dve.tensor_tensor(t.same[k][:, 1:], wrow[k][:, 1:], wrow[k][:, 0:TABLE - 1], ALU.is_equal))
                step(dve.tensor_scalar(t.newwin[:, :], t.same["A"][:, :], -1.0, BIG, ALU.add, ALU.mult))
                for n, (_, out) in enumerate(turns):
                    dve.wait_ge(s_turned, n + 1)
                    dve.tensor_copy(out, bank[:, n % 4, 0:P]).then_inc(s_taken, 1)

            @block.tensor
            def _(pe):
                pe.wait_ge(s_ready, 3)
                for n, (source, _) in enumerate(turns):
                    if n >= 4:
                        pe.wait_ge(s_taken, n - 3)
                    if n >= plain and (n - plain) % 12 == 0:
                        pe.wait_ge(s_attr, 32 * ((n - plain) // 12 + 1))
                    pe.transpose(bank[:, n % 4, 0:P], source, t.ident[:, :]).then_inc(s_turned, 1)


def gather_rows(pool, t, sched, groups, table, width, slots, rows, s_rows_used, used_per_group, s_index, s_gathered, s_tick):
    def index_g(g, q, r):
        wait(pool, s_gathered[q], 16 * GROUP * r)
        pool.sem_inc(s_tick, 1)
        pool.tensor_copy(slots[:, q, :], t.src[sched][:, bass.ds(g * GROUP, GROUP)]).then_inc(s_index, 1)

    def gather_g(g, q, r):
        wait(pool, s_rows_used, (g - UNROLL + 1) * used_per_group)
        wait(pool, s_index, g + 1)
        pool.sem_inc(s_tick, 1)
        for j in range(GROUP):
            pool.indirect_dma_start(out=rows[:, q, j, 0:width], out_offset=None, in_=table,
                                    in_offset=bass.IndirectOffsetOnAxis(ap=slots[:, q, j:j + 1], axis=0)).then_inc(s_gathered[q], 16)
    run_groups(pool, groups, [(0, index_g), (3, gather_g)])


def load_windows(nc, sp, t, sched, g, table, out, sem):
    _, windows = nc.values_load_multi_w_load_instructions(
        t.window_row[sched][0:1, bass.ds(g * GROUP, GROUP)], engines=[mybir.EngineType.SP], min_val=0, max_val=WINDOWS - 1)
    for j in range(GROUP):
        sp.dma_start(out[:, j, :], table.rearrange("(w p) d -> w p d", p=P)[bass.ds(windows[j], 1)]
                     .rearrange("w p d -> p (w d)")).then_inc(sem, 16)


def node_batch(ap, b):
    return ap[b * BATCH * P:(b + 1) * BATCH * P, :].rearrange("(w p) d -> p w d", p=P)


def load_last(nc, sp, t, sched, b, slab, out, sem):
    _, tiles = nc.values_load_multi_w_load_instructions(
        t.last_tile[sched][0:1, b * BATCH:(b + 1) * BATCH], engines=[mybir.EngineType.SP], min_val=0,
        max_val=(TILES_A if sched == "A" else TILES_B) - 1)
    for w in range(BATCH):
        sp.dma_start(out[:, w, :], slab[bass.ds(tiles[w], 1)].rearrange("w p d -> p (w d)")).then_inc(sem, 16)


def row(ap):
    return ap.rearrange("(o n) -> o n", o=1).to_broadcast([P, ap.shape[0]])


def attention_nodes(nc, t, layer, Wl, bl, Wr, br, Wres, bias):
    with nc.cleanup_on_exit(), ExitStack() as ctx:
        def sem(name):
            return nc.alloc_semaphore(f"an{layer}" + "_" + name)

        def sb(name, shape, dt=F32):
            return ctx.enter_context(nc.sbuf_tensor(f"an{layer}_" + name, shape, dt))

        W = sb("W", [P, 3, P])
        WT = sb("WT", [P, 3, P])
        biases = sb("biases", [P, 3, P])
        H = sb("H", [P, 2, BATCH, D])
        acc = sb("acc", [P, 2, BATCH, D + 1])
        res = sb("res", [P, 2, BATCH, D])
        rec = sb("rec", [P, BATCH])
        HT = sb("HT", [P, BATCH, P])
        O = sb("O", [P, 2, BATCH, 3 * D])
        turned = ctx.enter_context(nc.psum_tensor(f"an{layer}_turned", [P, 2, 512], F32))
        prod = ctx.enter_context(nc.psum_tensor(f"an{layer}_prod", [P, 4, 512], F32))

        s_w = sem("s_w")
        s_wturn = sem("s_wturn")
        s_wt = sem("s_wt")
        s_in = [sem(f"s_in{p}") for p in range(2)]
        s_dve = sem("s_dve")
        s_h = sem("s_h")
        s_turn = sem("s_turn")
        s_ht = sem("s_ht")
        s_prod = sem("s_prod")
        s_o = sem("s_o")
        s_out = [sem(f"s_out{p}") for p in range(2)]
        loads = 1 if layer == 0 else BATCH + 1

        with nc.Block() as block:
            @block.sync
            def _(sp):
                for i, m in enumerate((Wl, Wr, Wres)):
                    sp.dma_start(W[:, i, :], m).then_inc(s_w, 16)
                for i, v in enumerate((bl, br, bias)):
                    sp.dma_start(biases[:, i, :], row(v)).then_inc(s_w, 16)

                def load(b):
                    p = b % 2
                    wait(sp, s_turn, b - 1)
                    if layer == 0:
                        sp.dma_start(H[:, p, :, :], node_batch(t.x_pad, b)).then_inc(s_in[p], 16)
                    else:
                        load_last(nc, sp, t, "A", b, t.slab_att[0], acc[:, p], s_in[p])
                        sp.dma_start(res[:, p, :, :], node_batch(t.res[0], b)).then_inc(s_in[p], 16)

                load(0)
                load(1)
                for b in range(NBATCH):
                    if b + 2 < NBATCH:
                        load(b + 2)
                for p in range(2):
                    sp.wait_ge(s_out[p], 48 * ((NBATCH + 1 - p) // 2))

            @block.vector
            def _(dve):
                step = Chain(dve, s_dve)
                dve.wait_ge(s_wturn, 1)
                dve.tensor_copy(WT[:, :, :].rearrange("k m n -> k (m n)"), prod[:, 0, 0:3 * P]).then_inc(s_wt, 1)
                dve.wait_ge(s_w, 16 * 6)

                def inputs(b):
                    p = b % 2
                    if layer > 0:
                        wait(dve, s_turn, b - 1)
                        dve.wait_ge(s_in[p], 16 * loads * (b // 2 + 1))
                        step(dve.reciprocal(rec[:, :], acc[:, p, :, D]))
                        step(dve.tensor_tensor(H[:, p], acc[:, p, :, 0:D], bcast_last(rec[:, :], D), ALU.mult))
                        step(dve.tensor_tensor(H[:, p], H[:, p], res[:, p], ALU.add))
                        dve.tensor_scalar(H[:, p], H[:, p], 0.0, None, ALU.max).then_inc(s_h, 1)

                def products(b):
                    p = b % 2
                    wait(dve, s_out[p], 48 * (b // 2))
                    for w in range(BATCH):
                        n = b * BATCH + w
                        dve.wait_ge(s_prod, n + 1)
                        dve.tensor_tensor(O[:, p, w, :], prod[:, n % 4, 0:3 * P], biases[:, :, :].rearrange("p k c -> p (k c)"),
                                          ALU.add).then_inc(s_o, 1)
                run_batches([(0, inputs), (1, products)])

            @block.scalar
            def _(act):
                def copies(b):
                    act.wait_ge(s_turn, b + 1)
                    wait(act, s_prod, b * BATCH)
                    copy_batch(act, HT, turned).then_inc(s_ht, 1)

                def store(b):
                    act.wait_ge(s_o, (b + 1) * BATCH)
                    for k, table in enumerate((t.xl[layer], t.xr[layer], t.res[layer])):
                        act.dma_start(node_batch(table, b), O[:, b % 2, :, k * D:(k + 1) * D]).then_inc(s_out[b % 2], 16)
                run_batches([(0, copies), (1, store)])

            @block.tensor
            def _(pe):
                pe.wait_ge(s_w, 16 * 6)
                for i in range(3):
                    last = pe.transpose(prod[:, 0, i * P:(i + 1) * P], W[:, i, :], t.ident[:, :])
                last.then_inc(s_wturn, 1)
                pe.wait_ge(s_wt, 1)
                for b in range(NBATCH):
                    p = b % 2
                    if layer == 0:
                        pe.wait_ge(s_in[p], 16 * (b // 2 + 1))
                    else:
                        pe.wait_ge(s_h, b + 1)
                    wait(pe, s_ht, b)
                    for w in range(BATCH):
                        last = pe.transpose(turned[:, w // 4, (w % 4) * P:(w % 4 + 1) * P], H[:, p, w, :], t.ident[:, :])
                    last.then_inc(s_turn, 1)
                    pe.wait_ge(s_ht, b + 1)
                    for w in range(BATCH):
                        n = b * BATCH + w
                        wait(pe, s_o, n - 3)
                        pe.matmul(prod[:, n % 4, 0:3 * P], HT[:, w, :], WT[:, :, :].rearrange("k m n -> k (m n)"),
                                  start=True, stop=True).then_inc(s_prod, 1)


def attention_sweep(nc, t, layer, att):
    groups = TILES_A // GROUP
    C = D + 1
    E = GROUP * P
    with nc.cleanup_on_exit(), ExitStack() as ctx:
        def sem(name):
            return nc.alloc_semaphore(f"as{layer}" + "_" + name)

        def sb(name, shape, dt=F32):
            return ctx.enter_context(nc.sbuf_tensor(f"as{layer}_" + name, shape, dt))

        def ps(name, shape):
            return ctx.enter_context(nc.psum_tensor(f"as{layer}_" + name, shape, F32))

        slots = sb("slots", [P, UNROLL, GROUP], I32)
        rows = sb("rows", [P, UNROLL, GROUP, C])
        xr = sb("xr", [P, 4, GROUP, D])
        dst_row = sb("dst_row", [P, 4, E])
        hot_t = sb("hot_t", [P, 4, GROUP, P])
        masked = sb("masked", [P, 2, GROUP, P])
        leaky = sb("leaky", [P, 2, E])
        att_col = sb("att_col", [P, 1])
        att_all = sb("att_all", [P, P])
        tile_max = sb("tile_max", [P, 2, GROUP])
        run_max = sb("run_max", [P, TILES_A + 1])
        minus_max = sb("minus_max", [P, 4, GROUP])
        step_down = sb("step_down", [P, 4, GROUP])
        rescale = sb("rescale", [P, 4, GROUP])
        weight_t = sb("weight_t", [P, 2, GROUP, P])
        weight = sb("weight", [P, 2, GROUP, P])
        acc = sb("acc", [P, 4, GROUP, C])
        z = ps("z", [P, 2, E])
        score = ps("score", [P, 2, GROUP, P])
        turned = ps("turned", [P, 2, GROUP, P])
        total = ps("total", [P, 2, 512])

        s_att = sem("s_att")
        s_init = sem("s_init")
        s_tick = sem("s_tick")
        s_index = sem("s_index")
        s_pace = sem("s_pace")
        s_gathered = [sem(f"s_gathered{q}") for q in range(UNROLL)]
        s_window = [sem(f"s_window{q}") for q in range(4)]
        s_hot = sem("s_hot")
        s_z = sem("s_z")
        s_relu = sem("s_relu")
        s_leaky = sem("s_leaky")
        s_score = sem("s_score")
        s_outside = sem("s_outside")
        s_tmax = sem("s_tmax")
        s_run = sem("s_run")
        s_max = sem("s_max")
        s_exps = sem("s_exps")
        s_turned = sem("s_turned")
        s_weight = sem("s_weight")
        s_total = sem("s_total")
        s_acc = sem("s_acc")
        s_stored = [sem(f"s_stored{q}") for q in range(4)]

        with nc.Block() as block:
            @block.gpsimd
            def _(pool):
                gather_rows(pool, t, "A", groups, t.xl[layer], D, slots, rows, s_total, 1, s_index, s_gathered, s_tick)

            @block.sync
            def _(sp):
                sp.dma_start(att_col[:, :], att.rearrange("(p o) -> p o", o=1)).then_inc(s_att, 16)

                def stage(g, q, r):
                    wait(sp, s_z, g - 3)
                    wait(sp, s_hot, g - 3)
                    load_windows(nc, sp, t, "A", g, t.xr[layer], xr[:, q % 4], s_window[q % 4])
                    sp.dma_start(dst_row[:, q % 4, :], t.dst_rows["A"].rearrange("(g j) e -> g (j e)", j=GROUP)[bass.ds(g, 1)]
                                 .to_broadcast([P, E])).then_inc(s_window[q % 4], 16)
                run_groups(sp, groups, [(0, stage)])
                for q in range(4):
                    sp.wait_ge(s_stored[q], 16 * groups // 4)

            @block.scalar
            def _(act):
                def store(g, q, r):
                    wait(act, s_acc, GROUP * (g + 1))
                    act.dma_start(t.slab_att[layer][bass.ds(g * GROUP, GROUP)].rearrange("j p c -> p j c"), acc[:, q % 4]).then_inc(s_stored[q % 4], 16)

                def relu_g(g, q, r):
                    wait(act, s_z, g + 1)
                    wait(act, s_score, g - 1)
                    act.activation(leaky[:, q % 2, :], z[:, q % 2, :], ACT.Relu, scale=0.8).then_inc(s_relu, 1)

                def outside_t(g, q, r):
                    wait(act, s_hot, g + 1)
                    wait(act, s_exps, g - 1)
                    act.activation(masked[:, q % 2], hot_t[:, q % 4], ACT.Copy, scale=BIG, bias=-BIG).then_inc(s_outside, 1)

                def weight_g(g, q, r):
                    wait(act, s_turned, g + 1)
                    wait(act, s_total, g - 1)
                    act.activation(weight[:, q % 2], turned[:, q % 2], ACT.Copy).then_inc(s_weight, 1)

                def exps_g(g, q, r):
                    wait(act, s_max, g + 1)
                    wait(act, s_turned, g - 1)
                    wait(act, s_acc, GROUP * (g - 3))
                    act.activation(rescale[:, q % 4, :], step_down[:, q % 4, :], ACT.Exp)
                    for j in range(GROUP):
                        last = act.activation(weight_t[:, q % 2, j, :], masked[:, q % 2, j, :], ACT.Exp, bias=minus_max[:, q % 4, j:j + 1])
                    last.then_inc(s_exps, 1)
                run_groups(act, groups, [(2, outside_t), (1, relu_g), (4, weight_g), (3, exps_g), (7, store)])

            @block.tensor
            def _(pe):
                pe.wait_ge(s_init, 2)

                def z_g(g, q, r):
                    wait(pe, s_gathered[q], 16 * GROUP * (r + 1))
                    wait(pe, s_window[q % 4], 16 * (GROUP + 1) * (uses(q, r, 4) + 1))
                    wait(pe, s_hot, g + 1)
                    wait(pe, s_leaky, g - 1)
                    for j in range(GROUP):
                        out = z[:, q % 2, j * P:(j + 1) * P]
                        pe.matmul(out, rows[:, q, j, 0:D], t.ident[:, :], start=True, stop=False, skip_group_check=True)
                        last = pe.matmul(out, xr[:, q % 4, j, :], hot_t[:, q % 4, j, :], start=False, stop=True, skip_group_check=True)
                    last.then_inc(s_z, 1)

                def score_g(g, q, r):
                    wait(pe, s_leaky, g + 1)
                    wait(pe, s_tmax, g - 1)
                    pe.matmul(score[:, q % 2].rearrange("p j e -> p (j e)"), att_all[:, :], leaky[:, q % 2, :],
                              start=True, stop=True).then_inc(s_score, 1)

                def turn_g(g, q, r):
                    wait(pe, s_exps, g + 1)
                    wait(pe, s_weight, g - 1)
                    for j in range(GROUP):
                        last = pe.transpose(turned[:, q % 2, j, :], weight_t[:, q % 2, j, :], t.ident[:, :])
                    last.then_inc(s_turned, 1)

                def total_g(g, q, r):
                    wait(pe, s_weight, g + 1)
                    wait(pe, s_acc, GROUP * g)
                    for j in range(GROUP):
                        last = pe.matmul(total[:, j // 2, (j % 2) * C:(j % 2 + 1) * C], weight[:, q % 2, j, :], rows[:, q, j, :],
                                         start=True, stop=True)
                    last.then_inc(s_total, 1)
                run_groups(pe, groups, [(1, z_g), (4, turn_g), (2, score_g), (5, total_g)])

            @block.vector
            def _(dve):
                dve.memset(rows[:, :, :, D:], 1.0)
                dve.memset(run_max[:, 0:1], -BIG)
                dve.memset(acc[:, 3, GROUP - 1, :], 0.0).then_inc(s_init, 1)
                dve.wait_ge(s_init, 1)
                dve.wait_ge(s_att, 16)
                dve.tensor_copy(att_all[:, :], att_col[:, :].to_broadcast([P, P])).then_inc(s_init, 1)

                def leaky_g(g, q, r):
                    wait(dve, s_relu, g + 1)
                    dve.scalar_tensor_tensor(out=leaky[:, q % 2, :], in0=z[:, q % 2, :], scalar=0.2, in1=leaky[:, q % 2, :],
                                             op0=ALU.mult, op1=ALU.add).then_inc(s_leaky, 1)

                def tile_max_g(g, q, r):
                    wait(dve, s_score, g + 1)
                    wait(dve, s_outside, g + 1)
                    dve.sem_inc(s_pace, 1)
                    for j in range(GROUP):
                        last = dve.tensor_tensor_reduce(masked[:, q % 2, j, :], score[:, q % 2, j, :], masked[:, q % 2, j, :], 1.0, -BIG,
                                                        ALU.add, ALU.max, tile_max[:, q % 2, j:j + 1])
                    last.then_inc(s_tmax, 1)

                def max_g(g, q, r, j):
                    old, new = run_max[:, bass.ds(g * GROUP, GROUP)], run_max[:, bass.ds(g * GROUP + 1, GROUP)]
                    newwin = t.newwin[:, bass.ds(g * GROUP, GROUP)]
                    if j == 0:
                        wait(dve, s_tmax, g + 1)
                        dve.tensor_tensor_scan(new, newwin, tile_max[:, q % 2, :], run_max[:, bass.ds(g * GROUP, 1)],
                                               ALU.add, ALU.max).then_inc(s_run, 1)
                    elif j == 1:
                        wait(dve, s_run, 2 * g + 1)
                        wait(dve, s_exps, g - 3)
                        dve.tensor_scalar(minus_max[:, q % 4, :], new, -1.0, None, ALU.mult)
                        dve.tensor_tensor(step_down[:, q % 4, :], old, newwin, ALU.add).then_inc(s_run, 1)
                    elif j == 2:
                        wait(dve, s_run, 2 * g + 2)
                        dve.tensor_tensor(step_down[:, q % 4, :], step_down[:, q % 4, :], new, ALU.subtract).then_inc(s_max, 1)

                def hot_g(g, q, r):
                    wait(dve, s_window[q % 4], 16 * (GROUP + 1) * (uses(q, r, 4) + 1))
                    wait(dve, s_z, g - 3)
                    wait(dve, s_outside, g - 3)
                    dve.tensor_scalar(hot_t[:, q % 4].rearrange("p j e -> p (j e)"), dst_row[:, q % 4, :], t.iota_p[:, :], None,
                                      ALU.is_equal).then_inc(s_hot, 1)

                def acc_g(g, q, r, j):
                    wait(dve, s_total, g + 1)
                    wait(dve, s_stored[q % 4], 16 * uses(q, r, 4))
                    before = acc[:, q % 4, j - 1, :] if j else acc[:, (q - 1) % 4, GROUP - 1, :]
                    wait(dve, s_acc, g * GROUP + j)
                    dve.scalar_tensor_tensor(out=acc[:, q % 4, j, :], in0=before, scalar=rescale[:, q % 4, j:j + 1],
                                             in1=total[:, j // 2, (j % 2) * C:(j % 2 + 1) * C], op0=ALU.mult, op1=ALU.add).then_inc(s_acc, 1)
                run_groups(dve, groups, [(2, leaky_g), (3, tile_max_g), [(6, acc_g), (3, max_g)], (0, hot_g)])


def normalise(dve, step, y, stats, square, s_var, s_sd, n):
    centre(dve, step, y, stats, square, s_var)
    scale(dve, step, y, stats, s_sd, n)


def centre(dve, step, y, stats, square, s_var):
    mean, var = stats[:, 0, :], stats[:, 1, :]
    step(dve.tensor_reduce(mean, y, AX.X, ALU.add))
    step(dve.tensor_scalar(mean, mean, 1.0 / D, None, ALU.mult))
    step(dve.tensor_tensor(y, y, bcast_last(mean, D), ALU.subtract))
    step(dve.tensor_tensor(square, y, y, ALU.mult))
    step(dve.tensor_reduce(var, square, AX.X, ALU.add))
    dve.tensor_scalar(var, var, 1.0 / D, EPS, ALU.mult, ALU.add).then_inc(s_var, 1)


def scale(dve, step, y, stats, s_sd, n):
    var, dev, inv, tmp = (stats[:, i, :] for i in range(1, 5))
    dve.wait_ge(s_sd, n)
    inverse_root(dve, step, var, dev, inv, tmp)
    step(dve.tensor_tensor(y, y, bcast_last(inv, D), ALU.mult))


def inverse_root(dve, step, value, root, inv, tmp):
    step(dve.reciprocal(inv, root))
    step(dve.tensor_tensor(tmp, inv, inv, ALU.mult))
    step(dve.tensor_tensor(tmp, tmp, value, ALU.mult))
    step(dve.tensor_scalar(tmp, tmp, -0.5, 1.5, ALU.mult, ALU.add))
    step(dve.tensor_tensor(inv, inv, tmp, ALU.mult))


def turn_batch(pe, t, bank, source):
    for w in range(BATCH):
        last = pe.transpose(bank[:, w // 4, (w % 4) * P:(w % 4 + 1) * P], source[:, w, :], t.ident[:, :])
    return last


def copy_batch(act, out, bank):
    act.activation(out[:, 0:4, :], bank[:, 0, :].rearrange("p (w n) -> p w n", w=4), ACT.Copy)
    return act.activation(out[:, 4:7, :], bank[:, 1, 0:3 * P].rearrange("p (w n) -> p w n", w=3), ACT.Copy)


def max_nodes(nc, t, W1, b1):
    with nc.cleanup_on_exit(), ExitStack() as ctx:
        def sem(name):
            return nc.alloc_semaphore("mn_" + name)

        def sb(name, shape, dt=F32):
            return ctx.enter_context(nc.sbuf_tensor("mn_" + name, shape, dt))

        W = sb("W", [P, 2, P])
        bias = sb("bias", [P, P])
        acc = sb("acc", [P, 3, BATCH, D + 1])
        res = sb("res", [P, 3, BATCH, D])
        x = sb("x", [P, 3, BATCH, D])
        y = sb("y", [P, 2, BATCH, D])
        square = sb("square", [P, BATCH, D])
        rec = sb("rec", [P, BATCH])
        stats = sb("stats", [P, 5, BATCH])
        yT = sb("yT", [P, BATCH, P])
        O = sb("O", [P, 2, BATCH, 2 * D])
        turned = ctx.enter_context(nc.psum_tensor("mn_turned", [P, 2, 512], F32))
        prod = ctx.enter_context(nc.psum_tensor("mn_prod", [P, 4, 512], F32))
        s_w = sem("s_w")
        s_in = [sem(f"s_in{p}") for p in range(3)]
        s_dve = sem("s_dve")
        s_base = sem("s_base")
        s_used = sem("s_used")
        s_var = sem("s_var")
        s_sd = sem("s_sd")
        s_y = sem("s_y")
        s_turn = sem("s_turn")
        s_yt = sem("s_yt")
        s_prod = sem("s_prod")
        s_o = sem("s_o")
        s_out = [sem(f"s_out{p}") for p in range(2)]
        s_xout = [sem(f"s_xout{p}") for p in range(2)]

        with nc.Block() as block:
            @block.sync
            def _(sp):
                sp.dma_start(W[:, :, :], W1[0:2 * D, :].rearrange("(k p) n -> p k n", p=P)).then_inc(s_w, 16)
                sp.dma_start(bias[:, :], row(b1)).then_inc(s_w, 16)

                def load(b):
                    p = b % 3
                    wait(sp, s_used, b - 2)
                    load_last(nc, sp, t, "A", b, t.slab_att[1], acc[:, p], s_in[p])
                    sp.dma_start(res[:, p], node_batch(t.res[1], b)).then_inc(s_in[p], 16)
                    sp.dma_start(x[:, p], node_batch(t.x_pad, b)).then_inc(s_in[p], 16)

                def out(b):
                    p = b % 2
                    sp.wait_ge(s_o, (b + 1) * BATCH)
                    sp.dma_start(node_batch(t.ha, b), O[:, p, :, 0:D]).then_inc(s_out[p], 16)
                    sp.dma_start(node_batch(t.hb, b), O[:, p, :, D:]).then_inc(s_out[p], 16)

                for b in range(3):
                    load(b)
                for b in range(NBATCH):
                    if 3 <= b + 2 < NBATCH:
                        load(b + 2)
                    p = b % 2
                    sp.wait_ge(s_y, b + 1)
                    sp.dma_start(node_batch(t.x1, b), y[:, p]).then_inc(s_xout[p], 16)
                    if b:
                        out(b - 1)
                out(NBATCH - 1)
                for p in range(2):
                    n = (NBATCH + 1 - p) // 2
                    sp.wait_ge(s_out[p], 32 * n)
                    sp.wait_ge(s_xout[p], 16 * n)

            @block.gpsimd
            def _(pool):
                for b in range(NBATCH):
                    i = b % 3
                    pool.wait_ge(s_in[i], 16 * (BATCH + 2) * (b // 3 + 1))
                    pool.tensor_tensor(x[:, i], x[:, i], res[:, i], ALU.add).then_inc(s_base, 1)

            @block.vector
            def _(dve):
                step = Chain(dve, s_dve)
                dve.wait_ge(s_w, 32)

                def products(b):
                    p = b % 2
                    wait(dve, s_out[p], 32 * (b // 2))
                    for w in range(BATCH):
                        n = b * BATCH + w
                        dve.wait_ge(s_prod, n + 1)
                        dve.tensor_copy(O[:, p, w, 0:D], prod[:, n % 4, 0:D])
                        dve.tensor_tensor(O[:, p, w, D:], prod[:, n % 4, D:2 * D], bias[:, :], ALU.add).then_inc(s_o, 1)

                for b in range(NBATCH):
                    p = b % 2
                    i = b % 3
                    dve.wait_ge(s_in[i], 16 * (BATCH + 2) * (b // 3 + 1))
                    step(dve.reciprocal(rec[:, :], acc[:, i, :, D]))
                    wait(dve, s_xout[p], 16 * (b // 2))
                    wait(dve, s_turn, b - 1)
                    step(dve.tensor_tensor(y[:, p], acc[:, i, :, 0:D], bcast_last(rec[:, :], D), ALU.mult))
                    dve.wait_ge(s_base, b + 1)
                    dve.tensor_tensor(y[:, p], y[:, p], x[:, i], ALU.add).then_inc(s_used, 1)
                    dve.wait_ge(s_used, b + 1)
                    centre(dve, step, y[:, p], stats, square[:, :, :], s_var)
                    if b:
                        products(b - 1)
                    scale(dve, step, y[:, p], stats, s_sd, b + 1)
                    dve.engine_nop().then_inc(s_y, 1)
                products(NBATCH - 1)

            @block.scalar
            def _(act):
                for b in range(NBATCH):
                    act.wait_ge(s_var, b + 1)
                    act.activation(stats[:, 2, :], stats[:, 1, :], ACT.Sqrt).then_inc(s_sd, 1)
                    act.wait_ge(s_turn, b + 1)
                    wait(act, s_prod, b * BATCH)
                    copy_batch(act, yT, turned).then_inc(s_yt, 1)

            @block.tensor
            def _(pe):
                pe.wait_ge(s_w, 32)
                for b in range(NBATCH):
                    pe.wait_ge(s_y, b + 1)
                    wait(pe, s_yt, b)
                    turn_batch(pe, t, turned, y[:, b % 2]).then_inc(s_turn, 1)
                    pe.wait_ge(s_yt, b + 1)
                    for w in range(BATCH):
                        n = b * BATCH + w
                        wait(pe, s_o, n - 3)
                        pe.matmul(prod[:, n % 4, 0:2 * D], yT[:, w, :], W[:, :, :].rearrange("p k n -> p (k n)"),
                                  start=True, stop=True).then_inc(s_prod, 1)


def max_sweep(nc, t, W1, W2):
    groups = TILES_B // GROUP
    E = GROUP * P
    with nc.cleanup_on_exit(), ExitStack() as ctx:
        def sem(name):
            return nc.alloc_semaphore("ms_" + name)

        def sb(name, shape, dt=F32):
            return ctx.enter_context(nc.sbuf_tensor("ms_" + name, shape, dt))

        def ps(name, shape):
            return ctx.enter_context(nc.psum_tensor("ms_" + name, shape, F32))

        slots = sb("slots", [P, UNROLL, GROUP], I32)
        rows = sb("rows", [P, UNROLL, GROUP, D])
        hb = sb("hb", [P, 4, GROUP, D])
        dst_row = sb("dst_row", [P, 4, E])
        seg_row = sb("seg_row", [P, UNROLL, E])
        ew_row = sb("ew_row", [9, 4, GROUP, P], BF16)
        W1c = sb("W1c", [1, D])
        W1c_parts = sb("W1c_parts", [1, 3, D], BF16)
        W1c_rest = sb("W1c_rest", [1, D])
        W1c_rows = sb("W1c_rows", [9, D], BF16)
        W2_sb = sb("W2", [P, D])
        hot_t = sb("hot_t", [P, 2, GROUP, P])
        hidden_sb = sb("hidden", [P, 2, E])
        running = sb("running", [P, 2, E])
        edge_major = sb("edge_major", [P, 2, GROUP, P])
        pick = sb("pick", [P, 2, GROUP, P])
        degree = sb("degree", [P, UNROLL, GROUP])
        acc = sb("acc", [P, 4, GROUP, D + 1])
        hidden = ps("hidden_ps", [P, 2, E])
        message = ps("message", [P, 2, E])
        turned = ps("turned", [P, 2, E])
        total = ps("total", [P, 2, GROUP, P])

        s_w = sem("s_w")
        s_init = sem("s_init")
        s_tick = sem("s_tick")
        s_index = sem("s_index")
        s_gathered = [sem(f"s_gathered{q}") for q in range(UNROLL)]
        s_window = [sem(f"s_window{q}") for q in range(4)]
        s_hot = sem("s_hot")
        s_degree = sem("s_degree")
        s_split = sem("s_split")
        s_hidden = sem("s_hidden")
        s_relu = sem("s_relu")
        s_message = sem("s_message")
        s_running = sem("s_running")
        s_turned = sem("s_turned")
        s_edge = sem("s_edge")
        s_pick = sem("s_pick")
        s_total = sem("s_total")
        s_acc = sem("s_acc")
        s_summed = sem("s_summed")
        s_stored = [sem(f"s_stored{q}") for q in range(4)]
        LOADS = GROUP + 3

        with nc.Block() as block:
            @block.gpsimd
            def _(pool):
                gather_rows(pool, t, "B", groups, t.ha, D, slots, rows, s_hidden, 1, s_index, s_gathered, s_tick)

            @block.sync
            def _(sp):
                sp.dma_start(W1c[:, :], W1[2 * D:2 * D + 1, :]).then_inc(s_w, 16)
                sp.dma_start(W2_sb[:, :], W2).then_inc(s_w, 16)
                sp.wait_ge(s_split, 5)
                for i in range(3):
                    for k in range(3):
                        sp.dma_start(W1c_rows[3 * i + k:3 * i + k + 1, :], W1c_parts[:, k, :]).then_inc(s_w, 16)

                def stage(g, q, r):
                    k = q % 4
                    wait(sp, s_hidden, g - 3)
                    load_windows(nc, sp, t, "B", g, t.hb, hb[:, k], s_window[k])
                run_groups(sp, groups, [(0, stage)])
                for q in range(4):
                    sp.wait_ge(s_stored[q], 16 * groups // 4)

            @block.scalar
            def _(act):
                def store(g, q, r):
                    wait(act, s_acc, GROUP * (g + 1))
                    wait(act, s_summed, g + 1)
                    act.dma_start(t.slab_max[bass.ds(g * GROUP, GROUP)].rearrange("j p c -> p j c"), acc[:, q % 4]).then_inc(s_stored[q % 4], 16)

                def rows_g(g, q, r):
                    k = q % 4
                    wait(act, s_hidden, g - 3)
                    wait(act, s_hot, g - 3)
                    wait(act, s_running, g - 7)
                    for out, table in ((dst_row[:, k], t.dst_rows["B"]), (seg_row[:, q], t.seg_rows)):
                        act.dma_start(out, table.rearrange("(g j) e -> g (j e)", j=GROUP)[bass.ds(g, 1)]
                                      .to_broadcast([P, E])).then_inc(s_window[k], 16)
                    act.dma_start(ew_row[:, k], t.ew_rows[bass.ds(g * GROUP, GROUP)].rearrange("j k e -> k j e")).then_inc(s_window[k], 16)

                def relu_g(g, q, r):
                    wait(act, s_hidden, g + 1)
                    wait(act, s_message, g - 1)
                    act.activation(hidden_sb[:, q % 2, :], hidden[:, q % 2, :], ACT.Relu).then_inc(s_relu, 1)

                def edge_g(g, q, r):
                    wait(act, s_turned, g + 1)
                    wait(act, s_total, g - 1)
                    act.activation(edge_major[:, q % 2].rearrange("p j e -> p (j e)"), turned[:, q % 2, :], ACT.Copy).then_inc(s_edge, 1)
                run_groups(act, groups, [(0, rows_g), (2, relu_g), (5, edge_g), (8, store)])

            @block.tensor
            def _(pe):
                pe.wait_ge(s_w, 16 * 11)

                def message_g(g, q, r):
                    wait(pe, s_relu, g + 1)
                    wait(pe, s_running, g - 1)
                    pe.matmul(message[:, q % 2, :], W2_sb[:, :], hidden_sb[:, q % 2, :], start=True, stop=True).then_inc(s_message, 1)

                def hidden_g(g, q, r):
                    wait(pe, s_gathered[q], 16 * GROUP * (r + 1))
                    wait(pe, s_window[q % 4], 16 * LOADS * (uses(q, r, 4) + 1))
                    wait(pe, s_hot, g + 1)
                    wait(pe, s_relu, g - 1)
                    pe.matmul(hidden[:, q % 2, :], W1c_rows[:, :], ew_row[:, q % 4].rearrange("k j e -> k (j e)"), start=True, stop=False,
                              skip_group_check=True)
                    for j in range(GROUP):
                        out = hidden[:, q % 2, j * P:(j + 1) * P]
                        pe.matmul(out, rows[:, q, j, :], t.ident[:, :], start=False, stop=False, skip_group_check=True)
                        last = pe.matmul(out, hb[:, q % 4, j, :], hot_t[:, q % 2, j, :], start=False, stop=True, skip_group_check=True)
                    last.then_inc(s_hidden, 1)

                def turn_g(g, q, r):
                    wait(pe, s_running, g + 1)
                    wait(pe, s_edge, g - 1)
                    for j in range(GROUP):
                        last = pe.transpose(turned[:, q % 2, j * P:(j + 1) * P], running[:, q % 2, j * P:(j + 1) * P], t.ident[:, :])
                    last.then_inc(s_turned, 1)

                def total_g(g, q, r):
                    wait(pe, s_pick, GROUP * (g + 1))
                    wait(pe, s_edge, g + 1)
                    wait(pe, s_acc, GROUP * (g - 1))
                    for j in range(GROUP):
                        last = pe.matmul(total[:, q % 2, j, :], pick[:, q % 2, j, :], edge_major[:, q % 2, j, :], start=True, stop=True)
                    last.then_inc(s_total, 1)
                run_groups(pe, groups, [(2, hidden_g), (3, message_g), (5, turn_g), (6, total_g)])

            @block.vector
            def _(dve):
                dve.memset(running[:, 1, E - 1:E], 0.0)
                dve.memset(acc[:, 3, GROUP - 1, :], 0.0).then_inc(s_init, 1)
                dve.wait_ge(s_init, 1)
                dve.wait_ge(s_w, 32)
                split_bf16(dve, Chain(dve, s_split), W1c[:, :], [W1c_parts[:, i, :] for i in range(3)], W1c_rest[:, :])

                def hot_g(g, q, r):
                    wait(dve, s_window[q % 4], 16 * LOADS * (uses(q, r, 4) + 1))
                    wait(dve, s_hidden, g - 1)
                    dve.tensor_scalar(hot_t[:, q % 2].rearrange("p j e -> p (j e)"), dst_row[:, q % 4, :], t.iota_p[:, :], None,
                                      ALU.is_equal).then_inc(s_hot, 1)
                    wait(dve, s_hot, g + 1)
                    wait(dve, s_summed, g - 7)
                    dve.tensor_reduce(degree[:, q, :], hot_t[:, q % 2], AX.X, ALU.add).then_inc(s_degree, 1)

                def running_g(g, q, r):
                    wait(dve, s_message, g + 1)
                    wait(dve, s_turned, g - 1)
                    wait(dve, s_running, g)
                    dve.tensor_tensor_scan(running[:, q % 2, :], seg_row[:, q, :], message[:, q % 2, :],
                                           running[:, (q - 1) % 2, E - 1:E], ALU.add, ALU.max).then_inc(s_running, 1)

                def pick_g(g, q, r, j):
                    wait(dve, s_total, g - 1)
                    dve.tensor_scalar(pick[:, q % 2, j, :], t.iota_f[:, :], t.lastrel[:, bass.ds(g * GROUP + j, 1)],
                                      None, ALU.is_equal).then_inc(s_pick, 1)

                def degree_g(g, q, r):
                    wait(dve, s_stored[q % 4], 16 * uses(q, r, 4))
                    wait(dve, s_degree, g + 1)
                    wait(dve, s_summed, g)
                    dve.tensor_tensor_scan(acc[:, q % 4, :, D], t.same["B"][:, bass.ds(g * GROUP, GROUP)], degree[:, q, :],
                                           acc[:, (q - 1) % 4, GROUP - 1, D:], ALU.mult, ALU.add).then_inc(s_summed, 1)

                def acc_g(g, q, r, j):
                    wait(dve, s_total, g + 1)
                    wait(dve, s_stored[q % 4], 16 * uses(q, r, 4))
                    before = acc[:, q % 4, j - 1, 0:D] if j else acc[:, (q - 1) % 4, GROUP - 1, 0:D]
                    wait(dve, s_acc, g * GROUP + j)
                    dve.scalar_tensor_tensor(out=acc[:, q % 4, j, 0:D], in0=before, scalar=t.same["B"][:, bass.ds(g * GROUP + j, 1)],
                                             in1=total[:, q % 2, j, :], op0=ALU.mult, op1=ALU.add).then_inc(s_acc, 1)
                run_groups(dve, groups, [(4, running_g), (7, degree_g), [(5, pick_g), (7, acc_g)], (1, hot_g)])


def update_nodes(nc, t, b2, U1, c1, U2, c2, W1_s, W1_v, Ws_s, Ws_v):
    inv = 1.0 / 32 ** 0.5
    with nc.cleanup_on_exit(), ExitStack() as ctx:
        def sem(name):
            return nc.alloc_semaphore("un_" + name)

        def sb(name, shape, dt=F32):
            return ctx.enter_context(nc.sbuf_tensor("un_" + name, shape, dt))

        U1_sb = sb("U1", [P, 2, D])
        U2_sb = sb("U2", [P, D])
        c1_col = sb("c1_col", [P, 1])
        c2_row = sb("c2_row", [P, D])
        b2_row = sb("b2_row", [P, D])
        WP = sb("WP", [P, 2, D])
        acc = sb("acc", [P, 3, BATCH, D + 1])
        x1 = sb("x1", [P, 3, BATCH, D])
        agg = sb("agg", [P, BATCH, D])
        deg = sb("deg", [P, 4, BATCH])
        has = sb("has", [P, BATCH])
        inT = sb("inT", [P, 2, BATCH, P])
        hidT = sb("hidT", [P, BATCH, P])
        y = sb("y", [P, 2, BATCH, D])
        square = sb("square", [P, BATCH, D])
        stats = sb("stats", [P, 5, BATCH])
        yT = sb("yT", [P, BATCH, P])
        O = sb("O", [P, 2, BATCH, 2 * D])
        left = ctx.enter_context(nc.psum_tensor("un_left", [P, 4, 512], F32))
        right = ctx.enter_context(nc.psum_tensor("un_right", [P, 4, 512], F32))
        s_zero = sem("s_zero")
        s_w = sem("s_w")
        s_scaled = sem("s_scaled")
        s_in = [sem(f"s_in{p}") for p in range(3)]
        s_dve = sem("s_dve")
        s_base = sem("s_base")
        s_deg = sem("s_deg")
        s_root = sem("s_root")
        s_agg = sem("s_agg")
        s_turn = sem("s_turn")
        s_int = sem("s_int")
        s_hid = sem("s_hid")
        s_hidt = sem("s_hidt")
        s_upd = sem("s_upd")
        s_used = sem("s_used")
        s_var = sem("s_var")
        s_sd = sem("s_sd")
        s_y = sem("s_y")
        s_turn2 = sem("s_turn2")
        s_yt = sem("s_yt")
        s_prod = sem("s_prod")
        s_o = sem("s_o")
        s_out = [sem(f"s_out{p}") for p in range(2)]
        s_xout = [sem(f"s_xout{p}") for p in range(2)]
        WLOADS = 5 + 8

        with nc.Block() as block:
            @block.gpsimd
            def _(pool):
                pool.memset(WP[:, :, :], 0.0).then_inc(s_zero, 1)
                pool.wait_ge(s_w, 16 * WLOADS)
                for b in range(NBATCH):
                    p = b % 2
                    pool.wait_ge(s_in[b % 3], 16 * (BATCH + 1) * (b // 3 + 1))
                    wait(pool, s_xout[p], 16 * (b // 2))
                    wait(pool, s_turn2, b - 1)
                    pool.tensor_tensor(y[:, p], x1[:, b % 3], bcast_mid(c2_row[:, :], BATCH), ALU.add).then_inc(s_base, 1)

            @block.sync
            def _(sp):
                sp.dma_start(U1_sb[:, :, :], U1.rearrange("(k p) n -> p k n", p=P)).then_inc(s_w, 16)
                sp.dma_start(U2_sb[:, :], U2).then_inc(s_w, 16)
                sp.dma_start(c1_col[:, :], c1.rearrange("(p o) -> p o", o=1)).then_inc(s_w, 16)
                sp.dma_start(c2_row[:, :], row(c2)).then_inc(s_w, 16)
                sp.dma_start(b2_row[:, :], row(b2)).then_inc(s_w, 16)
                sp.wait_ge(s_zero, 1)
                for k, (ws, wv) in enumerate(((W1_s, W1_v), (Ws_s, Ws_v))):
                    sp.dma_start(WP[0:32, k, 0:32], ws).then_inc(s_w, 16)
                    for d in range(3):
                        out = WP[32 + d:P:3, k, 32 + 32 * d:64 + 32 * d] if k == 0 else WP[32 + d:P:3, k, 32 + d:P:3]
                        sp.dma_start(out, wv, allow_slow_non_contiguous=True).then_inc(s_w, 16)

                def load(b):
                    p = b % 3
                    wait(sp, s_used, b - 2)
                    load_last(nc, sp, t, "B", b, t.slab_max, acc[:, p], s_in[p])
                    sp.dma_start(x1[:, p], node_batch(t.x1, b)).then_inc(s_in[p], 16)

                def out(b):
                    p = b % 2
                    sp.wait_ge(s_o, (b + 1) * BATCH)
                    sp.dma_start(node_batch(t.sv, b), O[:, p, :, 0:D]).then_inc(s_out[p], 16)
                    sp.dma_start(node_batch(t.skip, b), O[:, p, :, D:]).then_inc(s_out[p], 16)

                for b in range(3):
                    load(b)
                for b in range(NBATCH):
                    if b:
                        out(b - 1)
                    if 3 <= b + 2 < NBATCH:
                        load(b + 2)
                    sp.wait_ge(s_y, b + 1)
                    sp.dma_start(node_batch(t.x2, b), y[:, b % 2]).then_inc(s_xout[b % 2], 16)
                out(NBATCH - 1)
                for p in range(2):
                    n = (NBATCH + 1 - p) // 2
                    sp.wait_ge(s_out[p], 32 * n)
                    sp.wait_ge(s_xout[p], 16 * n)

            @block.vector
            def _(dve):
                step = Chain(dve, s_dve)
                dve.wait_ge(s_w, 16 * WLOADS)
                dve.tensor_scalar(WP[:, :, :], WP[:, :, :], inv, None, ALU.mult).then_inc(s_scaled, 1)
                dve.wait_ge(s_scaled, 1)

                def aggregate(b):
                    p = b % 3
                    dve.wait_ge(s_in[p], 16 * (BATCH + 1) * (b // 3 + 1))
                    filled = t.filled[:, b * BATCH:(b + 1) * BATCH]
                    step(dve.tensor_tensor(deg[:, 0, :], acc[:, p, :, D], filled, ALU.mult))
                    step(dve.tensor_scalar(has[:, :], deg[:, 0, :], 1.0, None, ALU.min))
                    dve.tensor_scalar(deg[:, 0, :], deg[:, 0, :], 1.0, None, ALU.max).then_inc(s_deg, 1)
                    wait(dve, s_turn, b)
                    step(dve.tensor_tensor(agg[:, :, :], acc[:, p, :, 0:D], bcast_mid(b2_row[:, :], BATCH), ALU.add))
                    dve.tensor_tensor(agg[:, :, :], agg[:, :, :], bcast_last(has[:, :], D), ALU.mult).then_inc(s_agg, 1)
                    dve.wait_ge(s_root, b + 1)
                    inverse_root(dve, step, deg[:, 0, :], deg[:, 1, :], deg[:, 2, :], deg[:, 3, :])
                    step(dve.tensor_tensor(t.dinv_sb[:, b * BATCH:(b + 1) * BATCH], deg[:, 2, :], has[:, :], ALU.mult))

                def residual(b):
                    p = b % 2
                    dve.wait_ge(s_upd, b + 1)
                    dve.wait_ge(s_base, b + 1)
                    step(dve.tensor_tensor(y[:, p, 0:4, :], y[:, p, 0:4, :], right[:, 2, :].rearrange("p (w n) -> p w n", w=4), ALU.add))
                    dve.tensor_tensor(y[:, p, 4:7, :], y[:, p, 4:7, :], right[:, 3, 0:3 * P].rearrange("p (w n) -> p w n", w=3),
                                      ALU.add).then_inc(s_used, 1)
                    dve.wait_ge(s_used, b + 1)
                    normalise(dve, step, y[:, p], stats, square[:, :, :], s_var, s_sd, b + 1)
                    dve.engine_nop().then_inc(s_y, 1)

                run_batches([(0, aggregate), (1, residual)])

            @block.scalar
            def _(act):
                def inputs(b):
                    act.wait_ge(s_deg, b + 1)
                    act.activation(deg[:, 1, :], deg[:, 0, :], ACT.Sqrt).then_inc(s_root, 1)
                    act.wait_ge(s_turn, b + 1)
                    copy_batch(act, inT[:, 0], left[:, 0:2])
                    copy_batch(act, inT[:, 1], left[:, 2:4]).then_inc(s_int, 1)

                def hidden(b):
                    act.wait_ge(s_hid, b + 1)
                    act.activation(hidT[:, 0:4, :].rearrange("p w n -> p (w n)"), right[:, 0, :], ACT.Relu, bias=c1_col[:, :])
                    act.activation(hidT[:, 4:7, :].rearrange("p w n -> p (w n)"), right[:, 1, 0:3 * P], ACT.Relu,
                                   bias=c1_col[:, :]).then_inc(s_hidt, 1)

                def root(b):
                    act.wait_ge(s_var, b + 1)
                    act.activation(stats[:, 2, :], stats[:, 1, :], ACT.Sqrt).then_inc(s_sd, 1)
                    act.wait_ge(s_turn2, b + 1)
                    copy_batch(act, yT, left[:, 0:2]).then_inc(s_yt, 1)

                def products(b):
                    p = b % 2
                    wait(act, s_out[p], 32 * (b // 2))
                    for w in range(BATCH):
                        n = b * BATCH + w
                        act.wait_ge(s_prod, n + 1)
                        act.activation(O[:, p, w, :], right[:, n % 2, 0:2 * D], ACT.Copy).then_inc(s_o, 1)
                run_batches([(0, inputs), (2, products), (0, hidden), (1, root)])

            @block.tensor
            def _(pe):
                pe.wait_ge(s_w, 16 * WLOADS)
                pe.wait_ge(s_scaled, 1)

                def turn_in(b):
                    pe.wait_ge(s_agg, b + 1)
                    wait(pe, s_yt, b - 1)
                    turn_batch(pe, t, left[:, 0:2], x1[:, b % 3])
                    turn_batch(pe, t, left[:, 2:4], agg).then_inc(s_turn, 1)

                def products(b):
                    for w in range(BATCH):
                        n = b * BATCH + w
                        wait(pe, s_o, n - 1)
                        if w < 2:
                            wait(pe, s_hidt, b + 2 if b + 2 <= NBATCH else NBATCH)
                        pe.matmul(right[:, n % 2, 0:2 * D], yT[:, w, :], WP[:, :, :].rearrange("p k n -> p (k n)"),
                                  start=True, stop=True).then_inc(s_prod, 1)

                def hidden(b):
                    pe.wait_ge(s_int, b + 1)
                    wait(pe, s_o, (b - 1) * BATCH)
                    for c, n in ((0, 4), (1, 3)):
                        for k in range(2):
                            last = pe.matmul(right[:, c, 0:n * P], U1_sb[:, k, :],
                                             inT[:, k, 4 * c:4 * c + n, :].rearrange("p w n -> p (w n)"), start=(k == 0), stop=(k == 1))
                    last.then_inc(s_hid, 1)

                def turn_out(b):
                    pe.wait_ge(s_y, b + 1)
                    wait(pe, s_int, min(b + 2, NBATCH))
                    turn_batch(pe, t, left[:, 0:2], y[:, b % 2]).then_inc(s_turn2, 1)

                def update(b):
                    pe.wait_ge(s_hidt, b + 1)
                    wait(pe, s_used, b)
                    for w in range(BATCH):
                        last = pe.matmul(right[:, 2 + w // 4, (w % 4) * P:(w % 4 + 1) * P], hidT[:, w, :], U2_sb[:, :], start=True, stop=True)
                    last.then_inc(s_upd, 1)

                def product_inputs_ready(b):
                    pe.wait_ge(s_yt, b + 1)
                run_batches([(0, turn_in), (2, product_inputs_ready), (2, products), (0, hidden), (0, update), (1, turn_out)])


def equi_sweep(nc, t, mW0, mb0, mW1, mb1, mW2, mb2):
    groups = TILES_B // GROUP
    E = GROUP * P
    M = 2 * D
    U = 32
    HID = 64
    with nc.cleanup_on_exit(), ExitStack() as ctx:
        def sem(name):
            return nc.alloc_semaphore("es_" + name)

        def sb(name, shape, dt=F32):
            return ctx.enter_context(nc.sbuf_tensor("es_" + name, shape, dt))

        def ps(name, shape):
            return ctx.enter_context(nc.psum_tensor("es_" + name, shape, F32))

        slots = sb("slots", [P, UNROLL, GROUP], I32)
        rows = sb("rows", [P, UNROLL, GROUP, D])
        W0 = sb("W0", [GROUP * 8, 2, 2, HID])
        W1_sb = sb("W1", [2 * HID, 2, HID])
        W2_sb = sb("W2", [HID + 1, D])
        b0 = sb("b0", [2 * HID, 1])
        b1 = sb("b1", [HID, 1])
        radial = sb("radial", [P, 2, GROUP, 8])
        radial_t = sb("radial_t", [GROUP * 8, 2, P])
        hid0 = sb("hid0", [2 * HID, 2, E // 2])
        hid1 = sb("hid1", [HID + 1, 2, E])
        scaled = sb("scaled", [P, 4, GROUP, D])
        q_s = sb("q_s", [P, 2, GROUP, U])
        dots = sb("dots", [P, 2, GROUP, 3, U])
        dot = sb("dot", [P, 2, GROUP, U])
        apart = sb("apart", [P, GROUP, P])
        pick = sb("pick", [P, 4, GROUP, P])
        msg = sb("msg", [P, 4, GROUP, M])
        acc = sb("acc", [P, 4, GROUP, M])
        radial_ps = ps("radial_ps", [GROUP * 8, 2, 512])
        h0 = ps("h0", [P, 512])
        h1 = ps("h1", [HID, 512])
        w = ps("w", [P, 2, GROUP, D])
        total = ps("total", [P, GROUP, M])

        s_w = sem("s_w")
        s_zero = sem("s_zero")
        s_init = sem("s_init")
        s_tick = sem("s_tick")
        s_pace = sem("s_pace")
        s_index = sem("s_index")
        s_gathered = [sem(f"s_gathered{q}") for q in range(UNROLL)]
        s_radial = sem("s_radial")
        s_turned = sem("s_turned")
        s_radial_t = sem("s_radial_t")
        s_h0 = sem("s_h0")
        s_hid0 = sem("s_hid0")
        s_h1 = sem("s_h1")
        s_hid1 = sem("s_hid1")
        s_weights = sem("s_weights")
        s_scaled = sem("s_scaled")
        s_pick = sem("s_pick")
        s_q = sem("s_q")
        s_apart = sem("s_apart")
        s_dots = sem("s_dots")
        s_dot = sem("s_dot")
        s_msg = sem("s_msg")
        s_total = sem("s_total")
        s_acc = sem("s_acc")
        s_stored = [sem(f"s_stored{q}") for q in range(4)]

        with nc.Block() as block:
            @block.gpsimd
            def _(pool):
                pool.memset(W0[:, :, :, :], 0.0).then_inc(s_zero, 1)
                pool.memset(W1_sb[:, :, :], 0.0).then_inc(s_zero, 1)
                gather_rows(pool, t, "B", groups, t.sv, D, slots, rows, s_msg, 1, s_index, s_gathered, s_tick)

            @block.sync
            def _(sp):
                sp.wait_ge(s_zero, 2)
                for j in range(GROUP):
                    sp.dma_start(W0[8 * j:8 * j + 8, j // 2, j % 2, :], mW0).then_inc(s_w, 16)
                for i in range(2):
                    sp.dma_start(W1_sb[i * HID:(i + 1) * HID, i, :], mW1).then_inc(s_w, 16)
                    sp.dma_start(b0[i * HID:(i + 1) * HID, :], mb0.rearrange("(p o) -> p o", o=1)).then_inc(s_w, 16)
                sp.dma_start(W2_sb[0:HID, :], mW2).then_inc(s_w, 16)
                sp.dma_start(W2_sb[HID:, :], mb2.rearrange("(o n) -> o n", o=1)).then_inc(s_w, 16)
                sp.dma_start(b1[:, :], mb1.rearrange("(p o) -> p o", o=1)).then_inc(s_w, 16)

                def store(g, q, r):
                    wait(sp, s_acc, GROUP * (g + 1))
                    sp.dma_start(t.slab_equi[bass.ds(g * GROUP, GROUP)].rearrange("j p c -> p j c"), acc[:, q % 4]).then_inc(s_stored[q % 4], 16)
                run_groups(sp, groups, [(0, store)])
                for q in range(4):
                    sp.wait_ge(s_stored[q], 16 * groups // 4)

            @block.scalar
            def _(act):
                act.wait_ge(s_w, 16 * 11)
                act.wait_ge(s_init, 1)

                def radial_g(g, q, r):
                    wait(act, s_turned, g - 1)
                    act.activation(radial[:, q % 2], t.ea8[:, bass.ds(g * GROUP, GROUP), :], ACT.Copy).then_inc(s_radial, 1)

                def radial_t_g(g, q, r):
                    wait(act, s_turned, g + 1)
                    wait(act, s_h0, g - 1)
                    act.activation(radial_t[:, q % 2, :], radial_ps[:, q % 2, 0:P], ACT.Copy).then_inc(s_radial_t, 1)

                def hid0_g(g, q, r):
                    wait(act, s_h0, g + 1)
                    wait(act, s_h1, g - 1)
                    act.activation(hid0[:, q % 2, :], h0[:, 0:2 * P], ACT.Silu, bias=b0[:, :]).then_inc(s_hid0, 1)

                def hid1_g(g, q, r):
                    wait(act, s_h1, g + 1)
                    wait(act, s_weights, g - 1)
                    act.activation(hid1[0:HID, q % 2, :], h1[:, :], ACT.Silu, bias=b1[:, :]).then_inc(s_hid1, 1)

                def scaled_g(g, q, r):
                    wait(act, s_gathered[q], 16 * GROUP * (r + 1))
                    wait(act, s_msg, g - 3)
                    for j in range(GROUP):
                        last = act.activation(scaled[:, q % 4, j, :], rows[:, q, j, :], ACT.Copy,
                                              scale=t.ea4[:, bass.ds(g * GROUP + j, 1), 0])
                    last.then_inc(s_scaled, 1)
                def pick_g(g, q, r):
                    wait(act, s_total, 2 * (g - 3))
                    wait(act, s_pick, g)
                    for j in range(GROUP):
                        last = act.activation(apart[:, j, :], t.iota_f[:, :], ACT.Square, scale=-1.0,
                                              bias=t.dstrel["B"][:, bass.ds(g * GROUP + j, 1)])
                    last.then_inc(s_apart, 1)
                    wait(act, s_apart, g + 1)
                    act.activation(pick[:, q % 4], apart[:, :, :], ACT.Relu, scale=-1.0, bias=t.ones[:, 0:1]).then_inc(s_pick, 1)
                run_groups(act, groups, [(0, radial_g), (2, hid0_g), (1, radial_t_g), (3, hid1_g), (3, scaled_g), (4, pick_g)])

            @block.tensor
            def _(pe):
                pe.wait_ge(s_w, 16 * 11)
                pe.wait_ge(s_init, 1)

                def turn_g(g, q, r):
                    wait(pe, s_radial, g + 1)
                    wait(pe, s_radial_t, g - 1)
                    pe.transpose(radial_ps[:, q % 2, 0:P], radial[:, q % 2].rearrange("p j k -> p (j k)"), t.ident[:, :]).then_inc(s_turned, 1)

                def h0_g(g, q, r):
                    wait(pe, s_radial_t, g + 1)
                    wait(pe, s_hid0, g)
                    for c in range(2):
                        last = pe.matmul(h0[:, c * P:(c + 1) * P], W0[:, c, :, :].rearrange("k i n -> k (i n)"), radial_t[:, q % 2, :], start=True, stop=True)
                    last.then_inc(s_h0, 1)

                def h1_g(g, q, r):
                    wait(pe, s_hid0, g + 1)
                    wait(pe, s_hid1, g)
                    pe.sem_inc(s_pace, 1)
                    for i in range(2):
                        last = pe.matmul(h1[:, i * 2 * P:(i + 1) * 2 * P], W1_sb[:, i, :],
                                         hid0[:, q % 2, :], start=True, stop=True)
                    last.then_inc(s_h1, 1)

                def weights_g(g, q, r):
                    wait(pe, s_hid1, g + 1)
                    wait(pe, s_msg, g - 1)
                    pe.sem_inc(s_pace, 1)
                    for j in range(GROUP):
                        place = (2 * (j % 2) + j // 2) * P
                        last = pe.matmul(w[:, q % 2, j, :], hid1[:, q % 2, place:place + P], W2_sb[:, :], start=True, stop=True)
                    last.then_inc(s_weights, 1)

                def total_first(g, q, r):
                    wait(pe, s_pick, g + 1)
                    wait(pe, s_msg, g + 1)
                    wait(pe, s_acc, GROUP * g - 2)
                    for j in (0, 1):
                        last = pe.matmul(total[:, j, :], pick[:, q % 4, j, :], msg[:, q % 4, j, :], start=True, stop=True)
                    last.then_inc(s_total, 1)

                def total_second(g, q, r):
                    wait(pe, s_acc, GROUP * g)
                    for j in (2, 3):
                        last = pe.matmul(total[:, j, :], pick[:, q % 4, j, :], msg[:, q % 4, j, :], start=True, stop=True)
                    last.then_inc(s_total, 1)
                run_groups(pe, groups, [(6, total_second), (0, turn_g), (1, h0_g), (2, h1_g), (3, weights_g), (5, total_first)])

            @block.vector
            def _(dve):
                dve.memset(hid1[HID:, :, :], 1.0)
                dve.memset(acc[:, 3, GROUP - 1, :], 0.0).then_inc(s_init, 1)
                dve.wait_ge(s_init, 1)

                def part(g, q, i):
                    return w[:, q % 2, :, i * U:(i + 1) * U]

                def msg_g(g, q, r, j):
                    k = q % 2
                    m = q % 4
                    sh = t.ea4[:, bass.ds(g * GROUP, GROUP), 1:4].unsqueeze(3).to_broadcast([P, GROUP, 3, U])
                    vectors = rows[:, q, :, U:].rearrange("p j (d u) -> p j d u", d=3)
                    if j == 0:
                        wait(dve, s_gathered[q], 16 * GROUP * (r + 1))
                        wait(dve, s_weights, g + 1)
                        wait(dve, s_dot, 2 * (g - 1))
                        dve.tensor_tensor(dots[:, k], vectors, sh, ALU.mult).then_inc(s_dots, 1)
                        dve.tensor_tensor(q_s[:, k], part(g, q, 2), rows[:, q, :, 0:U], ALU.mult).then_inc(s_q, 1)
                    elif j == 1:
                        wait(dve, s_dots, g + 1)
                        dve.tensor_tensor(dot[:, k], dots[:, k, :, 0, :], dots[:, k, :, 1, :], ALU.add).then_inc(s_dot, 1)
                        wait(dve, s_scaled, g + 1)
                        wait(dve, s_total, 2 * (g - 3))
                        dve.tensor_tensor(msg[:, m, :, 0:U], part(g, q, 0), scaled[:, m, :, 0:U], ALU.mult)
                    elif j == 2:
                        wait(dve, s_dot, 2 * g + 1)
                        dve.tensor_tensor(dot[:, k], dot[:, k], dots[:, k, :, 2, :], ALU.add).then_inc(s_dot, 1)
                        wait(dve, s_q, g + 1)
                        dve.tensor_tensor(msg[:, m, :, 2 * U:5 * U].rearrange("p j (d u) -> p j d u", d=3),
                                          q_s[:, k].unsqueeze(2).to_broadcast([P, GROUP, 3, U]), sh, ALU.mult)
                    else:
                        wait(dve, s_dot, 2 * g + 2)
                        dve.tensor_tensor(msg[:, m, :, U:2 * U], part(g, q, 1), dot[:, k], ALU.mult)
                        dve.tensor_tensor(msg[:, m, :, 5 * U:].rearrange("p j (d u) -> p j d u", d=3),
                                          part(g, q, 3).unsqueeze(2).to_broadcast([P, GROUP, 3, U]),
                                          scaled[:, m, :, U:].rearrange("p j (d u) -> p j d u", d=3), ALU.mult).then_inc(s_msg, 1)

                def acc_g(g, q, r, j):
                    wait(dve, s_total, 2 * g + 1 + j // 2)
                    wait(dve, s_stored[q % 4], 16 * uses(q, r, 4))
                    before = acc[:, q % 4, j - 1, :] if j else acc[:, (q - 1) % 4, GROUP - 1, :]
                    wait(dve, s_acc, g * GROUP + j)
                    dve.scalar_tensor_tensor(out=acc[:, q % 4, j, :], in0=before, scalar=t.same["B"][:, bass.ds(g * GROUP + j, 1)],
                                             in1=total[:, j, :], op0=ALU.mult, op1=ALU.add).then_inc(s_acc, 1)
                run_groups(dve, groups, [[(6, acc_g), (4, msg_g)]])


def equi_nodes(nc, t, W2_s, W2_v):
    U = 32
    C = D + 1
    SILU_C = 1.6790524
    with nc.cleanup_on_exit(), ExitStack() as ctx:
        def sem(name):
            return nc.alloc_semaphore("en_" + name)

        def sb(name, shape, dt=F32):
            return ctx.enter_context(nc.sbuf_tensor("en_" + name, shape, dt))

        WB = sb("WB", [P, 2, 5 * U])
        acc = sb("acc", [P, 3, BATCH, 2 * D])
        skip = sb("skip", [P, 3, BATCH, D])
        x2 = sb("x2", [P, 3, BATCH, D])
        accT = sb("accT", [P, 2, BATCH, P])
        G = sb("G", [P, BATCH, 5 * U])
        gates = sb("gates", [P, BATCH, 2 * U])
        y = sb("y", [P, 2, BATCH, D])
        square = sb("square", [P, BATCH, D])
        stats = sb("stats", [P, 5, BATCH])
        O = sb("O", [P, 2, BATCH, C])
        turned = ctx.enter_context(nc.psum_tensor("en_turned", [P, 4, 512], F32))
        prod = ctx.enter_context(nc.psum_tensor("en_prod", [P, 4, 512], F32))
        s_zero = sem("s_zero")
        s_w = sem("s_w")
        s_in = [sem(f"s_in{p}") for p in range(3)]
        s_dve = sem("s_dve")
        s_turn = sem("s_turn")
        s_at = sem("s_at")
        s_prod = sem("s_prod")
        s_g = sem("s_g")
        s_gates = sem("s_gates")
        s_used = sem("s_used")
        s_var = sem("s_var")
        s_sd = sem("s_sd")
        s_y = sem("s_y")
        s_o = sem("s_o")
        s_out = [sem(f"s_out{p}") for p in range(2)]
        s_xout = [sem(f"s_xout{p}") for p in range(2)]
        vector_rows = [(0, 2 * U, 0, 0), (0, 3 * U, 0, 1), (1, 0, 0, 2), (1, U, U, 0), (1, 2 * U, U, 1), (1, 3 * U, U, 2)]
        WLOADS = 1 + len(vector_rows)

        with nc.Block() as block:
            @block.gpsimd
            def _(pool):
                pool.memset(WB[:, :, :], 0.0).then_inc(s_zero, 1)
                for b in range(NBATCH):
                    p = b % 2
                    pool.wait_ge(s_in[b % 3], 16 * (BATCH + 2) * (b // 3 + 1))
                    wait(pool, s_xout[p], 16 * (b // 2))
                    wait(pool, s_o, b - 1)
                    pool.tensor_tensor(y[:, p], x2[:, b % 3], skip[:, b % 3], ALU.add).then_inc(s_used, 1)

            @block.sync
            def _(sp):
                sp.wait_ge(s_zero, 1)
                sp.dma_start(WB[0:2 * U, 0, 0:2 * U], W2_s).then_inc(s_w, 16)
                for half, row0, source, d in vector_rows:
                    sp.dma_start(WB[row0:row0 + U, half, 2 * U + d::3], W2_v[source:source + U, :],
                                 allow_slow_non_contiguous=True).then_inc(s_w, 16)

                def load(b):
                    p = b % 3
                    wait(sp, s_used, b - 2)
                    wait(sp, s_turn, b - 2)
                    load_last(nc, sp, t, "B", b, t.slab_equi, acc[:, p], s_in[p])
                    sp.dma_start(skip[:, p], node_batch(t.skip, b)).then_inc(s_in[p], 16)
                    sp.dma_start(x2[:, p], node_batch(t.x2, b)).then_inc(s_in[p], 16)

                for b in range(3):
                    load(b)
                for b in range(NBATCH):
                    if 3 <= b + 2 < NBATCH:
                        load(b + 2)
                    p = b % 2
                    sp.wait_ge(s_y, b + 1)
                    sp.dma_start(node_batch(t.x3, b), y[:, p]).then_inc(s_xout[p], 16)
                    sp.wait_ge(s_o, b + 1)
                    sp.dma_start(node_batch(t.xd, b), O[:, p]).then_inc(s_out[p], 16)
                for p in range(2):
                    n = (NBATCH + 1 - p) // 2
                    sp.wait_ge(s_out[p], 16 * n)
                    sp.wait_ge(s_xout[p], 16 * n)

            @block.vector
            def _(dve):
                step = Chain(dve, s_dve)
                dve.wait_ge(s_w, 16 * WLOADS)
                step(dve.tensor_scalar(WB[:, :, :], WB[:, :, :], 1.0 / 32, None, ALU.mult))
                step(dve.tensor_scalar(WB[U:2 * U, 0, :], WB[U:2 * U, 0, :], 1.0 / 3 ** 0.5, None, ALU.mult))
                for b in range(NBATCH):
                    p = b % 2
                    filled = t.filled[:, b * BATCH:(b + 1) * BATCH]
                    dinv = t.dinv_sb[:, b * BATCH:(b + 1) * BATCH]
                    i = b % 3
                    dve.wait_ge(s_in[i], 16 * (BATCH + 2) * (b // 3 + 1))
                    wait(dve, s_gates, b)
                    for c, n in ((0, 3), (3, 3), (6, 1)):
                        dve.wait_ge(s_prod, b * BATCH + c + n)
                        last = dve.tensor_tensor(G[:, c:c + n, :], prod[:, c // 3, 0:n * 5 * U].rearrange("p (w c) -> p w c", w=n),
                                                 bcast_last(filled[:, c:c + n], 5 * U), ALU.mult)
                    last.then_inc(s_g, 1)
                    dve.wait_ge(s_used, b + 1)
                    dve.wait_ge(s_gates, b + 1)
                    step(dve.tensor_scalar(gates[:, :, :], gates[:, :, :], SILU_C, None, ALU.mult))
                    vectors = G[:, :, 2 * U:].rearrange("p w (u d) -> p w u d", d=3)
                    step(dve.tensor_tensor(vectors, vectors, gates[:, :, U:].unsqueeze(3).to_broadcast([P, BATCH, U, 3]), ALU.mult))
                    step(dve.tensor_tensor(y[:, p, :, 0:U], y[:, p, :, 0:U], gates[:, :, 0:U], ALU.add))
                    step(dve.tensor_tensor(y[:, p, :, U:], y[:, p, :, U:], G[:, :, 2 * U:], ALU.add))
                    normalise(dve, step, y[:, p], stats, square[:, :, :], s_var, s_sd, b + 1)
                    dve.engine_nop().then_inc(s_y, 1)
                    wait(dve, s_out[p], 16 * (b // 2))
                    step(dve.tensor_tensor(O[:, p, :, 0:D], y[:, p], bcast_last(dinv, D), ALU.mult))
                    dve.tensor_copy(O[:, p, :, D], dinv).then_inc(s_o, 1)

            @block.scalar
            def _(act):
                def copies(b):
                    act.wait_ge(s_turn, b + 1)
                    wait(act, s_prod, b * BATCH)
                    copy_batch(act, accT[:, 0], turned[:, 0:2])
                    copy_batch(act, accT[:, 1], turned[:, 2:4]).then_inc(s_at, 1)

                def gates_and_root(b):
                    act.wait_ge(s_g, b + 1)
                    wait(act, s_y, b)
                    act.activation(gates[:, :, :], G[:, :, 0:2 * U], ACT.Silu).then_inc(s_gates, 1)
                    act.wait_ge(s_var, b + 1)
                    act.activation(stats[:, 2, :], stats[:, 1, :], ACT.Sqrt).then_inc(s_sd, 1)
                run_batches([(0, copies), (1, gates_and_root)])

            @block.tensor
            def _(pe):
                pe.wait_ge(s_dve, 2)
                for b in range(NBATCH):
                    p = b % 3
                    pe.wait_ge(s_in[p], 16 * (BATCH + 2) * (b // 3 + 1))
                    wait(pe, s_at, b)
                    turn_batch(pe, t, turned[:, 0:2], acc[:, p, :, 0:D])
                    turn_batch(pe, t, turned[:, 2:4], acc[:, p, :, D:]).then_inc(s_turn, 1)
                    pe.wait_ge(s_at, b + 1)
                    wait(pe, s_g, b)
                    for w in range(BATCH):
                        for k in range(2):
                            last = pe.matmul(prod[:, w // 3, (w % 3) * 5 * U:(w % 3 + 1) * 5 * U], accT[:, k, w, :], WB[:, k, :],
                                             start=(k == 0), stop=(k == 1))
                        last.then_inc(s_prod, 1)


def norm_sweep(nc, t):
    groups = TILES_B // GROUP
    C = D + 1
    with nc.cleanup_on_exit(), ExitStack() as ctx:
        def sem(name):
            return nc.alloc_semaphore("ns_" + name)

        def sb(name, shape, dt=F32):
            return ctx.enter_context(nc.sbuf_tensor("ns_" + name, shape, dt))

        slots = sb("slots", [P, UNROLL, GROUP], I32)
        rows = sb("rows", [P, UNROLL, GROUP, C])
        pick = sb("pick", [P, 2, GROUP, P])
        acc = sb("acc", [P, 4, GROUP, C])
        total = ctx.enter_context(nc.psum_tensor("ns_total", [P, 2, 2, 512], F32))
        s_init = sem("s_init")
        s_tick = sem("s_tick")
        s_index = sem("s_index")
        s_gathered = [sem(f"s_gathered{q}") for q in range(UNROLL)]
        s_pick = sem("s_pick")
        s_total = sem("s_total")
        s_acc = sem("s_acc")
        s_stored = [sem(f"s_stored{q}") for q in range(4)]

        with nc.Block() as block:
            @block.gpsimd
            def _(pool):
                gather_rows(pool, t, "B", groups, t.xd, C, slots, rows, s_total, 1, s_index, s_gathered, s_tick)

            @block.sync
            def _(sp):
                def store(g, q, r):
                    wait(sp, s_acc, GROUP * (g + 1))
                    sp.dma_start(t.slab_norm[bass.ds(g * GROUP, GROUP)].rearrange("j p c -> p j c"), acc[:, q % 4]).then_inc(s_stored[q % 4], 16)
                run_groups(sp, groups, [(0, store)])
                for q in range(4):
                    sp.wait_ge(s_stored[q], 16 * groups // 4)

            @block.tensor
            def _(pe):
                def total_g(g, q, r):
                    wait(pe, s_gathered[q], 16 * GROUP * (r + 1))
                    wait(pe, s_pick, GROUP * (g + 1))
                    wait(pe, s_acc, GROUP * (g - 1))
                    for j in range(GROUP):
                        last = pe.matmul(total[:, q % 2, j // 2, (j % 2) * C:(j % 2 + 1) * C], pick[:, q % 2, j, :], rows[:, q, j, :],
                                         start=True, stop=True)
                    last.then_inc(s_total, 1)
                run_groups(pe, groups, [(1, total_g)])

            @block.vector
            def _(dve):
                dve.memset(acc[:, 3, GROUP - 1, :], 0.0).then_inc(s_init, 1)
                dve.wait_ge(s_init, 1)

                def pick_g(g, q, r, j):
                    wait(dve, s_total, g - 1)
                    dve.tensor_scalar(pick[:, q % 2, j, :], t.iota_f[:, :], t.dstrel["B"][:, bass.ds(g * GROUP + j, 1)],
                                      None, ALU.is_equal).then_inc(s_pick, 1)

                def acc_g(g, q, r, j):
                    wait(dve, s_total, g + 1)
                    wait(dve, s_stored[q % 4], 16 * uses(q, r, 4))
                    before = acc[:, q % 4, j - 1, :] if j else acc[:, (q - 1) % 4, GROUP - 1, :]
                    wait(dve, s_acc, g * GROUP + j)
                    dve.scalar_tensor_tensor(out=acc[:, q % 4, j, :], in0=before, scalar=t.same["B"][:, bass.ds(g * GROUP + j, 1)],
                                             in1=total[:, q % 2, j // 2, (j % 2) * C:(j % 2 + 1) * C], op0=ALU.mult,
                                             op1=ALU.add).then_inc(s_acc, 1)
                run_groups(dve, groups, [[(0, pick_g), (2, acc_g)]])


def norm_nodes(nc, t, W1_w, W1_b, out):
    C = D + 1
    with nc.cleanup_on_exit(), ExitStack() as ctx:
        def sem(name):
            return nc.alloc_semaphore("nn_" + name)

        def sb(name, shape, dt=F32):
            return ctx.enter_context(nc.sbuf_tensor("nn_" + name, shape, dt))

        W = sb("W", [P, P])
        WT = sb("WT", [P, P])
        bias = sb("bias", [P, D])
        acc = sb("acc", [P, 3, BATCH, C])
        x3 = sb("x3", [P, 3, BATCH, D])
        prod_in = sb("prod_in", [P, BATCH, D])
        prod_inT = sb("prod_inT", [P, BATCH, P])
        r = sb("r", [P, 2, BATCH, D])
        coef = sb("coef", [P, 2, BATCH])
        y = sb("y", [P, 2, BATCH, D])
        square = sb("square", [P, BATCH, D])
        stats = sb("stats", [P, 5, BATCH])
        turned = ctx.enter_context(nc.psum_tensor("nn_turned", [P, 2, 512], F32))
        prod = ctx.enter_context(nc.psum_tensor("nn_prod", [P, 2, 512], F32))
        s_w = sem("s_w")
        s_wturn = sem("s_wturn")
        s_in = [sem(f"s_in{p}") for p in range(3)]
        s_dve = sem("s_dve")
        s_wt = sem("s_wt")
        s_biased = sem("s_biased")
        s_r = sem("s_r")
        s_coef = sem("s_coef")
        s_pin = sem("s_pin")
        s_turn = sem("s_turn")
        s_pt = sem("s_pt")
        s_prod = sem("s_prod")
        s_used = sem("s_used")
        s_var = sem("s_var")
        s_sd = sem("s_sd")
        s_y = sem("s_y")
        s_out = [sem(f"s_out{p}") for p in range(2)]

        with nc.Block() as block:
            @block.sync
            def _(sp):
                sp.dma_start(W[:, :], W1_w).then_inc(s_w, 16)
                sp.dma_start(bias[:, :], row(W1_b)).then_inc(s_w, 16)

                def load(b):
                    p = b % 3
                    wait(sp, s_used, b - 2)
                    load_last(nc, sp, t, "B", b, t.slab_norm, acc[:, p], s_in[p])
                    sp.dma_start(x3[:, p], node_batch(t.x3, b)).then_inc(s_in[p], 16)

                for b in range(3):
                    load(b)
                for b in range(NBATCH):
                    if 3 <= b + 2 < NBATCH:
                        load(b + 2)
                    p = b % 2
                    sp.wait_ge(s_y, b + 1)
                    if b < NBATCH - 1:
                        sp.dma_start(node_batch(out, b), y[:, p]).then_inc(s_out[p], 16)
                    else:
                        full = NODES // P * P
                        n = BATCH - 1
                        sp.dma_start(out[b * BATCH * P:full, :].rearrange("(w p) d -> p w d", p=P), y[:, p, 0:n, :]).then_inc(s_out[p], 16)
                        sp.dma_start(out[full:NODES, :], y[0:NODES - full, p, n, :]).then_inc(s_out[p], 16)
                sp.wait_ge(s_out[0], 16 * ((NBATCH + 1) // 2 + 1))
                sp.wait_ge(s_out[1], 16 * (NBATCH // 2))

            @block.gpsimd
            def _(pool):
                pool.wait_ge(s_w, 32)
                for b in range(NBATCH):
                    pool.wait_ge(s_in[b % 3], 16 * (BATCH + 1) * (b // 3 + 1))
                    wait(pool, s_used, b - 1)
                    pool.tensor_tensor(r[:, b % 2], x3[:, b % 3], bcast_mid(bias[:, :], BATCH), ALU.add).then_inc(s_biased, 1)
                    pool.wait_ge(s_biased, b + 1)
                    pool.tensor_tensor(r[:, b % 2], r[:, b % 2], acc[:, b % 3, :, D:].to_broadcast([P, BATCH, D]), ALU.mult).then_inc(s_r, 1)

            @block.vector
            def _(dve):
                step = Chain(dve, s_dve)
                dve.wait_ge(s_wturn, 1)
                dve.tensor_copy(WT[:, :], prod[:, 0, 0:P]).then_inc(s_wt, 1)
                dve.wait_ge(s_wt, 1)

                def inputs(b):
                    windows = slice(b * BATCH, (b + 1) * BATCH)
                    dve.wait_ge(s_in[b % 3], 16 * (BATCH + 1) * (b // 3 + 1))
                    wait(dve, s_turn, b)
                    dve.tensor_tensor(prod_in[:, :, :], acc[:, b % 3, :, 0:D], x3[:, b % 3], ALU.mult).then_inc(s_pin, 1)
                    wait(dve, s_used, b - 1)
                    dve.tensor_tensor(coef[:, b % 2, :], t.dinv_sb[:, windows], t.filled[:, windows], ALU.mult).then_inc(s_coef, 1)

                def outputs(b):
                    p = b % 2
                    R = r[:, p]
                    dve.wait_ge(s_r, b + 1)
                    dve.wait_ge(s_coef, b + 1)
                    dve.wait_ge(s_prod, b + 1)
                    dve.tensor_tensor(R[:, 0:4, :], R[:, 0:4, :], prod[:, 0, :].rearrange("p (w n) -> p w n", w=4), ALU.add)
                    step(dve.tensor_tensor(R[:, 4:7, :], R[:, 4:7, :], prod[:, 1, 0:3 * P].rearrange("p (w n) -> p w n", w=3), ALU.add))
                    step(dve.tensor_tensor(R, R, bcast_last(coef[:, p, :], D), ALU.mult))
                    step(dve.scalar_tensor_tensor(out=R, in0=R, scalar=0.01, in1=R, op0=ALU.mult, op1=ALU.max))
                    wait(dve, s_out[p], 16 * (b // 2))
                    dve.tensor_tensor(y[:, p], x3[:, b % 3], R, ALU.add).then_inc(s_used, 1)
                    dve.wait_ge(s_used, b + 1)
                    normalise(dve, step, y[:, p], stats, square[:, :, :], s_var, s_sd, b + 1)
                    dve.engine_nop().then_inc(s_y, 1)
                run_batches([(0, inputs), (1, outputs)])

            @block.scalar
            def _(act):
                def copies(b):
                    act.wait_ge(s_turn, b + 1)
                    wait(act, s_prod, b)
                    copy_batch(act, prod_inT, turned).then_inc(s_pt, 1)

                def root(b):
                    act.wait_ge(s_var, b + 1)
                    act.activation(stats[:, 2, :], stats[:, 1, :], ACT.Sqrt).then_inc(s_sd, 1)
                run_batches([(0, copies), (1, root)])

            @block.tensor
            def _(pe):
                pe.wait_ge(s_w, 32)
                pe.transpose(prod[:, 0, 0:P], W[:, :], t.ident[:, :]).then_inc(s_wturn, 1)
                pe.wait_ge(s_wt, 1)
                for b in range(NBATCH):
                    pe.wait_ge(s_pin, b + 1)
                    wait(pe, s_pt, b)
                    turn_batch(pe, t, turned, prod_in).then_inc(s_turn, 1)
                    pe.wait_ge(s_pt, b + 1)
                    wait(pe, s_used, b)
                    for w in range(BATCH):
                        last = pe.matmul(prod[:, w // 4, (w % 4) * P:(w % 4 + 1) * P], prod_inT[:, w, :], WT[:, :], start=True, stop=True)
                    last.then_inc(s_prod, 1)


def graph_layers(nc, a, out):
    with ExitStack() as ctx:
        t = Store()
        allocate(nc, ctx, t)

        def layer(prefix, names):
            return [a[f"{prefix}_{n}"] for n in names.split()]

        prepare_schedule(nc, t, a["x"], a["src"], a["dst"], a["edge_weight"], a["edge_attr_4"], a["edge_attr_8"])
        prepare_tables(nc, t)
        for i in range(2):
            attention_nodes(nc, t, i, *layer(f"L0_gnn_l{i + 1}", "Wl bl Wr br Wres bias"))
            attention_sweep(nc, t, i, a[f"L0_gnn_l{i + 1}_att"])
        max_nodes(nc, t, *layer("L1_gnn", "W1 b1"))
        max_sweep(nc, t, *layer("L1_gnn", "W1 W2"))
        update_nodes(nc, t, *layer("L1_gnn", "b2 U1 c1 U2 c2"), *layer("L2_gnn", "W1_s W1_v Ws_s Ws_v"))
        equi_sweep(nc, t, *layer("L2_gnn", "mW0 mb0 mW1 mb1 mW2 mb2"))
        equi_nodes(nc, t, *layer("L2_gnn", "W2_s W2_v"))
        norm_sweep(nc, t)
        norm_nodes(nc, t, *layer("L3_gnn", "W1_w W1_b"), out)


_INS = ['x', 'src', 'dst', 'edge_attr_4', 'edge_attr_8', 'edge_weight',
        'L0_gnn_l1_Wl', 'L0_gnn_l1_bl', 'L0_gnn_l1_Wr', 'L0_gnn_l1_br', 'L0_gnn_l1_att', 'L0_gnn_l1_Wres', 'L0_gnn_l1_bias',
        'L0_gnn_l2_Wl', 'L0_gnn_l2_bl', 'L0_gnn_l2_Wr', 'L0_gnn_l2_br', 'L0_gnn_l2_att', 'L0_gnn_l2_Wres', 'L0_gnn_l2_bias',
        'L1_gnn_W1', 'L1_gnn_b1', 'L1_gnn_W2', 'L1_gnn_b2', 'L1_gnn_U1', 'L1_gnn_c1', 'L1_gnn_U2', 'L1_gnn_c2',
        'L2_gnn_W1_s', 'L2_gnn_W1_v', 'L2_gnn_mW0', 'L2_gnn_mb0', 'L2_gnn_mW1', 'L2_gnn_mb1', 'L2_gnn_mW2', 'L2_gnn_mb2',
        'L2_gnn_W2_s', 'L2_gnn_W2_v', 'L2_gnn_Ws_s', 'L2_gnn_Ws_v', 'L3_gnn_W1_w', 'L3_gnn_W1_b']
_OUTS = [((6250, 128), 'float32')]


def kernel(**inputs):
    import numpy as _np
    import concourse.bacc as _bacc
    from concourse import mybir as _mybir
    from concourse.bass_utils import run_bass_kernel_spmd as _run

    nc = _bacc.Bacc("TRN2", target_bir_lowering=False, num_devices=1)
    arrays, args = {}, {}
    for name in _INS:
        a = _np.ascontiguousarray(inputs[name])
        arrays[f"in_{name}_dram"] = a
        args[name] = nc.dram_tensor(f"in_{name}_dram", a.shape, _mybir.dt.from_np(a.dtype), kind="ExternalInput").ap()
    outs = []
    for i, (shape, dtype) in enumerate(_OUTS):
        dt = _mybir.dt.from_np(_np.dtype(dtype))
        outs.append(nc.dram_tensor(f"out_{i}_dram", shape, dt, kind="ExternalOutput").ap())
    graph_layers(nc, args, *outs)
    r = _run(nc, [arrays], core_ids=[0])
    got = tuple(r.results[0][f"out_{i}_dram"] for i in range(len(_OUTS)))
    return got[0]
```
